# Optimizing a Trainium2 kernel written in Bass

```python
import numpy as np
import jax
import jax.numpy as jnp

def _softmax(x, axis=-1):
    return jax.nn.softmax(x, axis=axis)

def _gelu(x):
    return jax.nn.gelu(x, approximate=True)

def _silu(x):
    return jax.nn.silu(x)

def _sigmoid(x):
    return jax.nn.sigmoid(x)

def _layernorm(x, axis=-1, eps=1e-05):
    m = jnp.mean(x, axis=axis, keepdims=True)
    v = jnp.var(x, axis=axis, keepdims=True)
    return (x - m) / jnp.sqrt(v + eps)

def _scatter_add(tgt, idx, src, axis=0):
    return tgt.at[idx].add(src)

def _segment_sum(src, seg, n):
    return jax.ops.segment_sum(src, seg, n)
kernel_name = 'mk_xattn_ffn_d2_seqx_r8_40024c'

def setup_inputs(seed: int=0):
    np.random.seed(seed)
    _w = jnp.asarray

    def _rec_inputs():
        import jax
        import jax.numpy as jnp
        _rk = jax.random.key(seed)
        x = -0.0002928 + 1 * jax.random.normal(jax.random.fold_in(_rk, 1), (64, 64, 128), jnp.float32)
        _lenS = 64 - jax.random.randint(jax.random.fold_in(_rk, 7), (64,), 0, max(1, 64 // 4) + 1, jnp.int32)
        _lenS2 = 64 - jax.random.randint(jax.random.fold_in(_rk, 8), (64,), 0, max(1, 64 // 4) + 1, jnp.int32)
        _ctx_512P = jax.random.normal(jax.random.fold_in(_rk, 11), (64, 16, 64), jnp.float32)
        _ctx_512c = jax.random.dirichlet(jax.random.fold_in(_rk, 511), 0.3 * jnp.ones((16,), jnp.float32), (64, 64))
        _ctx_512t = jnp.einsum('bsk,bkd->bsd', _ctx_512c, _ctx_512P)
        _ctx_512t = _ctx_512t * jax.lax.rsqrt(jnp.mean(jnp.square(_ctx_512t)) + 1e-12) * 0.953939
        ctx_512 = -1.52775e-05 + 0.999936 * (_ctx_512t + 0.3 * jax.random.normal(jax.random.fold_in(_rk, 611), (64, 64, 64), jnp.float32))
        itok_BxS2xS_0_7 = jax.random.randint(jax.random.fold_in(_rk, 12), (64, 64, 64), 0, 8, jnp.int32)
        return (x, ctx_512, itok_BxS2xS_0_7)
    x, ctx_512, itok_BxS2xS_0_7 = _rec_inputs()

    def _L0_xattn_setup():
        import jax, jax.numpy as jnp
        import numpy as np
        NUM_HEADS = 16
        HEAD_DIM = 64
        Q_DIM = 128
        KV_DIM = 64
        INNER = NUM_HEADS * HEAD_DIM
        key = jax.random.key(seed)
        ks = jax.random.split(key, 7)
        B, N, M = (32, 128, 256)
        q = jax.random.normal(ks[0], (B, N, Q_DIM), dtype=jnp.float32)
        kv = jax.random.normal(ks[1], (B, M, KV_DIM), dtype=jnp.float32)
        Wq = jax.random.normal(ks[2], (Q_DIM, INNER), dtype=jnp.float32) / np.sqrt(Q_DIM)
        Wk = jax.random.normal(ks[3], (KV_DIM, INNER), dtype=jnp.float32) / np.sqrt(KV_DIM)
        Wv = jax.random.normal(ks[4], (KV_DIM, INNER), dtype=jnp.float32) / np.sqrt(KV_DIM)
        Wo = jax.random.normal(ks[5], (INNER, Q_DIM), dtype=jnp.float32) / np.sqrt(INNER)
        bo = jax.random.normal(ks[6], (Q_DIM,), dtype=jnp.float32) * 0.01
        return {'q': q, 'kv': kv, 'Wq': Wq, 'Wk': Wk, 'Wv': Wv, 'Wo': Wo, 'bo': bo}
    _L0_xattn_all = _L0_xattn_setup()
    _L0_xattn_in = {k: v for k, v in _L0_xattn_all.items() if k in ('Wq', 'Wk', 'Wv', 'Wo', 'bo')}
    del _L0_xattn_all

    def _L0_ffn_setup():
        import jax, jax.numpy as jnp
        import numpy as np
        E, K = (8, 4)
        B, S, D = (4, 128, 128)
        H = D * 2 * 4 // 3

        def _swiglu(u, w1, w2, w3):
            h = jnp.einsum('...d,hd->...h', u, w1)
            v = jnp.einsum('...d,hd->...h', u, w2)
            return jnp.einsum('...h,dh->...d', jax.nn.sigmoid(h) * h * v, w3)
        key = jax.random.key(seed)
        ks = jax.random.split(key, 9)
        std = 0.02
        return {'x': jax.random.normal(ks[0], (B, S, D), jnp.float32), 'Wg': jax.random.normal(ks[1], (E, D), jnp.float32) * std, 'routing_bias': jnp.zeros((E,), jnp.float32), 'W1': jax.random.normal(ks[2], (E, H, D), jnp.float32) * std, 'W2': jax.random.normal(ks[3], (E, H, D), jnp.float32) * std, 'W3': jax.random.normal(ks[4], (E, D, H), jnp.float32) * std, 'Ws1': jax.random.normal(ks[5], (H, D), jnp.float32) * std, 'Ws2': jax.random.normal(ks[6], (H, D), jnp.float32) * std, 'Ws3': jax.random.normal(ks[7], (D, H), jnp.float32) * std}
    _L0_ffn_all = _L0_ffn_setup()
    _L0_ffn_in = {k: v for k, v in _L0_ffn_all.items() if k in ('Wg', 'routing_bias', 'W1', 'W2', 'W3', 'Ws1', 'Ws2', 'Ws3')}
    del _L0_ffn_all

    def _L1_xattn_setup():
        import jax, jax.numpy as jnp
        import numpy as np
        key = jax.random.key(seed)
        k1, k2, k3, k4, k5 = jax.random.split(key, 5)
        B, K, S, E, I, D = (4, 2, 64, 8, 128, 256)
        x = jax.random.normal(k1, (B, S, I), dtype=jnp.float32)
        weights = jax.random.uniform(k2, (B, K, S), dtype=jnp.float32)
        ensembles = jax.random.randint(k3, (B, K, S), 0, E, dtype=jnp.int64)
        lim1 = float(np.sqrt(6.0 / (D + I)))
        proj_in = jax.random.uniform(k4, (E, D, I), dtype=jnp.float32, minval=-lim1, maxval=lim1)
        proj_out = jax.random.uniform(k5, (E, I, D), dtype=jnp.float32, minval=-lim1, maxval=lim1)
        return {'x': x, 'weights': weights, 'ensembles': ensembles, 'proj_in': proj_in, 'proj_out': proj_out}
    _L1_xattn_all = _L1_xattn_setup()
    _L1_xattn_in = {k: v for k, v in _L1_xattn_all.items() if k in ('proj_in', 'proj_out')}
    del _L1_xattn_all

    def _L1_ffn_setup():
        import jax, jax.numpy as jnp
        import numpy as np
        HIDDEN = 128
        INNER = 512

        def _weight_quant(w):
            scale = 1.0 / jnp.clip(jnp.mean(jnp.abs(w)), 1e-05)
            wq = jnp.clip(jnp.round(w * scale), -1.0, 1.0) / scale
            return w + jax.lax.stop_gradient(wq - w)

        def _act_quant(x):
            scale = 127.0 / jnp.clip(jnp.max(jnp.abs(x), axis=-1, keepdims=True), 1e-05)
            xq = jnp.clip(jnp.round(x * scale), -128.0, 127.0) / scale
            return x + jax.lax.stop_gradient(xq - x)

        def _bitlinear(x, w):
            return jnp.einsum('bsi,oi->bso', _act_quant(x), _weight_quant(w))
        key = jax.random.key(seed)
        k0, k1, k2, k3 = jax.random.split(key, 4)
        x = jax.random.normal(k0, (4, 256, HIDDEN), dtype=jnp.float32)
        w_gate = jax.random.normal(k1, (INNER, HIDDEN), dtype=jnp.float32) / np.sqrt(HIDDEN)
        w_up = jax.random.normal(k2, (INNER, HIDDEN), dtype=jnp.float32) / np.sqrt(HIDDEN)
        w_down = jax.random.normal(k3, (HIDDEN, INNER), dtype=jnp.float32) / np.sqrt(INNER)
        return {'x': x, 'w_gate': w_gate, 'w_up': w_up, 'w_down': w_down}
    _L1_ffn_all = _L1_ffn_setup()
    _L1_ffn_in = {k: v for k, v in _L1_ffn_all.items() if k in ('w_gate', 'w_up', 'w_down')}
    del _L1_ffn_all
    return {'x': x, 'ctx_512': ctx_512, 'itok_BxS2xS_0_7': itok_BxS2xS_0_7, 'L0_xattn_Wq': _L0_xattn_in['Wq'], 'L0_xattn_Wk': _L0_xattn_in['Wk'], 'L0_xattn_Wv': _L0_xattn_in['Wv'], 'L0_xattn_Wo': _L0_xattn_in['Wo'], 'L0_xattn_bo': _L0_xattn_in['bo'], 'L0_ffn_Wg': _L0_ffn_in['Wg'], 'L0_ffn_routing_bias': _L0_ffn_in['routing_bias'], 'L0_ffn_W1': _L0_ffn_in['W1'], 'L0_ffn_W2': _L0_ffn_in['W2'], 'L0_ffn_W3': _L0_ffn_in['W3'], 'L0_ffn_Ws1': _L0_ffn_in['Ws1'], 'L0_ffn_Ws2': _L0_ffn_in['Ws2'], 'L0_ffn_Ws3': _L0_ffn_in['Ws3'], 'L1_xattn_proj_in': _L1_xattn_in['proj_in'], 'L1_xattn_proj_out': _L1_xattn_in['proj_out'], 'L1_ffn_w_gate': _L1_ffn_in['w_gate'], 'L1_ffn_w_up': _L1_ffn_in['w_up'], 'L1_ffn_w_down': _L1_ffn_in['w_down']}

def reference(x, ctx_512, itok_BxS2xS_0_7, L0_xattn_Wq, L0_xattn_Wk, L0_xattn_Wv, L0_xattn_Wo, L0_xattn_bo, L0_ffn_Wg, L0_ffn_routing_bias, L0_ffn_W1, L0_ffn_W2, L0_ffn_W3, L0_ffn_Ws1, L0_ffn_Ws2, L0_ffn_Ws3, L1_xattn_proj_in, L1_xattn_proj_out, L1_ffn_w_gate, L1_ffn_w_up, L1_ffn_w_down):
    import jax
    import jax.numpy as jnp

    def _L0_xattn_ref(q, kv, Wq, Wk, Wv, Wo, bo):
        import jax, jax.numpy as jnp
        import numpy as np
        NUM_HEADS = 16
        HEAD_DIM = 64
        Q_DIM = 128
        KV_DIM = 64
        INNER = NUM_HEADS * HEAD_DIM
        B, N, _ = q.shape
        M = kv.shape[1]
        scale = HEAD_DIM ** (-0.5)
        qh = (q @ Wq).reshape(B, N, NUM_HEADS, HEAD_DIM).transpose(0, 2, 1, 3)
        kh = (kv @ Wk).reshape(B, M, NUM_HEADS, HEAD_DIM).transpose(0, 2, 1, 3)
        vh = (kv @ Wv).reshape(B, M, NUM_HEADS, HEAD_DIM).transpose(0, 2, 1, 3)
        scores = jnp.einsum('bhnd,bhmd->bhnm', qh, kh) * scale
        attn = jax.nn.softmax(scores, axis=-1)
        out = jnp.einsum('bhnm,bhmd->bhnd', attn, vh)
        out = out.transpose(0, 2, 1, 3).reshape(B, N, INNER)
        return out @ Wo + bo

    def _L0_ffn_ref(x, Wg, routing_bias, W1, W2, W3, Ws1, Ws2, Ws3):
        import jax, jax.numpy as jnp
        import numpy as np
        E, K = (8, 4)
        B, S, D = (4, 128, 128)
        H = D * 2 * 4 // 3

        def _swiglu(u, w1, w2, w3):
            h = jnp.einsum('...d,hd->...h', u, w1)
            v = jnp.einsum('...d,hd->...h', u, w2)
            return jnp.einsum('...h,dh->...d', jax.nn.sigmoid(h) * h * v, w3)
        gate = jnp.einsum('bsd,ed->bse', x, Wg) + routing_bias
        _, top_idx = jax.lax.top_k(gate, K)
        mask = jax.nn.one_hot(top_idx, E, dtype=gate.dtype).sum(-2)
        masked_gate = jnp.where(mask > 0, gate, -jnp.inf)
        probs = jax.nn.softmax(masked_gate, axis=-1)
        weights = probs * mask
        out = _swiglu(x, Ws1, Ws2, Ws3)
        h1 = jnp.einsum('bsd,ehd->ebsh', x, W1)
        h2 = jnp.einsum('bsd,ehd->ebsh', x, W2)
        eo = jnp.einsum('ebsh,edh->ebsd', jax.nn.sigmoid(h1) * h1 * h2, W3)
        out = out + jnp.einsum('ebsd,bse->bsd', eo, weights)
        return out

    def _L1_xattn_ref(x, weights, ensembles, proj_in, proj_out):
        import jax, jax.numpy as jnp
        import numpy as np
        E = proj_in.shape[0]
        h = jax.nn.relu(jnp.einsum('edi,bsi->bsed', proj_in, x))
        o = jnp.einsum('eid,bsed->bsei', proj_out, h)
        onehot = jax.nn.one_hot(ensembles, E, dtype=x.dtype)
        gate = jnp.einsum('bks,bkse->bse', weights, onehot)
        return jnp.einsum('bsei,bse->bsi', o, gate)

    def _L1_ffn_ref(x, w_gate, w_up, w_down):
        import jax, jax.numpy as jnp
        import numpy as np
        HIDDEN = 128
        INNER = 512

        def _weight_quant(w):
            scale = 1.0 / jnp.clip(jnp.mean(jnp.abs(w)), 1e-05)
            wq = jnp.clip(jnp.round(w * scale), -1.0, 1.0) / scale
            return w + jax.lax.stop_gradient(wq - w)

        def _act_quant(x):
            scale = 127.0 / jnp.clip(jnp.max(jnp.abs(x), axis=-1, keepdims=True), 1e-05)
            xq = jnp.clip(jnp.round(x * scale), -128.0, 127.0) / scale
            return x + jax.lax.stop_gradient(xq - x)

        def _bitlinear(x, w):
            return jnp.einsum('bsi,oi->bso', _act_quant(x), _weight_quant(w))
        gate = jax.nn.silu(_bitlinear(x, w_gate))
        up = _bitlinear(x, w_up)
        return _bitlinear(gate * up, w_down)
    x = x + _L0_xattn_ref(_layernorm(x, axis=-1), ctx_512, L0_xattn_Wq, L0_xattn_Wk, L0_xattn_Wv, L0_xattn_Wo, L0_xattn_bo)
    x = x + _L0_ffn_ref(_layernorm(x, axis=-1), L0_ffn_Wg, L0_ffn_routing_bias, L0_ffn_W1, L0_ffn_W2, L0_ffn_W3, L0_ffn_Ws1, L0_ffn_Ws2, L0_ffn_Ws3)
    x = x + _L1_xattn_ref(_layernorm(x, axis=-1), ctx_512, itok_BxS2xS_0_7, L1_xattn_proj_in, L1_xattn_proj_out)
    x = x + _L1_ffn_ref(_layernorm(x, axis=-1), L1_ffn_w_gate, L1_ffn_w_up, L1_ffn_w_down)
    return x

_drawn_inputs = setup_inputs


def setup_inputs(seed=0):
    import zlib

    import numpy as np

    out = dict(_drawn_inputs(seed))
    spreads = {'L0_ffn_routing_bias': (0.0, 0.8)}
    factors = {'L0_xattn_bo': 6.28,
     'L0_ffn_Wg': 8.0,
     'L0_ffn_W1': 8.0,
     'L0_ffn_W2': 8.0,
     'L0_ffn_W3': 8.0,
     'L0_ffn_Ws1': 6.921,
     'L0_ffn_Ws2': 6.826,
     'L0_ffn_Ws3': 6.819,
     'L1_ffn_w_gate': 3.4,
     'L1_ffn_w_up': 3.291,
     'L1_ffn_w_down': 3.286}
    for name, (base, spread) in spreads.items():
        noise = np.random.default_rng([zlib.crc32(name.encode()), seed]).standard_normal(out[name].shape)
        drawn = base * np.exp(spread * noise) if base else spread * noise
        out[name] = jnp.asarray(drawn.astype(out[name].dtype))
    for name, factor in factors.items():
        out[name] = (out[name] * factor).astype(out[name].dtype)
    return out
```

```python
import concourse.bass as bass
from concourse import mybir
from contextlib import ExitStack

fp32 = mybir.dt.float32
f32r = mybir.dt.float32r
bf16 = mybir.dt.bfloat16
int32 = mybir.dt.int32
ALU = mybir.AluOpType
ACT = mybir.ActivationFunctionType
AX = mybir.AxisListType

B, S, D = 64, 64, 128
DC = 64
TOK = B * S
P = 128
TILES = TOK // P
CT = 4
CHUNKS = TILES // CT
CW = CT * P
BPT = P // S
HEADS, HD = 16, 64
HP = HEADS // 2
E0, H0 = 9, D * 2 * 4 // 3
ER = E0 - 1
TOPK = 4
HK = [(k, min(P, H0 - k)) for k in range(0, H0, P)]
E1, D1 = 8, 256
I1 = 512
EPS = 1e-5
ROUND = 1.5 * 2.0 ** 23


class Self:

    def __init__(self, eng, sem):
        self.eng, self.sem, self.n = eng, sem, 0

    def done(self, ins):
        ins.then_inc(self.sem, 1)
        self.n += 1

    def wait(self):
        self.eng.wait_ge(self.sem, self.n)

    def clear(self):
        self.wait()
        self.eng.sem_clear(self.sem)
        self.n = 0


class Ring:

    def __init__(self, banks, full, free, mid=None):
        self.banks, self.full, self.free, self.mid = banks, full, free, mid

    def bank(self, k):
        return self.banks[k % len(self.banks)]

    def wait_free(self, eng, n):
        eng.wait_ge(self.free, n + 1)

    def wait_full(self, eng, n):
        eng.wait_ge(self.full, n + 1)

    def wait_mid(self, eng, n):
        eng.wait_ge(self.mid, n + 1)

    def wait_read(self, eng, n):
        eng.wait_ge(self.free, n + 1 + len(self.banks))


def raw(ap):
    return ap.bitcast(fp32)


def kernel_program(nc, x, ctx_in, itok, Wq, Wk, Wv, Wo, bo, Wg, rbias, W1, W2, W3, Ws1, Ws2, Ws3,
                   p_in, p_out, w_gate, w_up, w_down, out, phases=4):
    top = ExitStack()
    with top:
        def sb(stack, name, shape, dt=fp32):
            return stack.enter_context(nc.sbuf_tensor(name, shape, dt))

        def sem(stack, name):
            return stack.enter_context(nc.semaphore(name))

        X = sb(top, "X", [P, TILES, D])
        MV = sb(top, "MV", [P, TILES, 2])
        ident = sb(top, "ident", [P, P])
        identb = sb(top, "identb", [P, P], bf16)
        w1n, w2n = (sb(top, n, [P, E0, len(HK), D]) for n in ("w1n", "w2n"))
        w3n = sb(top, "w3n", [D, E0, H0])
        wgn, rb_bc = sb(top, "wgn", [ER, D]), sb(top, "rb_bc", [P, ER])
        s_w0 = sem(top, "s_w0")
        W0_LOADS = 2 * len(HK) * 2 + 4
        bank = [top.enter_context(nc.psum_tensor(f"bank{i}", [P, 512], fp32)) for i in range(8)]
        x_t = x.rearrange("b s d -> (b s) d").rearrange("(t p) d -> p t d", p=P)
        out_t = out.rearrange("b s d -> (b s) d").rearrange("(t p) d -> p t d", p=P)


        def residual(dve, me, bs, ag, got, c, free):
            part = X[:, bass.ds(c * CT, CT), :]
            me.done(dve.tensor_tensor(part, got[:, :].rearrange("p (t d) -> p t d", t=CT), part, ALU.add))
            me.wait()
            for j in range(CT):
                ins = dve.bn_stats(bs[:, j, :], X[:, c * CT + j, :])
                if j == 0:
                    ins.then_inc(free, 1)
                else:
                    me.done(ins)
            me.wait()
            for j in range(CT):
                me.done(dve.bn_aggr(ag[:, j, :], bs[:, j, :]))
            me.wait()
            me.done(dve.tensor_copy(MV[:, bass.ds(c * CT, CT), :], ag[:, :, :]))

        def finish_deviation(stack, tag):
            dev = sb(stack, f"dev{tag}", [P, TILES])
            s_var, s_dev = sem(stack, f"s_var{tag}"), sem(stack, f"s_dev{tag}")

            def on_vector(dve, me):
                dve.tensor_scalar(dev[:, :], MV[:, :, 1], EPS, None, ALU.add).then_inc(s_var, 1)
                dve.wait_ge(s_dev, 1)
                me.done(dve.reciprocal(MV[:, :, 1], dev[:, :]))
                me.wait()

            def on_scalar(act):
                act.wait_ge(s_var, 1)
                act.activation(dev[:, :], dev[:, :], ACT.Sqrt).then_inc(s_dev, 1)
            return on_vector, on_scalar

        def normalise(dve, me, st, xn, c, signal):
            me.done(dve.tensor_copy(st[:, :, :], MV[:, bass.ds(c * CT, CT), :]))
            me.wait()
            for j in range(CT):
                ins = dve.tensor_scalar(xn[:, j, :], X[:, c * CT + j, :], st[:, j, 0:1], st[:, j, 1:2],
                                        ALU.subtract, ALU.mult)
            ins.then_inc(signal, 1)

        p1 = ExitStack()
        with p1:
            GH, GL = (sb(p1, n, [P, HP, P], f32r) for n in ("GH", "GL"))
            VH, VL = (sb(p1, n, [P, HP, P], f32r) for n in ("VH", "VL"))
            bo_bc = sb(p1, "bo_bc", [P, D])
            st_t = sb(p1, "st_t", [P, CT * BPT, P])
            st_v = sb(p1, "st_v", [P, CT, BPT, 2, DC + 1])
            sel = sb(p1, "sel", [2 * HEADS, HP, 2, S], bf16)
            bs, ag = sb(p1, "bs", [P, CT, 6]), sb(p1, "ag", [P, CT, 2])

            p0 = ExitStack()
            with p0:
                wq = sb(p0, "wq", [P, HP, P])
                wk, wv = sb(p0, "wk", [DC, HP, P]), sb(p0, "wv", [DC, HP, P])
                wo = sb(p0, "wo", [P, HP, D])
                wqT = sb(p0, "wqT", [P, HP, P])
                wkT, wvT = sb(p0, "wkT", [P, HP, 2, DC]), sb(p0, "wvT", [P, HP, 2, DC])
                s_x, s_w, s_ones = sem(p0, "s0_x"), sem(p0, "s0_w"), sem(p0, "s0_bo")
                s_const, s_tr, s_cp, s_cpa = (sem(p0, n) for n in ("s0_const", "s0_tr", "s0_cp", "s0_cpa"))
                s_mm, s_hi, s_lo, s_me, s_pool = (sem(p0, n) for n in ("s0_mm", "s0_hi", "s0_lo", "s0_me", "s0_pool"))
                wkT_bank, wvT_bank = (bank[i][:, :].rearrange("p (h c) -> p h c", h=HP) for i in (2, 3))
                with nc.Block() as block:
                    @block.sync
                    def _(sp):
                        sp.dma_start(wq[:, :, :], Wq.rearrange("i (h c) -> i h c", h=HP)).then_inc(s_w, 16)
                        sp.dma_start(wk[:, :, :], Wk.rearrange("i (h c) -> i h c", h=HP)).then_inc(s_w, 16)
                        for q in range(4):
                            n = TILES // 4
                            sp.dma_start(X[:, q * n:(q + 1) * n, :], x_t[:, q * n:(q + 1) * n, :]).then_inc(s_x, 16)
                        sp.wait_ge(s_x, 64)

                    @block.scalar
                    def _(act):
                        act.dma_start(wv[:, :, :], Wv.rearrange("i (h c) -> i h c", h=HP)).then_inc(s_w, 16)
                        act.dma_start(wo[:, :, :], Wo.rearrange("(h p) n -> p h n", p=P)).then_inc(s_w, 16)
                        act.dma_start(bo_bc[:, :], bo.rearrange("(a n) -> a n", a=1).to_broadcast([P, D])).then_inc(s_ones, 16)
                        for k in range(2):
                            act.wait_ge(s_tr, k + 1)
                            act.activation(wqT[:, 4 * k:4 * k + 4, :].rearrange("p h c -> p (h c)"), bank[k][:, :],
                                           ACT.Copy, scale=float(HD) ** -0.5).then_inc(s_cpa, 1)
                        act.wait_ge(s_tr, 4)
                        act.wait_ge(s_const, 2)
                        act.copy(wvT[0:DC, :, 0, :], wvT_bank[0:DC]).then_inc(s_cpa, 1)
                        act.copy(wvT[DC:P, :, 1, :], wvT_bank[DC:P]).then_inc(s_cpa, 1)
                        for k in range(4):
                            act.wait_ge(s_mm, k + 1)
                            hi = (GH, VH)[k // 2]
                            act.copy(hi[:, 4 * (k % 2):4 * (k % 2) + 4, :].rearrange("p h c -> p (h c)"),
                                     bank[4 + k][:, :]).then_inc(s_hi, 1)
                        act.wait_ge(s_ones, 16)

                    @block.gpsimd
                    def _(pool):
                        me = Self(pool, s_pool)
                        me.done(pool.memset(ident[:, :], 0.0))
                        me.done(pool.memset(sel[:, :, :, :], 0.0))
                        me.wait()
                        me.done(pool.affine_select(out=ident[:, :], in_=ident[:, :], compare_op=ALU.not_equal, fill=1.0,
                                                   base=0, pattern=[[-1, P]], channel_multiplier=1))
                        me.wait()
                        pool.tensor_copy(identb[:, :], ident[:, :]).then_inc(s_const, 1)
                        pool.memset(wkT[:, :, :, :], 0.0)
                        pool.memset(wvT[:, :, :, :], 0.0).then_inc(s_const, 1)
                        for base in (0, -HEADS):
                            me.done(pool.affine_select(out=sel[:, :, :, :], in_=sel[:, :, :, :],
                                                       compare_op=ALU.not_equal, fill=1.0, base=base,
                                                       pattern=[[-2, HP], [-1, 2], [0, S]], channel_multiplier=1))
                            me.wait()
                        pool.memset(st_t[:, :, :], 0.0)
                        me.done(pool.memset(st_v[:, :, :, :, :], 0.0))
                        me.wait()
                        for par in range(2):
                            me.done(pool.memset(st_v[par * S:(par + 1) * S, :, :, par, DC:DC + 1], 1.0))
                        me.wait()

                    @block.tensor
                    def _(pe):
                        pe.wait_ge(s_const, 1)
                        pe.wait_ge(s_w, 64)
                        for h in range(HP):
                            ins = pe.transpose(bank[h // 4][:, h % 4 * P:h % 4 * P + P], wq[:, h, :], ident[:, :])
                            if h % 4 == 3:
                                ins.then_inc(s_tr, 1)
                        for w, b in ((wk, 2), (wv, 3)):
                            for h in range(HP):
                                ins = pe.transpose(bank[b][:, h * DC:(h + 1) * DC], w[:, h, :], ident[0:DC, 0:DC])
                            ins.then_inc(s_tr, 1)
                        pe.wait_ge(s_cpa, 2)
                        pe.wait_ge(s_cp, 2)
                        for h in range(HP):
                            ins = pe.matmul(bank[4 + h // 4][:, h % 4 * P:h % 4 * P + P], wqT[:, h, :],
                                            wkT[:, h, :, :].rearrange("p a c -> p (a c)"), start=True, stop=True)
                            if h % 4 == 3:
                                ins.then_inc(s_mm, 1)
                        pe.wait_ge(s_cpa, 4)
                        for h in range(HP):
                            ins = pe.matmul(bank[6 + h // 4][:, h % 4 * P:h % 4 * P + P],
                                            wvT[:, h, :, :].rearrange("p a c -> p (a c)"), wo[:, h, :],
                                            start=True, stop=True)
                            if h % 4 == 3:
                                ins.then_inc(s_mm, 1)

                    @block.vector
                    def _(dve):
                        me = Self(dve, s_me)
                        dve.wait_ge(s_tr, 3)
                        dve.wait_ge(s_const, 2)
                        dve.tensor_copy(wkT[0:DC, :, 0, :], wkT_bank[0:DC]).then_inc(s_cp, 1)
                        dve.tensor_copy(wkT[DC:P, :, 1, :], wkT_bank[DC:P]).then_inc(s_cp, 1)
                        for k in range(4):
                            dve.wait_ge(s_hi, k + 1)
                            hi, lo = ((GH, GL), (VH, VL))[k // 2]
                            part = slice(4 * (k % 2), 4 * (k % 2) + 4)
                            dve.tensor_tensor(lo[:, part, :].rearrange("p h c -> p (h c)"), bank[4 + k][:, :],
                                              raw(hi[:, part, :]).rearrange("p h c -> p (h c)"),
                                              ALU.subtract).then_inc(s_lo, 1)
                        dve.wait_ge(s_x, 64)
                        with dve.Fori(0, CHUNKS) as c:
                            for j in range(CT):
                                me.done(dve.bn_stats(bs[:, j, :], X[:, c * CT + j, :]))
                            me.wait()
                            for j in range(CT):
                                me.done(dve.bn_aggr(ag[:, j, :], bs[:, j, :]))
                            me.wait()
                            me.done(dve.tensor_copy(MV[:, bass.ds(c * CT, CT), :], ag[:, :, :]))
                            me.clear()

            with ExitStack() as st1:
                XH, XL = (sb(st1, n, [P, CW], f32r) for n in ("XH", "XL"))
                QH, QL = (sb(st1, n, [P, HP, CW], f32r) for n in ("QH", "QL"))
                QB = sb(st1, "QB", [P, HP, CW], bf16)
                CH, CL = (sb(st1, n, [P, CT * BPT, P], f32r) for n in ("CH", "CL"))
                CB = sb(st1, "CB", [P, CT * BPT, P], bf16)
                PT = sb(st1, "PT", [P, HP, P])
                On = sb(st1, "On", [P, HEADS, HD])
                OH, OL = (sb(st1, n, [P, HP, CW], f32r) for n in ("OH", "OL"))
                xn, stt = sb(st1, "xn1", [P, CT, D]), sb(st1, "st1", [P, CT, 2])
                aT = sb(st1, "aT", [P, CW])
                nm = sb(st1, "nm", [P, HEADS])
                nmb = sb(st1, "nmb", [P, 2 * HEADS], bf16)
                mT = sb(st1, "mT", [2 * HEADS, P], bf16)
                rd = sb(st1, "rd", [P, HEADS])
                dve_dev, act_dev = finish_deviation(st1, "1")
                R = Ring(bank[0:2], sem(st1, "r_full"), sem(st1, "r_free"), sem(st1, "r_high"))
                A = Ring(bank[2:4], sem(st1, "scores_full"), sem(st1, "scores_free"))
                T = Ring(bank[4:6], sem(st1, "scoresT_full"), sem(st1, "scoresT_free"))
                O = Ring(bank[6:8], sem(st1, "o_full"), sem(st1, "o_free"))
                s_me, s_xn, s_nm = (sem(st1, n) for n in ("s1_me", "s1_xn", "s1_nm"))
                s_qb, s_cb, s_bo = (sem(st1, n) for n in ("s1_qb", "s1_cb", "s1_bo"))
                s_stt = sem(st1, "s1_st_t")
                s_stv = [sem(st1, f"s1_st_v{j}") for j in range(CT)]
                R0, RN, A0, AN, TN, ON = 12, 20, 2, 8, 8, 18
                GRP = [(0, 3), (3, 6), (6, HP)]

                ctx_k = ctx_in.rearrange("b k s -> k b s")

                def pv_item(c, j):
                    return c * ON + 4 * j + 1

                def chunk_order(c, more, do):
                    r, a, t, o = R0 + c * RN, A0 + c * AN, c * TN, c * ON
                    turned = (2, 4, 6, 18) if more else (0, 2, 4, 6)
                    for j in range(CT - 1):
                        do("scoresT", j, t, 2 * j, c, r - 1)
                        if j:
                            do("turn", j - 1, r, turned[j - 1], c)
                        do("max", j + 1, a, 2 * j, c)
                        do("pv", j, o, 4 * j + 1, c)
                        do("maxT", j + 1, o, 4 * j + 4, c)
                        if more and j == 0:
                            do("norm", 0, 0, 0, c + 1)
                            do("normT", 0, r, 0, c + 1)
                    do("scoresT", 3, t, 6, c)
                    do("turn", 2, r, turned[2], c)
                    if more:
                        do("ctxT", 0, r, 8, c + 1)
                        for h in range(HP // 2):
                            do("query", h, r, 10 + h, c + 1, r + 1)
                    do("pv", 3, o, 13, c)
                    if more:
                        for h in range(HP // 2, HP):
                            do("query", h, r, 10 + h, c + 1, r + 1)
                    do("turn", 3, r, turned[3], c)
                    if more:
                        do("max", 0, a, 6, c + 1)
                    do("project", 0, o, 16, c, r + turned[3] + 1)
                    do("back", 0, o, 17, c)
                    if more:
                        do("maxT", 0, o, 18, c + 1)

                def start_order(do):
                    do("norm", 0, 0, 0, 0)
                    do("normT", 0, 0, 0, 0)
                    do("ctxT", 0, 0, 2, 0)
                    for h in range(HP):
                        do("query", h, 0, 4 + h, 0, 1)
                    do("max", 0, 0, 0, 0)
                    do("maxT", 0, 0, 0, 0)

                def run(eng, do, clear=lambda: None):
                    start_order(do)
                    clear()
                    with eng.Fori(0, CHUNKS - 1) as c:
                        chunk_order(c, True, do)
                        clear()
                    chunk_order(CHUNKS - 1, False, do)

                with nc.Block() as block:
                    @block.sync
                    def _(sp):
                        def load_t(c):
                            for par in range(2):
                                sp.dma_start(st_t[par * S:(par + 1) * S, :, par * DC:(par + 1) * DC],
                                             ctx_k[:, bass.ds(c * CT * BPT, CT * BPT), :]).then_inc(s_stt, 16)

                        def load_v(c, j):
                            for par in range(2):
                                sp.dma_start(st_v[par * S:(par + 1) * S, j, :, par, 0:DC],
                                             ctx_k[:, bass.ds((c * CT + j) * BPT, BPT), :]).then_inc(s_stv[j], 16)
                        load_t(0)
                        for j in range(CT):
                            load_v(0, j)
                        sp.wait_ge(R.full, 4)
                        load_t(1)
                        for to, shared, routed in ((w1n, Ws1, W1), (w2n, Ws2, W2)):
                            for k, (h, n) in enumerate(HK):
                                sp.dma_start(to[0:n, 0, k, :], shared[h:h + n, :]).then_inc(s_w0, 16)
                                sp.dma_start(to[0:n, 1:E0, k, :],
                                             routed[:, h:h + n, :].rearrange("e h d -> h e d")).then_inc(s_w0, 16)
                        sp.dma_start(w3n[:, 0, :], Ws3).then_inc(s_w0, 16)
                        sp.dma_start(w3n[:, 1:E0, :], W3.rearrange("e d h -> d e h")).then_inc(s_w0, 16)
                        sp.dma_start(wgn[:, :], Wg).then_inc(s_w0, 16)
                        sp.dma_start(rb_bc[:, :], rbias.rearrange("(a e) -> a e", a=1).to_broadcast([P, ER])).then_inc(s_w0, 16)

                        def refill(c):
                            for j in range(CT):
                                sp.wait_ge(O.full, pv_item(c - 1, j) + 3)
                                load_v(c, j)
                        with sp.Fori(1, CHUNKS - 1) as c:
                            refill(c)
                            sp.wait_ge(R.full, R0 + (c - 1) * RN + 10)
                            load_t(c + 1)
                        refill(CHUNKS - 1)

                    @block.tensor
                    def _(pe):
                        def do(stage, j, base, k, c, needs=None):
                            n = base + k
                            if stage == "normT":
                                pe.wait_ge(s_xn, c + 1)
                                for i in range(2):
                                    R.wait_free(pe, n + i)
                                    for q in range(2):
                                        ins = pe.transpose(R.bank(k + i)[:, q * P:(q + 1) * P], xn[:, 2 * i + q, :], ident[:, :])
                                    ins.then_inc(R.full, 1)
                            elif stage == "ctxT":
                                pe.wait_ge(s_stt, 32 * (c + 1))
                                for i in range(2):
                                    R.wait_free(pe, n + i)
                                    for q in range(4):
                                        ins = pe.transpose(R.bank(k + i)[:, q * P:(q + 1) * P], st_t[:, 4 * i + q, :], ident[:, :])
                                    ins.then_inc(R.full, 1)
                            elif stage == "query":
                                if j == 0:
                                    R.wait_read(pe, needs)
                                R.wait_free(pe, n)
                                for i, (w, v) in enumerate(((GH, XH), (GL, XH), (GH, XL))):
                                    ins = pe.matmul(R.bank(k)[:, :], w[:, j, :], v[:, :], start=(i == 0), stop=(i == 2))
                                ins.then_inc(R.full, 1)
                            elif stage == "max":
                                if j == 0:
                                    pe.wait_ge(s_cb, c + 1)
                                for i in range(2):
                                    A.wait_free(pe, n + i)
                                    for h in range(4 * i, 4 * i + 4):
                                        if j == 0:
                                            pe.wait_ge(s_qb, HP * c + h + 1)
                                        for b in range(BPT):
                                            ins = pe.matmul(A.bank(k + i)[b * S:(b + 1) * S, h % 4 * P:(h % 4 + 1) * P],
                                                            QB[:, h, j * P + b * S:j * P + (b + 1) * S],
                                                            CB[:, j * BPT + b, :], start=True, stop=True,
                                                            skip_group_check=True)
                                    ins.then_inc(A.full, 1)
                            elif stage == "maxT":
                                pe.wait_ge(s_nm, c * CT + j + 1)
                                O.wait_free(pe, n)
                                pe.transpose(O.bank(k)[0:2 * HEADS, 0:S].bitcast(bf16), nmb[:, :], identb[:, :]).then_inc(O.full, 1)
                            elif stage == "scoresT":
                                if j == 0:
                                    R.wait_read(pe, needs)
                                for i in range(2):
                                    T.wait_free(pe, n + i)
                                    to = T.bank(k + i)[:, :].rearrange("p (h q) -> p h q", h=4)
                                    hs = slice(4 * i, 4 * i + 4)
                                    for b in range(BPT):
                                        q = slice(j * P + b * S, j * P + (b + 1) * S)
                                        for m, (w, v) in enumerate(((CH, QH), (CL, QH), (CH, QL))):
                                            pe.matmul(to[:, :, b * S:(b + 1) * S], w[:, j * BPT + b, :], v[:, hs, q],
                                                      start=(b == 0 and m == 0), stop=False, skip_group_check=True)
                                    if i == 0:
                                        O.wait_read(pe, c * ON + 4 * j)
                                    for h in range(4):
                                        ins = pe.matmul(to[:, h, :], sel[:, 4 * i + h, :, :].rearrange("p a c -> p (a c)"),
                                                        mT[:, :], start=False, stop=(h == 3), skip_group_check=True)
                                    ins.then_inc(T.full, 1)
                            elif stage == "pv":
                                pe.wait_ge(s_stv[j], 32 * (c + 1))
                                for g, (h0, h1) in enumerate(GRP):
                                    T.wait_read(pe, c * TN + 2 * j + (h1 > 4))
                                    O.wait_free(pe, n + g)
                                    for h in range(h0, h1):
                                        for b in range(BPT):
                                            ins = pe.matmul(O.bank(k + g)[b * S:(b + 1) * S, (h - h0) * 130:(h - h0 + 1) * 130],
                                                            PT[:, h, b * S:(b + 1) * S],
                                                            st_v[:, j, b, :, :].rearrange("p a c -> p (a c)"),
                                                            start=True, stop=True, skip_group_check=True)
                                    ins.then_inc(O.full, 1)
                            elif stage == "turn":
                                O.wait_read(pe, pv_item(c, j) + 2)
                                for i in range(2):
                                    R.wait_free(pe, n + i)
                                    for q in range(4):
                                        h = 4 * i + q
                                        ins = pe.transpose(R.bank(k + i)[:, q * P:(q + 1) * P],
                                                           On[:, 2 * h:2 * h + 2, :].rearrange("p a c -> p (a c)"), ident[:, :])
                                    ins.then_inc(R.full, 1)
                            elif stage == "project":
                                R.wait_read(pe, needs)
                                O.wait_free(pe, n)
                                steps = [(w, v, h) for h in range(HP) for w, v in ((VH, OH), (VH, OL), (VL, OH))]
                                for i, (w, v, h) in enumerate(steps):
                                    ins = pe.matmul(O.bank(k)[:, :], w[:, h, :], v[:, h, :],
                                                    start=(i == 0), stop=(i == len(steps) - 1))
                                ins.then_inc(O.full, 1)
                            elif stage == "back":
                                O.wait_read(pe, n - 1)
                                O.wait_free(pe, n)
                                for q in range(CT):
                                    ins = pe.transpose(O.bank(k)[:, q * P:(q + 1) * P], aT[:, q * P:(q + 1) * P], ident[:, :])
                                ins.then_inc(O.full, 1)
                        run(pe, do)

                    @block.scalar
                    def _(act):
                        act_dev(act)
                        act.sem_inc(T.free, 2)

                        def high(to, k, n, width=512, heads=1):
                            R.wait_full(act, n)
                            got = R.bank(k)[:, 0:width]
                            if heads > 1:
                                got = got.rearrange("p (h q) -> p h q", h=heads)
                            act.copy(to, got).then_inc(R.mid, 1)

                        def do(stage, j, base, k, c, needs=None):
                            n = base + k
                            if stage == "normT":
                                for i in range(2):
                                    high(XH[:, i * 2 * P:(i + 1) * 2 * P], k + i, n + i, 2 * P)
                            elif stage == "ctxT":
                                for i in range(2):
                                    high(CH[:, 4 * i:4 * i + 4, :].rearrange("p h c -> p (h c)"), k + i, n + i)
                                R.wait_mid(act, n + 1)
                                act.copy(CB[:, :, :], raw(CH[:, :, :])).then_inc(s_cb, 1)
                            elif stage == "query":
                                high(QH[:, j, :], k, n)
                                R.wait_mid(act, n)
                                act.copy(QB[:, j, :], raw(QH[:, j, :])).then_inc(s_qb, 1)
                            elif stage == "turn":
                                for i in range(2):
                                    high(OH[:, 4 * i:4 * i + 4, j * P:(j + 1) * P], k + i, n + i, heads=4)
                            elif stage == "scoresT":
                                for i in range(2):
                                    T.wait_full(act, n + i)
                                    act.activation(PT[:, 4 * i:4 * i + 4, :].rearrange("p h c -> p (h c)"),
                                                   T.bank(k + i)[:, :], ACT.Exp).then_inc(T.free, 1)
                        run(act, do)

                    @block.gpsimd
                    def _(pool):
                        def do(stage, j, base, k, c, needs=None):
                            n = base + k
                            if stage == "norm":
                                pool.wait_ge(s_xn, c + 1)
                                for q in range(CT):
                                    ins = pool.tensor_tensor(X[:, c * CT + q, :], X[:, c * CT + q, :], bo_bc[:, :], ALU.add)
                                ins.then_inc(s_bo, 1)
                        run(pool, do)

                    @block.vector
                    def _(dve):
                        me = Self(dve, s_me)
                        dve.sem_inc(R.free, 2)
                        dve.sem_inc(A.free, 2)
                        dve.sem_inc(O.free, 2)
                        dve_dev(dve, me)

                        def low(hi, lo, k, n, width=512, heads=1):
                            R.wait_mid(dve, n)
                            got = R.bank(k)[:, 0:width]
                            if heads > 1:
                                got = got.rearrange("p (h q) -> p h q", h=heads)
                            dve.tensor_tensor(lo, got, raw(hi), ALU.subtract).then_inc(R.free, 1)

                        def do(stage, j, base, k, c, needs=None):
                            n = base + k
                            if stage == "norm":
                                normalise(dve, me, stt, xn, c, s_xn)
                            elif stage == "normT":
                                for i in range(2):
                                    part = slice(i * 2 * P, (i + 1) * 2 * P)
                                    low(XH[:, part], XL[:, part], k + i, n + i, 2 * P)
                            elif stage == "ctxT":
                                for i in range(2):
                                    low(CH[:, 4 * i:4 * i + 4, :].rearrange("p h c -> p (h c)"),
                                        CL[:, 4 * i:4 * i + 4, :].rearrange("p h c -> p (h c)"), k + i, n + i)
                            elif stage == "turn":
                                for i in range(2):
                                    hs, q = slice(4 * i, 4 * i + 4), slice(j * P, (j + 1) * P)
                                    low(OH[:, hs, q], OL[:, hs, q], k + i, n + i, heads=4)
                            elif stage == "query":
                                low(QH[:, j, :], QL[:, j, :], k, n)
                            elif stage == "max":
                                for i in range(2):
                                    A.wait_full(dve, n + i)
                                    dve.tensor_reduce(nm[:, 8 * i:8 * i + 8], A.bank(k + i)[:, :].rearrange("p (h s) -> p h s", s=S),
                                                      AX.X, ALU.max, negate=True).then_inc(A.free, 1)
                                A.wait_read(dve, n + 1)
                                me.done(dve.tensor_copy(nmb[:, 0:HEADS], nm[:, :]))
                                me.wait()
                                dve.tensor_tensor(nmb[:, HEADS:2 * HEADS], nm[:, :], nmb[:, 0:HEADS], ALU.subtract).then_inc(s_nm, 1)
                            elif stage == "maxT":
                                O.wait_full(dve, n)
                                dve.tensor_copy(mT[:, :], O.bank(k)[0:2 * HEADS, 0:S].bitcast(bf16)).then_inc(O.free, 1)
                            elif stage == "pv":
                                for g, (h0, h1) in enumerate(GRP):
                                    O.wait_full(dve, n + g)
                                    w = 2 * (h1 - h0)
                                    got = O.bank(k + g)[:, 0:w * 65].rearrange("p (h c) -> p h c", c=65)
                                    me.done(dve.reciprocal(rd[:, 2 * h0:2 * h1], got[:, :, 64]))
                                    me.wait()
                                    dve.tensor_tensor(On[:, 2 * h0:2 * h1, :], got[:, :, 0:HD],
                                                      rd[:, 2 * h0:2 * h1].rearrange("p (h a) -> p h a", a=1).to_broadcast([P, w, HD]),
                                                      ALU.mult).then_inc(O.free, 1)
                            elif stage == "project":
                                O.wait_full(dve, n)
                                dve.tensor_copy(aT[:, :], O.bank(k)[:, :]).then_inc(O.free, 1)
                            elif stage == "back":
                                O.wait_full(dve, n)
                                dve.wait_ge(s_bo, c + 1)
                                residual(dve, me, bs, ag, O.bank(k), c, O.free)
                        run(dve, do, me.clear)
                        me.wait()

        def turn_weights(name, st, s_in, loads, items):
            K = Ring(bank[0:6], sem(st, name + "_full"), sem(st, name + "_free"), sem(st, name + "_high"))
            with nc.Block() as block:
                @block.sync
                def _(sp):
                    sp.wait_ge(s_in, 16 * loads)

                @block.tensor
                def _(pe):
                    pe.wait_ge(s_in, 16 * loads)
                    for n, (parts, rows, cols, hi, lo) in enumerate(items):
                        K.wait_free(pe, n)
                        for col, m, src in parts:
                            ins = pe.transpose(K.bank(n)[0:rows, col:col + m], src, ident[0:m, 0:m])
                        ins.then_inc(K.full, 1)

                @block.scalar
                def _(act):
                    for n, (parts, rows, cols, hi, lo) in enumerate(items):
                        K.wait_full(act, n)
                        act.copy(hi, K.bank(n)[0:rows, 0:cols]).then_inc(K.mid, 1)

                @block.vector
                def _(dve):
                    dve.sem_inc(K.free, len(K.banks))
                    for n, (parts, rows, cols, hi, lo) in enumerate(items):
                        K.wait_mid(dve, n)
                        dve.tensor_tensor(lo, K.bank(n)[0:rows, 0:cols], raw(hi), ALU.subtract).then_inc(K.free, 1)

        def make_selector(st, name, n):
            f, r = sb(st, name + "f", [n, n, P]), sb(st, name, [n, n, P], f32r)
            s = sem(st, name + "_made")
            with nc.Block() as block:
                @block.gpsimd
                def _(pool):
                    pool.memset(f[:, :, :], 0.0).then_inc(s, 1)
                    pool.wait_ge(s, 1)
                    pool.affine_select(out=f[:, :, :], in_=f[:, :, :], compare_op=ALU.not_equal, fill=1.0, base=0,
                                       pattern=[[-1, n], [0, P]], channel_multiplier=1).then_inc(s, 1)

                @block.vector
                def _(dve):
                    dve.wait_ge(s, 2)
                    dve.tensor_copy(r[:, :, :], f[:, :, :]).then_inc(s, 1)
                    dve.wait_ge(s, 3)
            return r

        def experts_phase(tag, st, nexp, nparts, up, down, rows, first_w, sel_e, gates):
            glu = len(up(0)) == 2
            NU, NW = nexp * nparts, nexp - first_w
            XH, XL = (sb(st, n + tag, [P, CW], f32r) for n in ("XH", "XL"))
            xn, stt = sb(st, "xn" + tag, [P, CT, D]), sb(st, "stt" + tag, [P, CT, 2])
            bs, ag = sb(st, "bs" + tag, [P, CT, 6]), sb(st, "ag" + tag, [P, CT, 2])
            act1 = sb(st, "act1" + tag, [P, 2, CW]) if glu else None
            prod = sb(st, "prod" + tag, [P, 2, CW]) if glu else None
            HH, HL = (sb(st, n + tag, [P, 2, CW], f32r) for n in ("HH", "HL"))
            wtok = sb(st, "wtok" + tag, [P, CT, ER])
            WTH, WTL = (sb(st, n + tag, [ER, CW], f32r) for n in ("WTH", "WTL"))
            WB = sb(st, "WB" + tag, [P, 2, CW])
            tmp, acc = sb(st, "tmp" + tag, [P, 2, CW]), sb(st, "acc" + tag, [P, CW])
            dve_dev, act_dev = finish_deviation(st, tag)
            U1 = Ring(bank[0:2] if glu else bank[0:4], sem(st, "u1_full" + tag), sem(st, "u1_free" + tag), sem(st, "u1_high" + tag))
            U2 = Ring(bank[2:4], sem(st, "u2_full" + tag), sem(st, "u2_free" + tag))
            EO = Ring(bank[4:6], None, sem(st, "eo_free" + tag))
            R = Ring(bank[6:7], sem(st, "r_full" + tag), sem(st, "r_free" + tag), sem(st, "r_high" + tag))
            WBK = Ring(bank[7:8], sem(st, "wb_full" + tag), sem(st, "wb_free" + tag))
            s_me, s_pool, s_xn, s_hi, s_lo, s_down, s_wtok, s_acc = (
                sem(st, n + tag) for n in ("me", "pool", "x_normal", "h_high", "h_low", "down_done", "w_ready", "acc_added"))
            WEIGH = nparts + 2
            NORM = max(NU - 8, NU // 2)
            LAG = 2

            def again(v, n, odd):
                return n if odd and v == 0 else n - 1

            def wait_count(eng, sem_, value):
                if not (isinstance(value, int) and value <= 0):
                    eng.wait_ge(sem_, value)

            r0 = gates.r0

            def r_item(c, i):
                return 4 * c + r0 + i

            def x_item(c):
                return r0 if isinstance(c, int) and c == 0 else r_item(c - 1, 3)

            def order(c, first, last, do):
                for v in range(NU + LAG + 1):
                    if v < NU:
                        do("up", v, c)
                    if v == 1 and not first:
                        do("back", r_item(c, 0), c - 1)
                    for stage, step, i, ahead in gates.stages:
                        if v == step and not (ahead and last):
                            do(stage, r_item(c, i), c + 1 if ahead else c)
                    if v == NORM and not last:
                        do("norm", 0, c + 1)
                    if v == NU and not last:
                        do("normT", r_item(c, 3), c + 1)
                    if 0 <= v - 1 < NU:
                        do("hidden", v - 1, c)
                    if 0 <= v - LAG < NU:
                        do("down", v - LAG, c)
                    e, k = divmod(v - nparts + 1, nparts)
                    if k == 0 and first_w <= e < nexp:
                        do("spread", e, c)
                    e, k = divmod(v - WEIGH, nparts)
                    if k == 0 and 0 <= e < nexp:
                        do("weigh", e, c)
                if (nexp - 1) * nparts + WEIGH > NU + LAG:
                    do("weigh", nexp - 1, c)

            def run(eng, do, clear=lambda: None):
                if r0:
                    for stage in gates.ahead:
                        do(stage, 0, 0)
                do("norm", 0, 0)
                do("normT", r0, 0)
                order(0, True, False, do)
                clear()
                with eng.Fori(1, CHUNKS - 1) as c:
                    order(c, False, False, do)
                    clear()
                order(CHUNKS - 1, False, True, do)
                do("back", r_item(CHUNKS - 1, 3 - r0), CHUNKS - 1)

            p = lambda ap: ap.rearrange("p t d -> p (t d)")
            with nc.Block() as block:
                @block.sync
                def _(sp):
                    gates.on_sync(sp, R)

                @block.tensor
                def _(pe):
                    def do(stage, v, c):
                        if stage == "up":
                            n = c * NU + v
                            if v == 0:
                                R.wait_read(pe, x_item(c))
                            for i, (hi, lo) in enumerate(up(v)):
                                U = (U1, U2)[i]
                                wait_count(pe, U.free, again(v, n, NU % 2) + 2 if glu else n + 1)
                                for m, (w, x_) in enumerate(((hi, XH), (lo, XH), (hi, XL))):
                                    ins = pe.matmul(U.bank(v)[0:rows(v), :], w, x_[:, :], start=(m == 0), stop=(m == 2))
                                ins.then_inc(U.full, 1)
                        elif stage == "down":
                            n = c * NU + v
                            e, k = divmod(v, nparts)
                            if glu:
                                pe.wait_ge(s_lo, n + 1)
                            else:
                                U1.wait_read(pe, n)
                            if k == 0:
                                wait_count(pe, EO.free, again(e, c * nexp + e, nexp % 2) + 2)
                            hi, lo = down(v)
                            for m, (w, h) in enumerate(((hi, HH), (lo, HH), (hi, HL))):
                                ins = pe.matmul(EO.bank(e)[:, :], w, h[0:rows(v), v % 2, :],
                                                start=(k == 0 and m == 0), stop=(k == nparts - 1 and m == 2))
                            ins.then_inc(s_down, 1)
                        elif stage == "spread":
                            n = c * NW + v - first_w
                            if v == first_w:
                                R.wait_read(pe, r_item(c, gates.turned))
                            WBK.wait_free(pe, n)
                            pe.matmul(WBK.bank(0)[:, :], sel_e[:, v - first_w, :], WTH[:, :], start=True, stop=False)
                            pe.matmul(WBK.bank(0)[:, :], sel_e[:, v - first_w, :], WTL[:, :], start=False,
                                      stop=True).then_inc(WBK.full, 1)
                        elif stage == "back":
                            pe.wait_ge(s_acc, (c + 1) * (nexp - 1))
                            R.wait_free(pe, v)
                            for j in range(CT):
                                ins = pe.transpose(R.bank(0)[:, j * P:(j + 1) * P], acc[:, j * P:(j + 1) * P], ident[:, :])
                            ins.then_inc(R.full, 1)
                        elif stage == "normT":
                            pe.wait_ge(s_xn, c + 1)
                            R.wait_free(pe, v)
                            for j in range(CT):
                                ins = pe.transpose(R.bank(0)[:, j * P:(j + 1) * P], xn[:, j, :], ident[:, :])
                            ins.then_inc(R.full, 1)
                        elif stage == "weightsT":
                            pe.wait_ge(s_wtok, c + 1)
                            R.wait_free(pe, v)
                            for j in range(CT):
                                ins = pe.transpose(R.bank(0)[0:ER, j * P:(j + 1) * P], wtok[:, j, :], ident[:, :])
                            ins.then_inc(R.full, 1)
                        elif stage in gates.own:
                            if stage == "weights":
                                R.wait_read(pe, x_item(c))
                            gates.on_tensor(pe, R, v, c, XH, XL)
                    run(pe, do)

                @block.scalar
                def _(act):
                    act_dev(act)
                    if glu:
                        act.sem_inc(U1.free, 2)
                    act.sem_inc(WBK.free, 1)

                    def do(stage, v, c):
                        n = c * NU + v
                        if stage == "up":
                            m = rows(v)
                            U1.wait_full(act, n)
                            if glu:
                                wait_count(act, U2.free, again(v, n, NU % 2) + 2)
                                act.activation(act1[0:m, v % 2, :], U1.bank(v)[0:m, :], ACT.Silu).then_inc(U1.free, 1)
                            else:
                                wait_count(act, s_down, again(v, n, NU % 2))
                                act.activation(HH[0:m, v % 2, :], U1.bank(v)[0:m, :], ACT.Relu).then_inc(U1.mid, 1)
                        elif stage == "hidden" and glu:
                            m = rows(v)
                            U2.wait_read(act, n)
                            wait_count(act, s_down, again(v, n, NU % 2))
                            act.copy(HH[0:m, v % 2, :], prod[0:m, v % 2, :]).then_inc(s_hi, 1)
                        elif stage == "spread":
                            n = c * NW + v - first_w
                            WBK.wait_full(act, n)
                            EO_done = c * nexp + v - 1
                            wait_count(act, EO.free, EO_done + 2)
                            act.copy(WB[:, (v - first_w) % 2, :], WBK.bank(0)[:, :]).then_inc(WBK.free, 1)
                        elif stage == "normT":
                            R.wait_full(act, v)
                            act.copy(XH[:, :], R.bank(0)[:, :]).then_inc(R.mid, 1)
                        elif stage in gates.scalar_stage:
                            gates.on_scalar(act, c)
                    run(act, do)

                @block.gpsimd
                def _(pool):
                    me = Self(pool, s_pool)

                    def do(stage, e, c):
                        if stage == "weigh" and e > 0:
                            EO.wait_read(pool, c * nexp + e)
                            wait_count(pool, s_acc, c * (nexp - 1) + e - 1)
                            pool.tensor_tensor(acc[:, :], acc[:, :], tmp[:, e % 2, :], ALU.add).then_inc(s_acc, 1)
                        elif stage in gates.own:
                            gates.on_gpsimd(pool, me, c)
                    run(pool, do, me.clear)

                @block.vector
                def _(dve):
                    me = Self(dve, s_me)
                    dve.sem_inc(R.free, 1)
                    dve.sem_inc(EO.free, 2)
                    dve.sem_inc(U2.free if glu else U1.free, 2 if glu else 4)
                    dve_dev(dve, me)
                    r_low = [0]

                    def do(stage, v, c):
                        n = c * NU + v
                        if stage == "up":
                            m = rows(v)
                            if glu:
                                U1.wait_read(dve, n)
                                U2.wait_full(dve, n)
                                wait_count(dve, s_hi, again(v, n, NU % 2))
                                wait_count(dve, s_lo, again(v, n, NU % 2))
                                dve.tensor_tensor(prod[0:m, v % 2, :], U2.bank(v)[0:m, :], act1[0:m, v % 2, :],
                                                  ALU.mult).then_inc(U2.free, 1)
                            else:
                                wait_count(dve, s_down, again(v, n, NU % 2))
                                U1.wait_mid(dve, n)
                                dve.scalar_tensor_tensor(HL[0:m, v % 2, :], U1.bank(v)[0:m, :], 0.0,
                                                         raw(HH[0:m, v % 2, :]), ALU.max,
                                                         ALU.subtract).then_inc(U1.free, 1)
                        elif stage == "hidden" and glu:
                            m = rows(v)
                            wait_count(dve, s_down, again(v, n, NU % 2))
                            dve.wait_ge(s_hi, n + 1)
                            dve.tensor_tensor(HL[0:m, v % 2, :], prod[0:m, v % 2, :], raw(HH[0:m, v % 2, :]),
                                              ALU.subtract).then_inc(s_lo, 1)
                        elif stage == "weigh":
                            if v > 0:
                                wait_count(dve, s_acc, c * (nexp - 1) + max(v - 2, 0))
                            if v >= first_w:
                                WBK.wait_read(dve, c * NW + v - first_w)
                            dve.wait_ge(s_down, c * NU + (v + 1) * nparts)
                            to = tmp[:, v % 2, :] if v else acc[:, :]
                            if v < first_w:
                                ins = dve.tensor_copy(to, EO.bank(v)[:, :])
                            else:
                                ins = dve.tensor_tensor(to, EO.bank(v)[:, :], WB[:, (v - first_w) % 2, :], ALU.mult)
                            ins.then_inc(EO.free, 1)
                        elif stage == "norm":
                            normalise(dve, me, stt, xn, c, s_xn)
                        elif stage == "normT":
                            R.wait_mid(dve, x_number(c))
                            dve.tensor_tensor(XL[:, :], R.bank(0)[:, :], raw(XH[:, :]), ALU.subtract).then_inc(R.free, 1)
                        elif stage == "weightsT":
                            R.wait_full(dve, v)
                            me.done(dve.tensor_copy(WTH[:, :], R.bank(0)[0:ER, :]))
                            me.wait()
                            dve.tensor_tensor(WTL[:, :], R.bank(0)[0:ER, :], raw(WTH[:, :]), ALU.subtract).then_inc(R.free, 1)
                        elif stage == "back":
                            R.wait_full(dve, v)
                            residual(dve, me, bs, ag, R.bank(0), c, R.free)
                        elif stage in gates.own:
                            gates.on_vector(dve, me, R, v, c, wtok, s_wtok)
                    run(dve, do, me.clear)
                    me.wait()

        def x_number(c):
            return c

        class Router:
            r0, turned, own, scalar_stage = 0, 2, ("weights",), ("weights",)
            stages = (("weights", 1, 1, False), ("weightsT", 5, 2, False))

            def __init__(self, st, wgT):
                self.wgH, self.wgL = wgT
                self.lg, self.ex, self.w0 = (sb(st, n, [P, CT, ER]) for n in ("logits", "exps", "w_raw"))
                self.mx, self.total = sb(st, "mx", [P, CT]), sb(st, "w_total", [P, CT])
                self.gt, self.eq = (sb(st, n, [P, CT, ER, ER]) for n in ("gt", "eq"))
                self.lower = sb(st, "lower", [P, ER, ER])
                self.s_sub, self.s_exp, self.s_tri = (sem(st, n) for n in ("s_sub", "s_exp", "s_tri"))
                with nc.Block() as block:
                    @block.gpsimd
                    def _(pool):
                        pool.memset(self.lower[:, :, :], 1.0).then_inc(self.s_tri, 1)
                        pool.wait_ge(self.s_tri, 1)
                        pool.affine_select(out=self.lower[:, :, :], in_=self.lower[:, :, :], compare_op=ALU.is_gt,
                                           fill=0.0, base=0, pattern=[[1, ER], [-1, ER]],
                                           channel_multiplier=0).then_inc(self.s_tri, 1)

            def on_sync(self, sp, R):
                pass

            def on_tensor(self, pe, R, n, c, XH, XL):
                R.wait_free(pe, n)
                for j in range(CT):
                    q = slice(j * P, (j + 1) * P)
                    for m, (x_, w) in enumerate(((XH, self.wgH), (XL, self.wgH), (XH, self.wgL))):
                        ins = pe.matmul(R.bank(0)[:, j * ER:(j + 1) * ER], x_[:, q], w[:, :], start=(m == 0), stop=(m == 2))
                ins.then_inc(R.full, 1)

            def on_scalar(self, act, c):
                act.wait_ge(self.s_sub, c + 1)
                act.activation(self.ex[:, :, :], self.ex[:, :, :], ACT.Exp).then_inc(self.s_exp, 1)

            def on_gpsimd(self, pool, me, c):
                pass

            def on_vector(self, dve, me, R, n, c, wtok, s_wtok):
                lg, ex = self.lg, self.ex
                wide = [P, CT, ER, ER]
                R.wait_full(dve, n)
                me.done(dve.tensor_tensor(lg[:, :, :], R.bank(0)[:, 0:CT * ER].rearrange("p (t e) -> p t e", t=CT),
                                          rb_bc[:, :].rearrange("p (a e) -> p a e", a=1).to_broadcast([P, CT, ER]), ALU.add))
                me.wait()
                me.done(dve.tensor_reduce(self.mx[:, :], lg[:, :, :], AX.X, ALU.max))
                me.wait()
                dve.tensor_tensor(ex[:, :, :], lg[:, :, :], self.mx[:, :].rearrange("p (t a) -> p t a", a=1).to_broadcast([P, CT, ER]),
                                  ALU.subtract).then_inc(self.s_sub, 1)
                other = lg[:, :, :].rearrange("p t (a f) -> p t a f", a=1).to_broadcast(wide)
                mine = lg[:, :, :].rearrange("p t (e a) -> p t e a", a=1).to_broadcast(wide)
                me.done(dve.tensor_tensor(self.gt[:, :, :, :], other, mine, ALU.is_gt))
                me.done(dve.tensor_tensor(self.eq[:, :, :, :], other, mine, ALU.is_equal))
                me.wait()
                me.done(dve.tensor_tensor(self.eq[:, :, :, :], self.eq[:, :, :, :],
                                          self.lower[:, :, :].rearrange("p (a e) f -> p a e f", a=1).to_broadcast(wide), ALU.mult))
                me.wait()
                me.done(dve.tensor_tensor(self.gt[:, :, :, :], self.gt[:, :, :, :], self.eq[:, :, :, :], ALU.add))
                me.wait()
                me.done(dve.tensor_reduce(self.w0[:, :, :], self.gt[:, :, :, :], AX.X, ALU.add))
                dve.wait_ge(self.s_exp, c + 1)
                me.wait()
                me.done(dve.scalar_tensor_tensor(self.w0[:, :, :], self.w0[:, :, :], float(TOPK), ex[:, :, :], ALU.is_lt, ALU.mult))
                me.wait()
                me.done(dve.tensor_reduce(self.total[:, :], self.w0[:, :, :], AX.X, ALU.add))
                me.wait()
                me.done(dve.reciprocal(self.total[:, :], self.total[:, :]))
                me.wait()
                me.done(dve.tensor_tensor(wtok[:, :, :], self.w0[:, :, :],
                                          self.total[:, :].rearrange("p (t a) -> p t a", a=1).to_broadcast([P, CT, ER]), ALU.mult))
                me.wait()
                dve.sem_inc(R.free, 1)
                dve.sem_inc(s_wtok, 1)

        class Gates:
            r0, turned, own, scalar_stage, ahead = 1, 1, ("sums",), ("names",), ("names", "sums")
            stages = (("weightsT", 1, 1, False), ("names", 4, 2, True), ("sums", 6, 2, True))

            def __init__(self, st):
                nb = CT * BPT
                self.cn, self.itn = sb(st, "cn", [S, nb, DC]), sb(st, "itn", [S, nb, S], int32)
                self.itf = sb(st, "itf", [S, nb, S])
                self.pair = sb(st, "pair", [P, 2, CT, S])
                self.masked = sb(st, "masked", [P, ER, CT, S])
                self.s_in, self.s_itf = sem(st, "s3_in"), sem(st, "s3_itf")

            def on_sync(self, sp, R):
                ck, ik = ctx_in.rearrange("b k s -> k b s"), itok.rearrange("b k s -> k b s")
                nb = CT * BPT

                def load(c):
                    sp.dma_start(self.cn[:, :, :], ck[:, bass.ds(c * nb, nb), :]).then_inc(self.s_in, 16)
                    sp.dma_start(self.itn[:, :, :], ik[:, bass.ds(c * nb, nb), :]).then_inc(self.s_in, 16)
                load(0)
                R.wait_full(sp, 0)
                load(1)
                with sp.Fori(2, CHUNKS) as c:
                    R.wait_full(sp, 4 * c - 5)
                    load(c)

            def on_gpsimd(self, pool, me, c):
                pass

            def on_scalar(self, act, c):
                act.wait_ge(self.s_in, 32 * (c + 1))
                act.copy(self.itf[:, :, :], self.itn[:, :, :]).then_inc(self.s_itf, 1)

            def on_tensor(self, pe, R, n, c, XH, XL):
                pe.wait_ge(self.s_in, 32 * (c + 1))
                pe.wait_ge(self.s_itf, c + 1)
                R.wait_free(pe, n)
                for i, src in enumerate((self.cn, self.itf)):
                    for j in range(CT):
                        at = (i * CT + j) * S
                        ins = pe.matmul(R.bank(0)[:, at:at + S], src[:, j * BPT:(j + 1) * BPT, :].rearrange("k b s -> k (b s)"),
                                        ident[0:S, 0:S], start=True, stop=True)
                ins.then_inc(R.full, 1)

            def on_vector(self, dve, me, R, n, c, wtok, s_wtok):
                R.wait_full(dve, n)
                dve.tensor_copy(self.pair[:, :, :, :].rearrange("p i t k -> p (i t k)"), R.bank(0)[:, :]).then_inc(R.free, 1)
                R.wait_read(dve, n)
                for e in range(E1):
                    me.done(dve.scalar_tensor_tensor(self.masked[:, e, :, :], self.pair[:, 1, :, :], float(e),
                                                     self.pair[:, 0, :, :], ALU.is_equal, ALU.mult))
                me.wait()
                dve.tensor_reduce(wtok[:, :, :].rearrange("p t e -> p e t"), self.masked[:, :, :, :], AX.X,
                                  ALU.add).then_inc(s_wtok, 1)

        pin_n = sb(top, "pin_n", [P, E1 * D1 // P, D])
        pout_n = sb(top, "pout_n", [D, E1, D1])
        q_n = [sb(top, "wgate_n", [P, I1 // P, D]), sb(top, "wup_n", [P, I1 // P, D]), sb(top, "wdown_n", [D, I1])]
        s_w1 = sem(top, "s_w1")

        if phases >= 2:
            with ExitStack() as st2:
                W1H, W1L, W2H, W2L = (sb(st2, n, [D, E0, H0], f32r) for n in ("W1H", "W1L", "W2H", "W2L"))
                W3H, W3L = (sb(st2, n, [P, len(HK), E0, D], f32r) for n in ("W3H", "W3L"))
                wgH, wgL = (sb(st2, n, [D, ER], f32r) for n in ("wgH", "wgL"))
                items = [([(0, ER, wgn[:, :])], P, ER, wgH[:, :], wgL[:, :])]
                for src, hi, lo in ((w1n, W1H, W1L), (w2n, W2H, W2L)):
                    for e in range(E0):
                        items.append(([(h, n, src[0:n, e, k, :]) for k, (h, n) in enumerate(HK)], D, H0,
                                      hi[:, e, :], lo[:, e, :]))
                for k, (h, n) in enumerate(HK):
                    for e in range(0, E0, 4):
                        m = min(4, E0 - e)
                        flat = lambda w: w[0:n, k, e:e + m, :].rearrange("p e d -> p (e d)")
                        items.append(([(i * D, D, w3n[:, e + i, h:h + n]) for i in range(m)], n, m * D, flat(W3H), flat(W3L)))
                with nc.Block() as block:
                    @block.sync
                    def _(sp):
                        sp.dma_start(pin_n[:, :, :], p_in.rearrange("e (h p) i -> p (e h) i", p=P)).then_inc(s_w1, 16)
                        sp.dma_start(pout_n[:, :, :], p_out.rearrange("e i d -> i e d")).then_inc(s_w1, 16)
                        sp.dma_start(q_n[0][:, :, :], w_gate.rearrange("(k p) i -> p k i", p=P)).then_inc(s_w1, 16)
                        sp.dma_start(q_n[1][:, :, :], w_up.rearrange("(k p) i -> p k i", p=P)).then_inc(s_w1, 16)
                        sp.dma_start(q_n[2][:, :], w_down).then_inc(s_w1, 16)
                with ExitStack() as st:
                    turn_weights("k0", st, s_w0, W0_LOADS, items)
                sel_e = make_selector(st2, "sel_e2", ER)
                gates = Router(st2, (wgH, wgL))

                def part(u):
                    e, k = divmod(u, len(HK))
                    return e, k, slice(HK[k][0], HK[k][0] + HK[k][1])

                def up2(u):
                    e, k, h = part(u)
                    return [(W1H[:, e, h], W1L[:, e, h]), (W2H[:, e, h], W2L[:, e, h])]

                def down2(u):
                    e, k, h = part(u)
                    return W3H[0:HK[k][1], k, e, :], W3L[0:HK[k][1], k, e, :]
                experts_phase("2", st2, E0, len(HK), up2, down2, lambda u: HK[u % len(HK)][1], E0 - ER, sel_e, gates)

        if phases >= 3:
            with ExitStack() as st3:
                PIH, PIL = (sb(st3, n, [D, E1 * D1], f32r) for n in ("PIH", "PIL"))
                POH, POL = (sb(st3, n, [P, E1 * D1 // P, D], f32r) for n in ("POH", "POL"))
                items = []
                for u in range(0, E1 * D1 // P, 4):
                    items.append(([(i * P, P, pin_n[:, u + i, :]) for i in range(4)], D, 4 * P,
                                  PIH[:, u * P:(u + 4) * P], PIL[:, u * P:(u + 4) * P]))
                    flat = lambda w: w[:, u:u + 4, :].rearrange("p u d -> p (u d)")
                    items.append(([(i * D, D, pout_n[:, (u + i) // 2, (u + i) % 2 * P:((u + i) % 2 + 1) * P]) for i in range(4)],
                                  P, 4 * D, flat(POH), flat(POL)))
                with ExitStack() as st:
                    turn_weights("k1", st, s_w1, 5, items)
                sel_e = make_selector(st3, "sel_e3", ER)
                experts_phase("3", st3, E1, D1 // P, lambda u: [(PIH[:, u * P:(u + 1) * P], PIL[:, u * P:(u + 1) * P])],
                              lambda u: (POH[:, u, :], POL[:, u, :]), lambda u: P, 0, sel_e, Gates(st3))

        if phases >= 4:
            with ExitStack() as st4:
                NQ = 3
                WQ = [sb(st4, n, [P, 4, P if n == "WQd" else P], bf16) for n in ("WQg", "WQu", "WQd")]
                ones = sb(st4, "ones4", [P, P])
                absum, mean = sb(st4, "absum", [P, NQ]), sb(st4, "meanw", [P, NQ])
                scale = sb(st4, "scalew", [P, NQ])
                wt, wi = sb(st4, "wt", [P, NQ, 4 * P]), sb(st4, "wi", [P, NQ, 4 * P], bf16)
                s_one, s_abs, s_sum, s_wi, s_wtb, s_wq, s_me = (
                    sem(st4, n) for n in ("s4_one", "s4_abs", "s4_sum", "s4_wi", "s4_wtb", "s4_wq", "s4_me0"))
                nat = [w[:, :, :].rearrange("p k i -> p (k i)") if n < 2 else w[:, :] for n, w in enumerate(q_n)]
                count = float(I1 * D)

                with nc.Block() as block:
                    @block.gpsimd
                    def _(pool):
                        pool.memset(ones[:, :], 1.0).then_inc(s_one, 1)

                    @block.tensor
                    def _(pe):
                        pe.wait_ge(s_one, 1)
                        pe.wait_ge(s_abs, NQ)
                        pe.matmul(bank[0][:, 0:NQ], ones[:, :], absum[:, :], start=True, stop=True).then_inc(s_sum, 1)
                        for n in range(NQ):
                            pe.wait_ge(s_wi, n + 1)
                            for k in range(4):
                                ins = pe.transpose(bank[1 + n][:, k * 64:(k + 1) * 64].bitcast(bf16),
                                                   wi[:, n, k * P:(k + 1) * P], identb[:, :])
                            ins.then_inc(s_wtb, 1)

                    @block.scalar
                    def _(act):
                        for n in range(NQ):
                            act.wait_ge(s_wtb, n + 1)
                            act.copy(WQ[n][:, :, :].rearrange("p k i -> p (k i)"),
                                     bank[1 + n][:, 0:256].bitcast(bf16)).then_inc(s_wq, 1)
                        act.wait_ge(s_wq, NQ)

                    @block.vector
                    def _(dve):
                        me = Self(dve, s_me)
                        dve.wait_ge(s_w1, 80)
                        for n in range(NQ):
                            dve.tensor_reduce(absum[:, n:n + 1], nat[n], AX.X, ALU.add,
                                              apply_absolute_value=True).then_inc(s_abs, 1)
                        dve.wait_ge(s_sum, 1)
                        me.done(dve.tensor_scalar(mean[:, :], bank[0][:, 0:NQ], 1.0 / count, 1e-5, ALU.mult, ALU.max))
                        me.wait()
                        me.done(dve.reciprocal(scale[:, :], mean[:, :]))
                        me.wait()
                        for n in range(NQ):
                            me.done(dve.tensor_scalar(wt[:, n, :], nat[n], scale[:, n:n + 1], ROUND, ALU.mult, ALU.add))
                        me.wait()
                        me.done(dve.tensor_scalar(wt[:, :, :], wt[:, :, :], -ROUND, 1.0, ALU.add, ALU.min))
                        me.wait()
                        for n in range(NQ):
                            dve.tensor_scalar(wi[:, n, :], wt[:, n, :], -1.0, None, ALU.max).then_inc(s_wi, 1)
                        me.done(dve.tensor_scalar(mean[:, :], mean[:, :], 1.0 / 127.0, None, ALU.mult))
                        me.wait()

                xn, stt = sb(st4, "xn4", [P, CT, D]), sb(st4, "stt4", [P, CT, 2])
                xr, xq = sb(st4, "xr4", [P, CT, D]), sb(st4, "xq4", [P, CT, D], bf16)
                xqT = sb(st4, "xqT", [D, CT, P], bf16)
                a1, r1, dg, du = (sb(st4, n, [P, CT]) for n in ("a1", "r1", "dg", "du"))
                sg, pr = sb(st4, "sg", [P, 2, I1]), sb(st4, "pr", [P, 2, I1])
                qr, qb = sb(st4, "qr", [P, 2, I1]), sb(st4, "qb", [P, 2, I1], bf16)
                qT = sb(st4, "qT", [P, 2, I1], bf16)
                a2, r2, dd = (sb(st4, n, [P, CT]) for n in ("a2", "r2", "dd"))
                dve_dev, act_dev = finish_deviation(st4, "4")
                G = Ring(bank[0:2], sem(st4, "gate_full"), sem(st4, "gate_free"))
                U = Ring(bank[2:4], sem(st4, "up_full"), sem(st4, "up_free"))
                T = Ring(bank[4:6], sem(st4, "turn_full"), sem(st4, "turn_free"))
                Y = Ring(bank[6:8], sem(st4, "y_full"), sem(st4, "y_free"))
                s_me, s_xq, s_dg, s_qr, s_qb, s_out = (
                    sem(st4, n) for n in ("s4_me", "s4_xq", "s4_dg", "s4_qr", "s4_qb", "s4_out"))
                TN4 = CT + 2

                def order4(c, more, do):
                    for j in range(CT + 1):
                        if j < CT:
                            do("first", j, c)
                        if j >= 1:
                            do("second", j - 1, c)
                        if j == 1 and more:
                            do("quant", 0, c + 1)

                def run4(eng, do, clear=lambda: None):
                    do("quant", 0, 0)
                    do("xT", 0, 0)
                    clear()
                    with eng.Fori(0, CHUNKS - 1) as c:
                        order4(c, True, do)
                        do("xT", 0, c + 1)
                        clear()
                    order4(CHUNKS - 1, False, do)

                XT = Ring(bank[4:5], T.full, T.free)
                with nc.Block() as block:
                    @block.sync
                    def _(sp):
                        def store(c):
                            Y.wait_read(sp, c * CT + CT - 1)
                            sp.dma_start(out_t[:, bass.ds(c * CT, CT), :], X[:, bass.ds(c * CT, CT), :]).then_inc(s_out, 16)
                        store(0)
                        with sp.Fori(1, CHUNKS) as c:
                            store(c)
                        sp.wait_ge(s_out, 16 * CHUNKS)

                    @block.tensor
                    def _(pe):
                        def do(stage, j, c):
                            n = c * CT + j
                            if stage == "xT":
                                pe.wait_ge(s_xq, c + 1)
                                pe.wait_ge(T.free, 5 * c + 1)
                                for q in range(CT):
                                    ins = pe.transpose(bank[4][:, q * 64:(q + 1) * 64].bitcast(bf16), xq[:, q, :], identb[:, :])
                                ins.then_inc(T.full, 1)
                            elif stage == "first":
                                if j == 0:
                                    pe.wait_ge(T.free, 5 * c + 2)
                                for R_, w in ((G, WQ[0]), (U, WQ[1])):
                                    R_.wait_free(pe, n)
                                    pe.matmul(R_.bank(j)[:, :], xqT[:, j, :], w[:, :, :].rearrange("p k i -> p (k i)"),
                                              start=True, stop=True).then_inc(R_.full, 1)
                            elif stage == "second":
                                pe.wait_ge(s_qb, n + 3)
                                pe.wait_ge(T.free, 5 * c + 1 + j)
                                b = bank[5 - j % 2]
                                for k in range(4):
                                    ins = pe.transpose(b[:, k * 64:(k + 1) * 64].bitcast(bf16),
                                                       qb[:, j % 2, k * P:(k + 1) * P], identb[:, :])
                                ins.then_inc(T.full, 1)
                                pe.wait_ge(T.free, 5 * c + 3 + j)
                                Y.wait_free(pe, n)
                                for k in range(4):
                                    ins = pe.matmul(Y.bank(j)[:, 0:D], qT[:, j % 2, k * P:(k + 1) * P], WQ[2][:, k, :],
                                                    start=(k == 0), stop=(k == 3))
                                ins.then_inc(Y.full, 1)
                        run4(pe, do)

                    @block.scalar
                    def _(act):
                        act_dev(act)
                        act.sem_inc(G.free, 2)
                        act.sem_inc(T.free, 1)
                        act.sem_inc(s_qb, 2)

                        def do(stage, j, c):
                            n = c * CT + j
                            if stage == "xT":
                                act.wait_ge(T.full, 5 * c + 1)
                                act.copy(xqT[:, :, :].rearrange("p t d -> p (t d)"), bank[4][:, 0:256].bitcast(bf16)).then_inc(T.free, 1)
                            elif stage == "first":
                                act.wait_ge(s_dg, c + 1)
                                U.wait_free(act, n)
                                G.wait_full(act, n)
                                act.activation(sg[:, j % 2, :], G.bank(j)[:, :], ACT.Silu, scale=dg[:, j:j + 1]).then_inc(G.free, 1)
                            elif stage == "second":
                                act.wait_ge(s_qr, n + 3)
                                act.activation(qb[:, j % 2, :], qr[:, j % 2, :], ACT.Copy, bias=-ROUND).then_inc(s_qb, 1)
                                act.wait_ge(T.full, 5 * c + 2 + j)
                                act.copy(qT[:, j % 2, :], bank[5 - j % 2][:, 0:256].bitcast(bf16)).then_inc(T.free, 1)
                        run4(act, do)

                    @block.vector
                    def _(dve):
                        me = Self(dve, s_me)
                        dve.sem_inc(U.free, 2)
                        dve.sem_inc(Y.free, 2)
                        dve.sem_inc(s_qr, 2)
                        dve_dev(dve, me)

                        def do(stage, j, c):
                            n = c * CT + j
                            if stage == "quant":
                                me.done(dve.tensor_copy(stt[:, :, :], MV[:, bass.ds(c * CT, CT), :]))
                                me.wait()
                                for q in range(CT):
                                    me.done(dve.tensor_scalar(xn[:, q, :], X[:, c * CT + q, :], stt[:, q, 0:1], stt[:, q, 1:2],
                                                              ALU.subtract, ALU.mult))
                                me.wait()
                                me.done(dve.tensor_reduce(a1[:, :], xn[:, :, :], AX.X, ALU.max, apply_absolute_value=True))
                                me.wait()
                                me.done(dve.tensor_scalar(a1[:, :], a1[:, :], 1e-5, None, ALU.max))
                                me.wait()
                                me.done(dve.reciprocal(r1[:, :], a1[:, :]))
                                me.wait()
                                me.done(dve.tensor_scalar(r1[:, :], r1[:, :], 127.0, None, ALU.mult))
                                me.wait()
                                for q in range(CT):
                                    me.done(dve.tensor_scalar(xr[:, q, :], xn[:, q, :], r1[:, q:q + 1], ROUND, ALU.mult, ALU.add))
                                me.wait()
                                if not (isinstance(c, int) and c == 0):
                                    dve.wait_ge(s_xq, c)
                                dve.tensor_scalar(xq[:, :, :], xr[:, :, :], -ROUND, None, ALU.add).then_inc(s_xq, 1)
                            elif stage == "xT":
                                dve.wait_ge(G.free, c * CT + 2)
                                dve.tensor_scalar(dg[:, :], a1[:, :], mean[:, 0:1], None, ALU.mult).then_inc(s_dg, 1)
                                me.done(dve.tensor_scalar(du[:, :], a1[:, :], mean[:, 1:2], None, ALU.mult))
                                me.wait()
                            elif stage == "first":
                                G.wait_read(dve, n)
                                U.wait_full(dve, n)
                                dve.wait_ge(s_qr, n + 1)
                                dve.scalar_tensor_tensor(pr[:, j % 2, :], U.bank(j)[:, :], du[:, j:j + 1], sg[:, j % 2, :],
                                                         ALU.mult, ALU.mult).then_inc(U.free, 1)
                                U.wait_read(dve, n)
                                me.wait()
                                me.done(dve.tensor_reduce(a2[:, j:j + 1], pr[:, j % 2, :], AX.X, ALU.max, apply_absolute_value=True))
                                me.wait()
                                me.done(dve.tensor_scalar(a2[:, j:j + 1], a2[:, j:j + 1], 1e-5, None, ALU.max))
                                me.wait()
                                me.done(dve.reciprocal(r2[:, j:j + 1], a2[:, j:j + 1]))
                                me.done(dve.tensor_scalar(dd[:, j:j + 1], a2[:, j:j + 1], mean[:, 2:3], None, ALU.mult))
                                me.wait()
                                me.done(dve.tensor_scalar(r2[:, j:j + 1], r2[:, j:j + 1], 127.0, None, ALU.mult))
                                me.wait()
                                dve.wait_ge(s_qb, n + 1)
                                dve.tensor_scalar(qr[:, j % 2, :], pr[:, j % 2, :], r2[:, j:j + 1], ROUND,
                                                  ALU.mult, ALU.add).then_inc(s_qr, 1)
                            elif stage == "second":
                                Y.wait_full(dve, n)
                                t = c * CT + j
                                dve.scalar_tensor_tensor(X[:, t, :], Y.bank(j)[:, 0:D], dd[:, j:j + 1], X[:, t, :],
                                                         ALU.mult, ALU.add).then_inc(Y.free, 1)
                        run4(dve, do, me.clear)
                        me.wait()

        if phases < 4:
            with ExitStack() as fin:
                s_out = sem(fin, "s_out")
                with nc.Block() as block:
                    @block.sync
                    def _(sp):
                        for q in range(4):
                            n = TILES // 4
                            sp.dma_start(out_t[:, q * n:(q + 1) * n, :], X[:, q * n:(q + 1) * n, :]).then_inc(s_out, 16)
                        sp.wait_ge(s_out, 64)



_INS = ["x", "ctx_512", "itok_BxS2xS_0_7", "L0_xattn_Wq", "L0_xattn_Wk", "L0_xattn_Wv", "L0_xattn_Wo", "L0_xattn_bo",
        "L0_ffn_Wg", "L0_ffn_routing_bias", "L0_ffn_W1", "L0_ffn_W2", "L0_ffn_W3", "L0_ffn_Ws1", "L0_ffn_Ws2",
        "L0_ffn_Ws3", "L1_xattn_proj_in", "L1_xattn_proj_out", "L1_ffn_w_gate", "L1_ffn_w_up", "L1_ffn_w_down"]


def kernel(**inputs):
    import numpy as np
    import concourse.bacc as bacc
    from concourse.bass_utils import run_bass_kernel_spmd

    nc = bacc.Bacc("TRN2", target_bir_lowering=False, num_devices=1)
    arrays, args = {}, []
    for name in _INS:
        a = np.ascontiguousarray(inputs[name])
        arrays[f"in_{name}"] = a
        args.append(nc.dram_tensor(f"in_{name}", a.shape, mybir.dt.from_np(a.dtype), kind="ExternalInput").ap())
    args.append(nc.dram_tensor("out_0", (B, S, D), fp32, kind="ExternalOutput").ap())
    kernel_program(nc, *args)
    return run_bass_kernel_spmd(nc, [arrays], core_ids=[0]).results[0]["out_0"]
```

```python
import concourse.bass as bass
from concourse import mybir
from contextlib import ExitStack

fp32 = mybir.dt.float32
f32r = mybir.dt.float32r
bf16 = mybir.dt.bfloat16
int32 = mybir.dt.int32
ALU = mybir.AluOpType
ACT = mybir.ActivationFunctionType
AX = mybir.AxisListType

B, S, D = 64, 64, 128
DC = 64
TOK = B * S
P = 128
TILES = TOK // P
CT = 4
CHUNKS = TILES // CT
CW = CT * P
BPT = P // S
HEADS, HD = 16, 64
HP = HEADS // 2
E0, H0 = 9, D * 2 * 4 // 3
ER = E0 - 1
TOPK = 4
HK = [(k, min(P, H0 - k)) for k in range(0, H0, P)]
E1, D1 = 8, 256
I1 = 512
EPS = 1e-5
ROUND = 1.5 * 2.0 ** 23


class Self:

    def __init__(self, eng, sem):
        self.eng, self.sem, self.n = eng, sem, 0

    def done(self, ins):
        ins.then_inc(self.sem, 1)
        self.n += 1

    def wait(self):
        self.eng.wait_ge(self.sem, self.n)

    def clear(self):
        self.wait()
        self.eng.sem_clear(self.sem)
        self.n = 0


class Ring:

    def __init__(self, banks, full, free, mid=None):
        self.banks, self.full, self.free, self.mid = banks, full, free, mid

    def bank(self, k):
        return self.banks[k % len(self.banks)]

    def wait_free(self, eng, n):
        eng.wait_ge(self.free, n + 1)

    def wait_full(self, eng, n):
        eng.wait_ge(self.full, n + 1)

    def wait_mid(self, eng, n):
        eng.wait_ge(self.mid, n + 1)

    def wait_read(self, eng, n):
        eng.wait_ge(self.free, n + 1 + len(self.banks))


def raw(ap):
    return ap.bitcast(fp32)


def kernel_program(nc, x, ctx_in, itok, Wq, Wk, Wv, Wo, bo, Wg, rbias, W1, W2, W3, Ws1, Ws2, Ws3,
                   p_in, p_out, w_gate, w_up, w_down, out, phases=4):
    top = ExitStack()
    with top:
        def sb(stack, name, shape, dt=fp32):
            return stack.enter_context(nc.sbuf_tensor(name, shape, dt))

        def sem(stack, name):
            return stack.enter_context(nc.semaphore(name))

        X = sb(top, "X", [P, TILES, D])
        MV = sb(top, "MV", [P, TILES, 2])
        ident = sb(top, "ident", [P, P])
        identb = sb(top, "identb", [P, P], bf16)
        w1n, w2n = (sb(top, n, [P, E0, len(HK), D]) for n in ("w1n", "w2n"))
        w3n = sb(top, "w3n", [D, E0, H0])
        wgn, rb_bc = sb(top, "wgn", [ER, D]), sb(top, "rb_bc", [P, ER])
        s_w0 = sem(top, "s_w0")
        W0_LOADS = 2 * len(HK) * 2 + 4
        bank = [top.enter_context(nc.psum_tensor(f"bank{i}", [P, 512], fp32)) for i in range(8)]
        x_t = x.rearrange("b s d -> (b s) d").rearrange("(t p) d -> p t d", p=P)
        out_t = out.rearrange("b s d -> (b s) d").rearrange("(t p) d -> p t d", p=P)


        def residual(dve, me, bs, ag, got, c, free):
            part = X[:, bass.ds(c * CT, CT), :]
            me.done(dve.tensor_tensor(part, got[:, :].rearrange("p (t d) -> p t d", t=CT), part, ALU.add))
            me.wait()
            for j in range(CT):
                ins = dve.bn_stats(bs[:, j, :], X[:, c * CT + j, :])
                if j == 0:
                    ins.then_inc(free, 1)
                else:
                    me.done(ins)
            me.wait()
            for j in range(CT):
                me.done(dve.bn_aggr(ag[:, j, :], bs[:, j, :]))
            me.wait()
            me.done(dve.tensor_copy(MV[:, bass.ds(c * CT, CT), :], ag[:, :, :]))

        def finish_deviation(stack, tag):
            dev = sb(stack, f"dev{tag}", [P, TILES])
            s_var, s_dev = sem(stack, f"s_var{tag}"), sem(stack, f"s_dev{tag}")

            def on_vector(dve, me):
                dve.tensor_scalar(dev[:, :], MV[:, :, 1], EPS, None, ALU.add).then_inc(s_var, 1)
                dve.wait_ge(s_dev, 1)
                me.done(dve.reciprocal(MV[:, :, 1], dev[:, :]))
                me.wait()

            def on_scalar(act):
                act.wait_ge(s_var, 1)
                act.activation(dev[:, :], dev[:, :], ACT.Sqrt).then_inc(s_dev, 1)
            return on_vector, on_scalar

        def normalise(dve, me, st, xn, c, signal):
            me.done(dve.tensor_copy(st[:, :, :], MV[:, bass.ds(c * CT, CT), :]))
            me.wait()
            for j in range(CT):
                ins = dve.tensor_scalar(xn[:, j, :], X[:, c * CT + j, :], st[:, j, 0:1], st[:, j, 1:2],
                                        ALU.subtract, ALU.mult)
            ins.then_inc(signal, 1)

        p1 = ExitStack()
        with p1:
            GH, GL = (sb(p1, n, [P, HP, P], f32r) for n in ("GH", "GL"))
            VH, VL = (sb(p1, n, [P, HP, P], f32r) for n in ("VH", "VL"))
            bo_bc = sb(p1, "bo_bc", [P, D])
            st_t = sb(p1, "st_t", [P, CT * BPT, P])
            st_v = sb(p1, "st_v", [P, CT, BPT, 2, DC + 1])
            sel = sb(p1, "sel", [2 * HEADS, HP, 2, S], bf16)
            bs, ag = sb(p1, "bs", [P, CT, 6]), sb(p1, "ag", [P, CT, 2])

            p0 = ExitStack()
            with p0:
                wq = sb(p0, "wq", [P, HP, P])
                wk, wv = sb(p0, "wk", [DC, HP, P]), sb(p0, "wv", [DC, HP, P])
                wo = sb(p0, "wo", [P, HP, D])
                wqT = sb(p0, "wqT", [P, HP, P])
                wkT, wvT = sb(p0, "wkT", [P, HP, 2, DC]), sb(p0, "wvT", [P, HP, 2, DC])
                bs0 = sb(p0, "bs0", [P, TILES // 2, 6])
                s_x, s_w, s_ones = [sem(p0, "s0_x0"), sem(p0, "s0_x1")], sem(p0, "s0_w"), sem(p0, "s0_bo")
                s_const, s_tr, s_cp, s_cpa = (sem(p0, n) for n in ("s0_const", "s0_tr", "s0_cp", "s0_cpa"))
                s_mm, s_hi, s_lo, s_me, s_pool = (sem(p0, n) for n in ("s0_mm", "s0_hi", "s0_lo", "s0_me", "s0_pool"))
                wkT_bank, wvT_bank = (bank[i][:, :].rearrange("p (h c) -> p h c", h=HP) for i in (2, 3))
                with nc.Block() as block:
                    @block.sync
                    def _(sp):
                        sp.dma_start(wq[:, :, :], Wq.rearrange("i (h c) -> i h c", h=HP)).then_inc(s_w, 16)
                        sp.dma_start(wk[:, :, :], Wk.rearrange("i (h c) -> i h c", h=HP)).then_inc(s_w, 16)
                        for q in range(4):
                            n = TILES // 4
                            sp.dma_start(X[:, q * n:(q + 1) * n, :], x_t[:, q * n:(q + 1) * n, :]).then_inc(s_x[q // 2], 16)

                    @block.scalar
                    def _(act):
                        act.dma_start(wv[:, :, :], Wv.rearrange("i (h c) -> i h c", h=HP)).then_inc(s_w, 16)
                        act.dma_start(wo[:, :, :], Wo.rearrange("(h p) n -> p h n", p=P)).then_inc(s_w, 16)
                        act.dma_start(bo_bc[:, :], bo.rearrange("(a n) -> a n", a=1).to_broadcast([P, D])).then_inc(s_ones, 16)
                        for k in range(2):
                            act.wait_ge(s_tr, k + 1)
                            act.activation(wqT[:, 4 * k:4 * k + 4, :].rearrange("p h c -> p (h c)"), bank[k][:, :],
                                           ACT.Copy, scale=float(HD) ** -0.5).then_inc(s_cpa, 1)
                        act.wait_ge(s_tr, 4)
                        act.wait_ge(s_const, 2)
                        act.copy(wvT[0:DC, :, 0, :], wvT_bank[0:DC]).then_inc(s_cpa, 1)
                        act.copy(wvT[DC:P, :, 1, :], wvT_bank[DC:P]).then_inc(s_cpa, 1)
                        for k in range(4):
                            act.wait_ge(s_mm, k + 1)
                            hi = (GH, VH)[k // 2]
                            act.copy(hi[:, 4 * (k % 2):4 * (k % 2) + 4, :].rearrange("p h c -> p (h c)"),
                                     bank[4 + k][:, :]).then_inc(s_hi, 1)
                        act.wait_ge(s_ones, 16)

                    @block.gpsimd
                    def _(pool):
                        me = Self(pool, s_pool)
                        me.done(pool.memset(ident[:, :], 0.0))
                        me.done(pool.memset(sel[:, :, :, :], 0.0))
                        me.wait()
                        me.done(pool.affine_select(out=ident[:, :], in_=ident[:, :], compare_op=ALU.not_equal, fill=1.0,
                                                   base=0, pattern=[[-1, P]], channel_multiplier=1))
                        me.wait()
                        pool.tensor_copy(identb[:, :], ident[:, :]).then_inc(s_const, 1)
                        pool.memset(wkT[:, :, :, :], 0.0)
                        pool.memset(wvT[:, :, :, :], 0.0).then_inc(s_const, 1)
                        for base in (0, -HEADS):
                            me.done(pool.affine_select(out=sel[:, :, :, :], in_=sel[:, :, :, :],
                                                       compare_op=ALU.not_equal, fill=1.0, base=base,
                                                       pattern=[[-2, HP], [-1, 2], [0, S]], channel_multiplier=1))
                            me.wait()
                        pool.memset(st_t[:, :, :], 0.0)
                        me.done(pool.memset(st_v[:, :, :, :, :], 0.0))
                        me.wait()
                        for par in range(2):
                            me.done(pool.memset(st_v[par * S:(par + 1) * S, :, :, par, DC:DC + 1], 1.0))
                        me.wait()

                    @block.tensor
                    def _(pe):
                        pe.wait_ge(s_const, 1)
                        pe.wait_ge(s_w, 64)
                        for h in range(HP):
                            ins = pe.transpose(bank[h // 4][:, h % 4 * P:h % 4 * P + P], wq[:, h, :], ident[:, :])
                            if h % 4 == 3:
                                ins.then_inc(s_tr, 1)
                        for w, b in ((wk, 2), (wv, 3)):
                            for h in range(HP):
                                ins = pe.transpose(bank[b][:, h * DC:(h + 1) * DC], w[:, h, :], ident[0:DC, 0:DC])
                            ins.then_inc(s_tr, 1)
                        pe.wait_ge(s_cpa, 2)
                        pe.wait_ge(s_cp, 2)
                        for h in range(HP):
                            ins = pe.matmul(bank[4 + h // 4][:, h % 4 * P:h % 4 * P + P], wqT[:, h, :],
                                            wkT[:, h, :, :].rearrange("p a c -> p (a c)"), start=True, stop=True)
                            if h % 4 == 3:
                                ins.then_inc(s_mm, 1)
                        pe.wait_ge(s_cpa, 4)
                        for h in range(HP):
                            ins = pe.matmul(bank[6 + h // 4][:, h % 4 * P:h % 4 * P + P],
                                            wvT[:, h, :, :].rearrange("p a c -> p (a c)"), wo[:, h, :],
                                            start=True, stop=True)
                            if h % 4 == 3:
                                ins.then_inc(s_mm, 1)

                    @block.vector
                    def _(dve):
                        me = Self(dve, s_me)

                        def statistics(half):
                            dve.wait_ge(s_x[half], 32)
                            for j in range(TILES // 2):
                                me.done(dve.bn_stats(bs0[:, j, :], X[:, half * (TILES // 2) + j, :]))
                            me.wait()
                            for j in range(TILES // 2):
                                me.done(dve.bn_aggr(MV[:, half * (TILES // 2) + j, :], bs0[:, j, :]))
                            me.wait()
                        dve.wait_ge(s_tr, 3)
                        dve.wait_ge(s_const, 2)
                        dve.tensor_copy(wkT[0:DC, :, 0, :], wkT_bank[0:DC]).then_inc(s_cp, 1)
                        dve.tensor_copy(wkT[DC:P, :, 1, :], wkT_bank[DC:P]).then_inc(s_cp, 1)
                        statistics(0)
                        statistics(1)
                        for k in range(4):
                            dve.wait_ge(s_hi, k + 1)
                            hi, lo = ((GH, GL), (VH, VL))[k // 2]
                            part = slice(4 * (k % 2), 4 * (k % 2) + 4)
                            dve.tensor_tensor(lo[:, part, :].rearrange("p h c -> p (h c)"), bank[4 + k][:, :],
                                              raw(hi[:, part, :]).rearrange("p h c -> p (h c)"),
                                              ALU.subtract).then_inc(s_lo, 1)

            with ExitStack() as st1:
                XH, XL = (sb(st1, n, [P, CW], f32r) for n in ("XH", "XL"))
                QH, QL = (sb(st1, n, [P, HP, CW], f32r) for n in ("QH", "QL"))
                QB = sb(st1, "QB", [P, HP, CW], bf16)
                CH, CL = (sb(st1, n, [P, CT * BPT, P], f32r) for n in ("CH", "CL"))
                CB = sb(st1, "CB", [P, CT * BPT, P], bf16)
                PT = sb(st1, "PT", [P, HP, P])
                On = sb(st1, "On", [P, HEADS, HD])
                OH, OL = (sb(st1, n, [P, HP, CW], f32r) for n in ("OH", "OL"))
                xn, stt = sb(st1, "xn1", [P, CT, D]), sb(st1, "st1", [P, CT, 2])
                aT = sb(st1, "aT", [P, CW])
                one = sb(st1, "one", [P, 1, 1])
                nm = sb(st1, "nm", [P, HEADS])
                nmb = sb(st1, "nmb", [P, 2 * HEADS], bf16)
                mT = sb(st1, "mT", [2 * HEADS, P], bf16)
                rd = sb(st1, "rd", [P, HEADS])
                dve_dev, act_dev = finish_deviation(st1, "1")
                R = Ring(bank[0:2], sem(st1, "r_full"), sem(st1, "r_free"), sem(st1, "r_high"))
                A = Ring(bank[2:4], sem(st1, "scores_full"), sem(st1, "scores_free"))
                T = Ring(bank[4:6], sem(st1, "scoresT_full"), sem(st1, "scoresT_free"), sem(st1, "query_high"))
                O = Ring(bank[6:8], sem(st1, "o_full"), sem(st1, "o_free"))
                s_me, s_xn, s_nm = (sem(st1, n) for n in ("s1_me", "s1_xn", "s1_nm"))
                s_qb, s_cb, s_bo = (sem(st1, n) for n in ("s1_qb", "s1_cb", "s1_bo"))
                s_stt, s_one = sem(st1, "s1_st_t"), sem(st1, "s1_one")
                s_stv = [sem(st1, f"s1_st_v{j}") for j in range(CT)]
                R0, RN, AN, T0, TN, ON = 8, 16, 12, 4, 12, 14
                Q_ORDER = (1, 3, 0, 5, 2, 7, 4, 6)
                GRP = [(0, 3), (3, 6), (6, HP)]

                ctx_k = ctx_in.rearrange("b k s -> k b s")

                def pv_item(c, j):
                    return c * ON + 3 * j

                def chunk_order(c, more, do):
                    r, a, t, o = R0 + c * RN, c * AN, T0 + c * TN, c * ON
                    turned = (0, 4, 6, 14) if more else (0, 2, 4, 6)

                    def query(h):
                        if h % 2:
                            do("query", h, t, 8 + h // 2, c + 1, r + 3)
                        else:
                            do("query", h, r, 10 + h // 2, c + 1, r + 3)
                    for j in range(CT):
                        if 0 < j < CT - 1:
                            do("max", j + 1, a, 3 * j + 3, c)
                        do("scoresT", j, t, 2 * j, c, r - 1)
                        if j:
                            do("turn", j - 1, r, turned[j - 1], c)
                        if j == CT - 1:
                            break
                        for g in range(3):
                            do("pv", j, o, 3 * j + g, c)
                        if more and j == 0:
                            do("norm", 0, 0, 0, c + 1)
                        if more and j == 1:
                            do("normT", 0, r, 2, c + 1)
                        do("maxT", j + 1, a, 3 * j + 5, c)
                    for g, heads in enumerate(((1,), (3, 0), (5, 2, 7, 4, 6))):
                        do("pv", 3, o, 9 + g, c)
                        if more:
                            for h in heads:
                                query(h)
                            if g == 0:
                                do("ctxT", 0, r, 8, c + 1)
                    do("turn", 3, r, turned[3], c)
                    if more:
                        do("max", 0, a, 12, c + 1)
                    do("project", 0, o, 12, c, r + turned[3] + 1)
                    if more:
                        do("maxT", 0, a, 14, c + 1)
                        do("max", 1, a, 15, c + 1)
                    do("back", 0, o, 13, c)

                def start_order(do):
                    do("norm", 0, 0, 0, 0)
                    do("normT", 0, 0, 0, 0)
                    do("ctxT", 0, 0, 2, 0)
                    for h in Q_ORDER:
                        do("query", h, 0, h // 2 if h % 2 else 4 + h // 2, 0, 1)
                    do("max", 0, 0, 0, 0)
                    do("maxT", 0, 0, 2, 0)
                    do("max", 1, 0, 3, 0)

                def run(eng, do, clear=lambda: None):
                    start_order(do)
                    clear()
                    with eng.Fori(0, CHUNKS - 1) as c:
                        chunk_order(c, True, do)
                        clear()
                    chunk_order(CHUNKS - 1, False, do)

                with nc.Block() as block:
                    @block.sync
                    def _(sp):
                        def load_t(c):
                            for par in range(2):
                                sp.dma_start(st_t[par * S:(par + 1) * S, :, par * DC:(par + 1) * DC],
                                             ctx_k[:, bass.ds(c * CT * BPT, CT * BPT), :]).then_inc(s_stt, 16)

                        def load_v(c, j):
                            for par in range(2):
                                sp.dma_start(st_v[par * S:(par + 1) * S, j, :, par, 0:DC],
                                             ctx_k[:, bass.ds((c * CT + j) * BPT, BPT), :]).then_inc(s_stv[j], 16)
                        load_t(0)
                        for j in range(CT):
                            load_v(0, j)
                        sp.wait_ge(R.full, 4)
                        load_t(1)
                        for to, shared, routed in ((w1n, Ws1, W1), (w2n, Ws2, W2)):
                            for k, (h, n) in enumerate(HK):
                                sp.dma_start(to[0:n, 0, k, :], shared[h:h + n, :]).then_inc(s_w0, 16)
                                sp.dma_start(to[0:n, 1:E0, k, :],
                                             routed[:, h:h + n, :].rearrange("e h d -> h e d")).then_inc(s_w0, 16)
                        sp.dma_start(w3n[:, 0, :], Ws3).then_inc(s_w0, 16)
                        sp.dma_start(w3n[:, 1:E0, :], W3.rearrange("e d h -> d e h")).then_inc(s_w0, 16)
                        sp.dma_start(wgn[:, :], Wg).then_inc(s_w0, 16)
                        sp.dma_start(rb_bc[:, :], rbias.rearrange("(a e) -> a e", a=1).to_broadcast([P, ER])).then_inc(s_w0, 16)

                        def refill(c):
                            for j in range(CT):
                                sp.wait_ge(O.full, pv_item(c - 1, j) + 3)
                                load_v(c, j)
                        with sp.Fori(1, CHUNKS - 1) as c:
                            refill(c)
                            sp.wait_ge(R.full, R0 + (c - 1) * RN + 10)
                            load_t(c + 1)
                        refill(CHUNKS - 1)

                    @block.tensor
                    def _(pe):
                        def do(stage, j, base, k, c, needs=None):
                            n = base + k
                            if stage == "normT":
                                pe.wait_ge(s_xn, c + 1)
                                for i in range(2):
                                    R.wait_free(pe, n + i)
                                    for q in range(2):
                                        ins = pe.transpose(R.bank(k + i)[:, q * P:(q + 1) * P], xn[:, 2 * i + q, :], ident[:, :])
                                    ins.then_inc(R.full, 1)
                            elif stage == "ctxT":
                                pe.wait_ge(s_stt, 32 * (c + 1))
                                for i in range(2):
                                    R.wait_free(pe, n + i)
                                    for q in range(4):
                                        ins = pe.transpose(R.bank(k + i)[:, q * P:(q + 1) * P], st_t[:, 4 * i + q, :], ident[:, :])
                                    ins.then_inc(R.full, 1)
                            elif stage == "query":
                                if j == Q_ORDER[0]:
                                    R.wait_read(pe, needs)
                                K = T if j % 2 else R
                                K.wait_free(pe, n)
                                for i, (w, v) in enumerate(((GH, XH), (GL, XH), (GH, XL))):
                                    ins = pe.matmul(K.bank(k)[:, :], w[:, j, :], v[:, :], start=(i == 0), stop=(i == 2))
                                ins.then_inc(K.full, 1)
                            elif stage == "max":
                                if j == 0:
                                    pe.wait_ge(s_cb, c + 1)
                                for i in range(2):
                                    A.wait_free(pe, n + i)
                                    for h in range(4 * i, 4 * i + 4):
                                        if j == 0:
                                            pe.wait_ge(s_qb, HP * c + Q_ORDER.index(h) + 1)
                                        for b in range(BPT):
                                            ins = pe.matmul(A.bank(k + i)[b * S:(b + 1) * S, h % 4 * P:(h % 4 + 1) * P],
                                                            QB[:, h, j * P + b * S:j * P + (b + 1) * S],
                                                            CB[:, j * BPT + b, :], start=True, stop=True,
                                                            skip_group_check=True)
                                    ins.then_inc(A.full, 1)
                            elif stage == "maxT":
                                pe.wait_ge(s_nm, c * CT + j + 1)
                                A.wait_free(pe, n)
                                pe.transpose(A.bank(k)[0:2 * HEADS, 0:S].bitcast(bf16), nmb[:, :], identb[:, :]).then_inc(A.full, 1)
                            elif stage == "scoresT":
                                if j == 0:
                                    R.wait_read(pe, needs)
                                    T.wait_read(pe, base - 1)
                                for i in range(2):
                                    T.wait_free(pe, n + i)
                                    to = T.bank(k + i)[:, :].rearrange("p (h q) -> p h q", h=4)
                                    hs = slice(4 * i, 4 * i + 4)
                                    for b in range(BPT):
                                        q = slice(j * P + b * S, j * P + (b + 1) * S)
                                        for m, (w, v) in enumerate(((CH, QH), (CL, QH), (CH, QL))):
                                            pe.matmul(to[:, :, b * S:(b + 1) * S], w[:, j * BPT + b, :], v[:, hs, q],
                                                      start=(b == 0 and m == 0), stop=False, skip_group_check=True)
                                    if i == 0:
                                        A.wait_read(pe, c * AN + 3 * j + 2)
                                    for h in range(4):
                                        ins = pe.matmul(to[:, h, :], sel[:, 4 * i + h, :, :].rearrange("p a c -> p (a c)"),
                                                        mT[:, :], start=False, stop=(h == 3), skip_group_check=True)
                                    ins.then_inc(T.full, 1)
                            elif stage == "pv":
                                g = k - 3 * j
                                h0, h1 = GRP[g]
                                if g == 0:
                                    pe.wait_ge(s_stv[j], 32 * (c + 1))
                                T.wait_read(pe, T0 + c * TN + 2 * j + (h1 > 4))
                                O.wait_free(pe, n)
                                for h in range(h0, h1):
                                    for b in range(BPT):
                                        ins = pe.matmul(O.bank(k)[b * S:(b + 1) * S, (h - h0) * 130:(h - h0 + 1) * 130],
                                                        PT[:, h, b * S:(b + 1) * S],
                                                        st_v[:, j, b, :, :].rearrange("p a c -> p (a c)"),
                                                        start=True, stop=True, skip_group_check=True)
                                ins.then_inc(O.full, 1)
                            elif stage == "turn":
                                O.wait_read(pe, pv_item(c, j) + 2)
                                for i in range(2):
                                    R.wait_free(pe, n + i)
                                    for q in range(4):
                                        h = 4 * i + q
                                        ins = pe.transpose(R.bank(k + i)[:, q * P:(q + 1) * P],
                                                           On[:, 2 * h:2 * h + 2, :].rearrange("p a c -> p (a c)"), ident[:, :])
                                    ins.then_inc(R.full, 1)
                            elif stage == "project":
                                R.wait_read(pe, needs)
                                O.wait_free(pe, n)
                                steps = [(w, v, h) for h in range(HP) for w, v in ((VH, OH), (VH, OL), (VL, OH))]
                                for i, (w, v, h) in enumerate(steps):
                                    ins = pe.matmul(O.bank(k)[:, :], w[:, h, :], v[:, h, :],
                                                    start=(i == 0), stop=(i == len(steps) - 1))
                                ins.then_inc(O.full, 1)
                            elif stage == "back":
                                O.wait_read(pe, n - 1)
                                O.wait_free(pe, n)
                                for q in range(CT):
                                    ins = pe.transpose(O.bank(k)[:, q * P:(q + 1) * P], aT[:, q * P:(q + 1) * P], ident[:, :])
                                ins.then_inc(O.full, 1)
                        run(pe, do)

                    @block.scalar
                    def _(act):
                        act_dev(act)
                        act.sem_inc(T.free, 2)

                        def high(to, k, n, width=512, heads=1):
                            R.wait_full(act, n)
                            got = R.bank(k)[:, 0:width]
                            if heads > 1:
                                got = got.rearrange("p (h q) -> p h q", h=heads)
                            act.copy(to, got).then_inc(R.mid, 1)

                        def do(stage, j, base, k, c, needs=None):
                            n = base + k
                            if stage == "normT":
                                for i in range(2):
                                    high(XH[:, i * 2 * P:(i + 1) * 2 * P], k + i, n + i, 2 * P)
                            elif stage == "ctxT":
                                for i in range(2):
                                    high(CH[:, 4 * i:4 * i + 4, :].rearrange("p h c -> p (h c)"), k + i, n + i)
                            elif stage == "query":
                                K = T if j % 2 else R
                                K.wait_full(act, n)
                                act.copy(QH[:, j, :], K.bank(k)[:, :]).then_inc(K.mid, 1)
                            elif stage == "maxT":
                                A.wait_full(act, n)
                                act.copy(mT[:, :], A.bank(k)[0:2 * HEADS, 0:S].bitcast(bf16)).then_inc(A.free, 1)
                            elif stage == "project":
                                O.wait_full(act, n)
                                act.copy(aT[:, :], O.bank(k)[:, :]).then_inc(O.free, 1)
                            elif stage == "turn":
                                for i in range(2):
                                    high(OH[:, 4 * i:4 * i + 4, j * P:(j + 1) * P], k + i, n + i, heads=4)
                            elif stage == "scoresT":
                                for i in range(2):
                                    T.wait_full(act, n + i)
                                    act.activation(PT[:, 4 * i:4 * i + 4, :].rearrange("p h c -> p (h c)"),
                                                   T.bank(k + i)[:, :], ACT.Exp).then_inc(T.free, 1)
                        run(act, do)

                    @block.gpsimd
                    def _(pool):
                        pool.memset(one[:, :, :], 1.0).then_inc(s_one, 1)
                        pool.wait_ge(s_one, 1)

                        def do(stage, j, base, k, c, needs=None):
                            n = base + k
                            if stage == "norm":
                                pool.wait_ge(s_xn, c + 1)
                                for q in range(CT):
                                    ins = pool.tensor_tensor(X[:, c * CT + q, :], X[:, c * CT + q, :], bo_bc[:, :], ALU.add)
                                ins.then_inc(s_bo, 1)
                            elif stage == "ctxT":
                                R.wait_mid(pool, n + 1)
                                pool.tensor_tensor(CB[:, :, :], raw(CH[:, :, :]), one[:, :, :].to_broadcast([P, CT * BPT, P]), ALU.mult).then_inc(s_cb, 1)
                            elif stage == "query":
                                if j % 2:
                                    pool.wait_ge(T.mid, HP // 2 * c + j // 2 + 1)
                                else:
                                    R.wait_mid(pool, n)
                                pool.tensor_tensor(QB[:, j, :], raw(QH[:, j, :]), one[:, 0, :].to_broadcast([P, CW]), ALU.mult).then_inc(s_qb, 1)
                        run(pool, do)

                    @block.vector
                    def _(dve):
                        me = Self(dve, s_me)
                        dve.sem_inc(R.free, 2)
                        dve.sem_inc(A.free, 2)
                        dve.sem_inc(O.free, 2)
                        dve_dev(dve, me)

                        def low(hi, lo, k, n, width=512, heads=1):
                            R.wait_mid(dve, n)
                            got = R.bank(k)[:, 0:width]
                            if heads > 1:
                                got = got.rearrange("p (h q) -> p h q", h=heads)
                            dve.tensor_tensor(lo, got, raw(hi), ALU.subtract).then_inc(R.free, 1)

                        def do(stage, j, base, k, c, needs=None):
                            n = base + k
                            if stage == "norm":
                                normalise(dve, me, stt, xn, c, s_xn)
                            elif stage == "normT":
                                for i in range(2):
                                    part = slice(i * 2 * P, (i + 1) * 2 * P)
                                    low(XH[:, part], XL[:, part], k + i, n + i, 2 * P)
                            elif stage == "ctxT":
                                for i in range(2):
                                    low(CH[:, 4 * i:4 * i + 4, :].rearrange("p h c -> p (h c)"),
                                        CL[:, 4 * i:4 * i + 4, :].rearrange("p h c -> p (h c)"), k + i, n + i)
                            elif stage == "turn":
                                for i in range(2):
                                    hs, q = slice(4 * i, 4 * i + 4), slice(j * P, (j + 1) * P)
                                    low(OH[:, hs, q], OL[:, hs, q], k + i, n + i, heads=4)
                            elif stage == "query":
                                if j % 2:
                                    dve.wait_ge(T.mid, HP // 2 * c + j // 2 + 1)
                                    dve.tensor_tensor(QL[:, j, :], T.bank(k)[:, :], raw(QH[:, j, :]), ALU.subtract).then_inc(T.free, 1)
                                else:
                                    low(QH[:, j, :], QL[:, j, :], k, n)
                            elif stage == "max":
                                if not (isinstance(n, int) and n == 0):
                                    A.wait_read(dve, n - 1)
                                for i in range(2):
                                    A.wait_full(dve, n + i)
                                    dve.tensor_reduce(nm[:, 8 * i:8 * i + 8], A.bank(k + i)[:, :].rearrange("p (h s) -> p h s", s=S),
                                                      AX.X, ALU.max, negate=True).then_inc(A.free, 1)
                                A.wait_read(dve, n + 1)
                                me.done(dve.tensor_copy(nmb[:, 0:HEADS], nm[:, :]))
                                me.wait()
                                dve.tensor_tensor(nmb[:, HEADS:2 * HEADS], nm[:, :], nmb[:, 0:HEADS], ALU.subtract).then_inc(s_nm, 1)
                            elif stage == "pv":
                                h0, h1 = GRP[k - 3 * j]
                                O.wait_full(dve, n)
                                w = 2 * (h1 - h0)
                                got = O.bank(k)[:, 0:w * 65].rearrange("p (h c) -> p h c", c=65)
                                me.done(dve.reciprocal(rd[:, 2 * h0:2 * h1], got[:, :, 64]))
                                me.wait()
                                dve.tensor_tensor(On[:, 2 * h0:2 * h1, :], got[:, :, 0:HD],
                                                  rd[:, 2 * h0:2 * h1].rearrange("p (h a) -> p h a", a=1).to_broadcast([P, w, HD]),
                                                  ALU.mult).then_inc(O.free, 1)
                            elif stage == "back":
                                O.wait_full(dve, n)
                                dve.wait_ge(s_bo, c + 1)
                                residual(dve, me, bs, ag, O.bank(k), c, O.free)
                        run(dve, do, me.clear)
                        me.wait()

        def turn_weights(name, st, s_in, loads, items):
            K = Ring(bank[0:6], sem(st, name + "_full"), sem(st, name + "_free"), sem(st, name + "_high"))
            with nc.Block() as block:
                @block.sync
                def _(sp):
                    sp.wait_ge(s_in, 16 * loads)

                @block.tensor
                def _(pe):
                    pe.wait_ge(s_in, 16 * loads)
                    for n, (parts, rows, cols, hi, lo) in enumerate(items):
                        K.wait_free(pe, n)
                        for col, m, src in parts:
                            ins = pe.transpose(K.bank(n)[0:rows, col:col + m], src, ident[0:m, 0:m])
                        ins.then_inc(K.full, 1)

                @block.scalar
                def _(act):
                    for n, (parts, rows, cols, hi, lo) in enumerate(items):
                        K.wait_full(act, n)
                        act.copy(hi, K.bank(n)[0:rows, 0:cols]).then_inc(K.mid, 1)

                @block.vector
                def _(dve):
                    dve.sem_inc(K.free, len(K.banks))
                    for n, (parts, rows, cols, hi, lo) in enumerate(items):
                        K.wait_mid(dve, n)
                        dve.tensor_tensor(lo, K.bank(n)[0:rows, 0:cols], raw(hi), ALU.subtract).then_inc(K.free, 1)

        def make_selector(st, name, n):
            f, r = sb(st, name + "f", [n, n, P]), sb(st, name, [n, n, P], f32r)
            s = sem(st, name + "_made")
            with nc.Block() as block:
                @block.gpsimd
                def _(pool):
                    pool.memset(f[:, :, :], 0.0).then_inc(s, 1)
                    pool.wait_ge(s, 1)
                    pool.affine_select(out=f[:, :, :], in_=f[:, :, :], compare_op=ALU.not_equal, fill=1.0, base=0,
                                       pattern=[[-1, n], [0, P]], channel_multiplier=1).then_inc(s, 1)

                @block.vector
                def _(dve):
                    dve.wait_ge(s, 2)
                    dve.tensor_copy(r[:, :, :], f[:, :, :]).then_inc(s, 1)
                    dve.wait_ge(s, 3)
            return r

        def experts_phase(tag, st, nexp, nparts, up, down, rows, first_w, gates):
            glu = len(up(0)) == 2
            NU, NW = nexp * nparts, nexp - first_w
            XH, XL = (sb(st, n + tag, [P, CW], f32r) for n in ("XH", "XL"))
            xn, stt = sb(st, "xn" + tag, [P, CT, D]), sb(st, "stt" + tag, [P, CT, 2])
            bs, ag = sb(st, "bs" + tag, [P, CT, 6]), sb(st, "ag" + tag, [P, CT, 2])
            act1 = sb(st, "act1" + tag, [P, 2, CW]) if glu else None
            prod = sb(st, "prod" + tag, [P, 2, CW]) if glu else None
            HD = 3 if glu else 4
            assert NU % HD == 0
            HH, HL = (sb(st, n + tag, [P, HD, CW], f32r) for n in ("HH", "HL"))
            WB = sb(st, "WB" + tag, [P, 2, CW])
            tmp, acc = sb(st, "tmp" + tag, [P, 2, CW]), sb(st, "acc" + tag, [P, CW])
            dve_dev, act_dev = finish_deviation(st, tag)
            U1 = Ring(bank[0:2] if glu else bank[0:4], sem(st, "u1_full" + tag), sem(st, "u1_free" + tag), sem(st, "u1_high" + tag))
            U2 = Ring(bank[2:4], sem(st, "u2_full" + tag), sem(st, "u2_free" + tag))
            EO = Ring(bank[4:6], None, sem(st, "eo_free" + tag))
            R = Ring(bank[6:7], sem(st, "r_full" + tag), sem(st, "r_free" + tag), sem(st, "r_high" + tag))
            WBK = Ring(bank[7:8], sem(st, "wb_full" + tag), sem(st, "wb_free" + tag))
            s_me, s_pool, s_xn, s_hi, s_lo, s_down, s_acc = (
                sem(st, n + tag) for n in ("me", "pool", "x_normal", "h_high", "h_low", "down_done", "acc_added"))
            LAG = 3
            WEIGH = nparts + LAG
            NORM = max(NU - 8, NU // 2)

            def again(v, n, odd):
                return n if odd and v == 0 else n - 1

            def wait_count(eng, sem_, value):
                if not (isinstance(value, int) and value <= 0):
                    eng.wait_ge(sem_, value)

            RI = gates.items

            def r_item(c, i):
                return RI * c + i

            def x_item(c):
                return 0 if isinstance(c, int) and c == 0 else r_item(c, -1)

            def place_free(eng, v, n):
                wait_count(eng, s_down, n + 1 - HD)

            def order(c, first, last, do):
                for v in range(NU + LAG + 1):
                    if v < NU:
                        do("up", v, c)
                    if v == 1 and not first:
                        do("back", r_item(c, 0), c - 1)
                    for stage, step, i, ahead in gates.stages:
                        if v == step and not (ahead and last):
                            do(stage, r_item(c, i), c + 1 if ahead else c)
                    if v == NORM and not last:
                        do("norm", 0, c + 1)
                    if v == NU and not last:
                        do("normT", r_item(c, RI - 1), c + 1)
                    if 0 <= v - 1 < NU:
                        do("hidden", v - 1, c)
                    if 0 <= v - LAG < NU:
                        do("down", v - LAG, c)
                    e, k = divmod(v, nparts)
                    if k == 0 and gates.masks and e < nexp:
                        do("mask", e, c)
                    e, k = divmod(v - nparts, nparts)
                    if k == 0 and first_w <= e < nexp:
                        do("spread", e, c)
                    e, k = divmod(v - WEIGH, nparts)
                    if k == 0 and 0 <= e < nexp:
                        do("weigh", e, c)

            def run(eng, do, clear=lambda: None):
                for stage in gates.ahead:
                    do(stage, 0, 0)
                do("norm", 0, 0)
                do("normT", 0, 0)
                order(0, True, False, do)
                clear()
                with eng.Fori(1, CHUNKS - 1) as c:
                    order(c, False, False, do)
                    clear()
                order(CHUNKS - 1, False, True, do)
                do("back", r_item(CHUNKS - 1, RI - 1), CHUNKS - 1)

            def on_pool(v):
                return glu and v % 3 == 1

            def low_part(eng, v, n):
                place_free(eng, v, n)
                eng.wait_ge(s_hi, n + 1)
                wait_count(eng, s_lo, n)
                m = rows(v)
                eng.tensor_tensor(HL[0:m, v % HD, :], prod[0:m, v % 2, :], raw(HH[0:m, v % HD, :]),
                                  ALU.subtract).then_inc(s_lo, 1)

            with nc.Block() as block:
                @block.tensor
                def _(pe):
                    def do(stage, v, c):
                        if stage == "up":
                            n = c * NU + v
                            if v == 0:
                                R.wait_read(pe, x_item(c))
                            for i, (hi, lo) in enumerate(up(v)):
                                U = (U1, U2)[i]
                                wait_count(pe, U.free, again(v, n, NU % 2) + 2 if glu else n + 1)
                                for m, (w, x_) in enumerate(((hi, XH), (lo, XH), (hi, XL))):
                                    ins = pe.matmul(U.bank(v)[0:rows(v), :], w, x_[:, :], start=(m == 0), stop=(m == 2))
                                ins.then_inc(U.full, 1)
                        elif stage == "down":
                            n = c * NU + v
                            e, k = divmod(v, nparts)
                            if glu:
                                pe.wait_ge(s_lo, n + 1)
                            else:
                                U1.wait_read(pe, n)
                            if k == 0:
                                wait_count(pe, EO.free, again(e, c * nexp + e, nexp % 2) + 2)
                            hi, lo = down(v)
                            for m, (w, h) in enumerate(((hi, HH), (lo, HH), (hi, HL))):
                                ins = pe.matmul(EO.bank(e)[:, :], w, h[0:rows(v), v % HD, :],
                                                start=(k == 0 and m == 0), stop=(k == nparts - 1 and m == 2))
                            ins.then_inc(s_down, 1)
                        elif stage == "spread":
                            n = c * NW + v - first_w
                            gates.ready(pe, R, v, n, r_item(c, gates.turned))
                            WBK.wait_free(pe, n)
                            pairs = gates.products(v - first_w)
                            for m, (w, x_) in enumerate(pairs):
                                ins = pe.matmul(WBK.bank(0)[:, :], w, x_, start=(m == 0), stop=(m == len(pairs) - 1))
                            ins.then_inc(WBK.full, 1)
                        elif stage == "back":
                            pe.wait_ge(s_acc, (c + 1) * (nexp - 1))
                            R.wait_free(pe, v)
                            for j in range(CT):
                                ins = pe.transpose(R.bank(0)[:, j * P:(j + 1) * P], acc[:, j * P:(j + 1) * P], ident[:, :])
                            ins.then_inc(R.full, 1)
                        elif stage == "normT":
                            pe.wait_ge(s_xn, c + 1)
                            R.wait_free(pe, v)
                            for j in range(CT):
                                ins = pe.transpose(R.bank(0)[:, j * P:(j + 1) * P], xn[:, j, :], ident[:, :])
                            ins.then_inc(R.full, 1)
                        else:
                            if stage == "weights":
                                R.wait_read(pe, x_item(c))
                            gates.on_tensor(pe, stage, R, v, c, XH, XL)
                    run(pe, do)

                @block.scalar
                def _(act):
                    act_dev(act)
                    if glu:
                        act.sem_inc(U1.free, 2)
                    act.sem_inc(WBK.free, 1)

                    def do(stage, v, c):
                        n = c * NU + v
                        if stage == "up":
                            m = rows(v)
                            U1.wait_full(act, n)
                            if glu:
                                wait_count(act, U2.free, again(v, n, NU % 2) + 2)
                                act.activation(act1[0:m, v % 2, :], U1.bank(v)[0:m, :], ACT.Silu).then_inc(U1.free, 1)
                            else:
                                place_free(act, v, n)
                                act.activation(HH[0:m, v % HD, :], U1.bank(v)[0:m, :], ACT.Relu).then_inc(U1.mid, 1)
                        elif stage == "hidden" and glu:
                            m = rows(v)
                            U2.wait_read(act, n)
                            place_free(act, v, n)
                            act.copy(HH[0:m, v % HD, :], prod[0:m, v % 2, :]).then_inc(s_hi, 1)
                        elif stage == "spread":
                            n = c * NW + v - first_w
                            WBK.wait_full(act, n)
                            EO_done = c * nexp + v - 1
                            wait_count(act, EO.free, EO_done + 2)
                            act.copy(WB[:, (v - first_w) % 2, :], WBK.bank(0)[:, :]).then_inc(WBK.free, 1)
                        elif stage == "normT":
                            R.wait_full(act, v)
                            act.copy(XH[:, :], R.bank(0)[:, :]).then_inc(R.mid, 1)
                        else:
                            gates.on_scalar(act, stage, c)
                    run(act, do)

                @block.gpsimd
                def _(pool):
                    def do(stage, v, c):
                        e = v
                        if stage == "weigh" and e > 0:
                            EO.wait_read(pool, c * nexp + e)
                            wait_count(pool, s_acc, c * (nexp - 1) + e - 1)
                            pool.tensor_tensor(acc[:, :], acc[:, :], tmp[:, e % 2, :], ALU.add).then_inc(s_acc, 1)
                        elif stage == "hidden" and on_pool(v):
                            low_part(pool, v, c * NU + v)
                    run(pool, do)

                @block.vector
                def _(dve):
                    me = Self(dve, s_me)
                    dve.sem_inc(R.free, 1)
                    dve.sem_inc(EO.free, 2)
                    dve.sem_inc(U2.free if glu else U1.free, 2 if glu else 4)
                    dve_dev(dve, me)
                    r_low = [0]

                    def do(stage, v, c):
                        n = c * NU + v
                        if stage == "up":
                            m = rows(v)
                            if glu:
                                U1.wait_read(dve, n)
                                U2.wait_full(dve, n)
                                wait_count(dve, s_hi, again(v, n, NU % 2))
                                wait_count(dve, s_lo, again(v, n, NU % 2))
                                dve.tensor_tensor(prod[0:m, v % 2, :], U2.bank(v)[0:m, :], act1[0:m, v % 2, :],
                                                  ALU.mult).then_inc(U2.free, 1)
                            else:
                                place_free(dve, v, n)
                                U1.wait_mid(dve, n)
                                dve.scalar_tensor_tensor(HL[0:m, v % HD, :], U1.bank(v)[0:m, :], 0.0,
                                                         raw(HH[0:m, v % HD, :]), ALU.max,
                                                         ALU.subtract).then_inc(U1.free, 1)
                        elif stage == "hidden" and glu and not on_pool(v):
                            low_part(dve, v, n)
                        elif stage == "weigh":
                            if v > 0:
                                wait_count(dve, s_acc, c * (nexp - 1) + max(v - 2, 0))
                            if v >= first_w:
                                WBK.wait_read(dve, c * NW + v - first_w)
                            dve.wait_ge(s_down, c * NU + (v + 1) * nparts)
                            to = tmp[:, v % 2, :] if v else acc[:, :]
                            if v < first_w:
                                ins = dve.tensor_copy(to, EO.bank(v)[:, :])
                            else:
                                ins = dve.tensor_tensor(to, EO.bank(v)[:, :], WB[:, (v - first_w) % 2, :], ALU.mult)
                            ins.then_inc(EO.free, 1)
                        elif stage == "norm":
                            normalise(dve, me, stt, xn, c, s_xn)
                        elif stage == "normT":
                            R.wait_mid(dve, x_number(c))
                            dve.tensor_tensor(XL[:, :], R.bank(0)[:, :], raw(XH[:, :]), ALU.subtract).then_inc(R.free, 1)
                        elif stage == "back":
                            R.wait_full(dve, v)
                            residual(dve, me, bs, ag, R.bank(0), c, R.free)
                        elif stage == "mask":
                            gates.mask(dve, v, c, WBK)
                        else:
                            gates.on_vector(dve, me, stage, R, v, c)
                    run(dve, do, me.clear)
                    me.wait()

        def x_number(c):
            return c

        class Router:
            items, turned, masks, ahead = 4, 2, False, ()
            stages = (("weights", 1, 1, False), ("exp", 2, 0, False), ("weightsT", 5, 2, False))

            def __init__(self, st, wgT):
                self.wgT = wgT
                self.sel = make_selector(st, "sel_e", ER)
                self.wtok = sb(st, "wtok", [P, CT, ER])
                self.WTH, self.WTL = (sb(st, n, [ER, CW], f32r) for n in ("WTH", "WTL"))
                self.s_wtok = sem(st, "w_ready")
                self.lg, self.ex, self.w0 = (sb(st, n, [P, CT, ER]) for n in ("logits", "exps", "w_raw"))
                self.mx, self.total = sb(st, "mx", [P, CT]), sb(st, "w_total", [P, CT])
                self.gt, self.eq = (sb(st, n, [P, CT, ER, ER]) for n in ("gt", "eq"))
                self.lower = sb(st, "lower", [P, ER, ER])
                self.s_sub, self.s_exp, self.s_tri = (sem(st, n) for n in ("s_sub", "s_exp", "s_tri"))
                with nc.Block() as block:
                    @block.gpsimd
                    def _(pool):
                        pool.memset(self.lower[:, :, :], 1.0).then_inc(self.s_tri, 1)
                        pool.wait_ge(self.s_tri, 1)
                        pool.affine_select(out=self.lower[:, :, :], in_=self.lower[:, :, :], compare_op=ALU.is_gt,
                                           fill=0.0, base=0, pattern=[[1, ER], [-1, ER]],
                                           channel_multiplier=0).then_inc(self.s_tri, 1)

            def ready(self, pe, R, e, n, turned):
                if e == E0 - ER:
                    R.wait_read(pe, turned)

            def products(self, e):
                return [(self.sel[:, e, :], self.WTH[:, :]), (self.sel[:, e, :], self.WTL[:, :])]

            def on_tensor(self, pe, stage, R, n, c, XH, XL):
                if stage == "weights":
                    R.wait_free(pe, n)
                    for j in range(CT):
                        for m, x_ in enumerate((XH, XL)):
                            ins = pe.matmul(R.bank(0)[:, j * 2 * ER:(j + 1) * 2 * ER], x_[:, j * P:(j + 1) * P], self.wgT[:, :],
                                            start=(m == 0), stop=(m == 1))
                    ins.then_inc(R.full, 1)
                elif stage == "weightsT":
                    pe.wait_ge(self.s_wtok, c + 1)
                    R.wait_free(pe, n)
                    for j in range(CT):
                        ins = pe.transpose(R.bank(0)[0:ER, j * P:(j + 1) * P], self.wtok[:, j, :], ident[:, :])
                    ins.then_inc(R.full, 1)

            def on_scalar(self, act, stage, c):
                if stage == "exp":
                    act.wait_ge(self.s_sub, c + 1)
                    act.activation(self.ex[:, :, :], self.ex[:, :, :], ACT.Exp).then_inc(self.s_exp, 1)

            def on_vector(self, dve, me, stage, R, n, c):
                if stage == "weights":
                    self.rank(dve, me, R, n)
                elif stage == "exp":
                    self.weigh(dve, me, c)
                elif stage == "weightsT":
                    R.wait_full(dve, n)
                    me.done(dve.tensor_copy(self.WTH[:, :], R.bank(0)[0:ER, :]))
                    me.wait()
                    dve.tensor_tensor(self.WTL[:, :], R.bank(0)[0:ER, :], raw(self.WTH[:, :]), ALU.subtract).then_inc(R.free, 1)

            def rank(self, dve, me, R, n):
                lg, ex = self.lg, self.ex
                wide = [P, CT, ER, ER]
                got = R.bank(0)[:, 0:CT * 2 * ER].rearrange("p (t h e) -> p t h e", t=CT, h=2)
                R.wait_full(dve, n)
                me.done(dve.tensor_tensor(lg[:, :, :], got[:, :, 1, :],
                                          rb_bc[:, :].rearrange("p (a e) -> p a e", a=1).to_broadcast([P, CT, ER]), ALU.add))
                me.wait()
                ins = dve.tensor_tensor(lg[:, :, :], got[:, :, 0, :], lg[:, :, :], ALU.add)
                ins.then_inc(R.free, 1)
                R.wait_read(dve, n)
                me.done(dve.tensor_reduce(self.mx[:, :], lg[:, :, :], AX.X, ALU.max))
                me.wait()
                dve.tensor_tensor(ex[:, :, :], lg[:, :, :], self.mx[:, :].rearrange("p (t a) -> p t a", a=1).to_broadcast([P, CT, ER]),
                                  ALU.subtract).then_inc(self.s_sub, 1)
                other = lg[:, :, :].rearrange("p t (a f) -> p t a f", a=1).to_broadcast(wide)
                mine = lg[:, :, :].rearrange("p t (e a) -> p t e a", a=1).to_broadcast(wide)
                me.done(dve.tensor_tensor(self.gt[:, :, :, :], other, mine, ALU.is_gt))
                me.done(dve.tensor_tensor(self.eq[:, :, :, :], other, mine, ALU.is_equal))
                me.wait()
                me.done(dve.tensor_tensor(self.eq[:, :, :, :], self.eq[:, :, :, :],
                                          self.lower[:, :, :].rearrange("p (a e) f -> p a e f", a=1).to_broadcast(wide), ALU.mult))
                me.wait()
                me.done(dve.tensor_tensor(self.gt[:, :, :, :], self.gt[:, :, :, :], self.eq[:, :, :, :], ALU.add))
                me.wait()
                me.done(dve.tensor_reduce(self.w0[:, :, :], self.gt[:, :, :, :], AX.X, ALU.add))
                me.wait()

            def weigh(self, dve, me, c):
                ex = self.ex
                dve.wait_ge(self.s_exp, c + 1)
                me.done(dve.scalar_tensor_tensor(self.w0[:, :, :], self.w0[:, :, :], float(TOPK), ex[:, :, :], ALU.is_lt, ALU.mult))
                me.wait()
                me.done(dve.tensor_reduce(self.total[:, :], self.w0[:, :, :], AX.X, ALU.add))
                me.wait()
                me.done(dve.reciprocal(self.total[:, :], self.total[:, :]))
                me.wait()
                dve.tensor_tensor(self.wtok[:, :, :], self.w0[:, :, :],
                                  self.total[:, :].rearrange("p (t a) -> p t a", a=1).to_broadcast([P, CT, ER]),
                                  ALU.mult).then_inc(self.s_wtok, 1)

        class Gates:
            items, turned, masks, ahead = 2, 0, True, ("names",)
            stages = (("names", 10, 0, True),)

            def __init__(self, st):
                self.names = sb(st, "names", [P, TILES * BPT, S], int32)
                self.cn = sb(st, "cn", [P, TILES * BPT, S])
                self.chl = sb(st, "chl", [P, CHUNKS, CW], f32r)
                self.masked = sb(st, "masked", [P, 2, CW], f32r)
                ones = sb(st, "ones3f", [P, P])
                self.ones = sb(st, "ones3", [P, P], f32r)
                self.s_first, self.s_rest, self.s_one, self.s_copied, self.s_split, self.s_mask = (
                    sem(st, n) for n in ("first_context", "rest_context", "ones3_made", "context_high", "context_split", "masked_ready"))
                ck, ik = ctx_in.rearrange("b k s -> k b s"), itok.rearrange("b k s -> k b s")
                nb = CT * BPT
                with nc.Block() as block:
                    @block.sync
                    def _(sp):
                        for part, done in ((slice(0, nb), self.s_first), (slice(nb, TILES * BPT), self.s_rest)):
                            for h in (0, S):
                                sp.dma_start(self.cn[h:h + S, part, :], ck[:, part, :]).then_inc(done, 16)
                                sp.dma_start(self.names[h:h + S, part, :], ik[:, part, :]).then_inc(done, 16)

                    @block.gpsimd
                    def _(pool):
                        pool.memset(ones[:, :], 1.0).then_inc(self.s_one, 1)

                    @block.vector
                    def _(dve):
                        dve.wait_ge(self.s_one, 1)
                        dve.tensor_copy(self.ones[:, :], ones[:, :]).then_inc(self.s_one, 1)
                        dve.wait_ge(self.s_one, 2)

            def of(self, c, h=0):
                nb = CT * BPT
                return self.cn[h:P, bass.ds(c * nb, nb), :].rearrange("k b s -> k (b s)")

            def here(self, eng, c):
                eng.wait_ge(*((self.s_first, 64) if isinstance(c, int) and c == 0 else (self.s_rest, 64)))

            def ready(self, pe, R, e, n, turned):
                pe.wait_ge(self.s_mask, n + 1)

            def products(self, e):
                return [(self.ones[:, :], self.masked[:, e % 2, :])]

            def on_tensor(self, pe, stage, R, n, c, XH, XL):
                pass

            def on_scalar(self, act, stage, c):
                if stage == "names":
                    self.here(act, c)
                    act.copy(self.chl[:, c, :], self.of(c)).then_inc(self.s_copied, 1)

            def on_vector(self, dve, me, stage, R, n, c):
                if stage == "names":
                    self.here(dve, c)
                    dve.wait_ge(self.s_copied, c + 1)
                    dve.tensor_tensor(self.chl[S:P, c, :], self.of(c, S), raw(self.chl[S:P, c, :]),
                                      ALU.subtract).then_inc(self.s_split, 1)

            def mask(self, dve, e, c, WBK):
                n = c * E1 + e
                if e == 0:
                    dve.wait_ge(self.s_split, c + 1)
                if not (isinstance(n, int) and n < 2):
                    WBK.wait_full(dve, n - 2)
                nb = CT * BPT
                names = self.names[:, bass.ds(c * nb, nb), :].rearrange("k b s -> k (b s)")
                dve.scalar_tensor_tensor(self.masked[:, e % 2, :], names, float(e), raw(self.chl[:, c, :]),
                                         ALU.is_equal, ALU.mult).then_inc(self.s_mask, 1)

        pin_n = sb(top, "pin_n", [P, E1 * D1 // P, D])
        pout_n = sb(top, "pout_n", [D, E1, D1])
        q_n = [sb(top, "wgate_n", [P, I1 // P, D]), sb(top, "wup_n", [P, I1 // P, D]), sb(top, "wdown_n", [D, I1])]
        s_w1 = sem(top, "s_w1")

        if phases >= 2:
            with ExitStack() as st2:
                W1H, W1L, W2H, W2L = (sb(st2, n, [D, E0, H0], f32r) for n in ("W1H", "W1L", "W2H", "W2L"))
                W3H, W3L = (sb(st2, n, [P, len(HK), E0, D], f32r) for n in ("W3H", "W3L"))
                wgT = sb(st2, "wgT", [D, 2 * ER], f32r)
                items = [([(0, ER, wgn[:, :])], P, ER, wgT[:, 0:ER], wgT[:, ER:2 * ER])]
                for src, hi, lo in ((w1n, W1H, W1L), (w2n, W2H, W2L)):
                    for e in range(E0):
                        items.append(([(h, n, src[0:n, e, k, :]) for k, (h, n) in enumerate(HK)], D, H0,
                                      hi[:, e, :], lo[:, e, :]))
                for k, (h, n) in enumerate(HK):
                    for e in range(0, E0, 4):
                        m = min(4, E0 - e)
                        flat = lambda w: w[0:n, k, e:e + m, :].rearrange("p e d -> p (e d)")
                        items.append(([(i * D, D, w3n[:, e + i, h:h + n]) for i in range(m)], n, m * D, flat(W3H), flat(W3L)))
                with nc.Block() as block:
                    @block.sync
                    def _(sp):
                        sp.dma_start(pin_n[:, :, :], p_in.rearrange("e (h p) i -> p (e h) i", p=P)).then_inc(s_w1, 16)
                        sp.dma_start(pout_n[:, :, :], p_out.rearrange("e i d -> i e d")).then_inc(s_w1, 16)
                        sp.dma_start(q_n[0][:, :, :], w_gate.rearrange("(k p) i -> p k i", p=P)).then_inc(s_w1, 16)
                        sp.dma_start(q_n[1][:, :, :], w_up.rearrange("(k p) i -> p k i", p=P)).then_inc(s_w1, 16)
                        sp.dma_start(q_n[2][:, :], w_down).then_inc(s_w1, 16)
                with ExitStack() as st:
                    turn_weights("k0", st, s_w0, W0_LOADS, items)
                gates = Router(st2, wgT)

                def part(u):
                    e, k = divmod(u, len(HK))
                    return e, k, slice(HK[k][0], HK[k][0] + HK[k][1])

                def up2(u):
                    e, k, h = part(u)
                    return [(W1H[:, e, h], W1L[:, e, h]), (W2H[:, e, h], W2L[:, e, h])]

                def down2(u):
                    e, k, h = part(u)
                    return W3H[0:HK[k][1], k, e, :], W3L[0:HK[k][1], k, e, :]
                experts_phase("2", st2, E0, len(HK), up2, down2, lambda u: HK[u % len(HK)][1], E0 - ER, gates)

        if phases >= 3:
            with ExitStack() as st3:
                PIH, PIL = (sb(st3, n, [D, E1 * D1], f32r) for n in ("PIH", "PIL"))
                POH, POL = (sb(st3, n, [P, E1 * D1 // P, D], f32r) for n in ("POH", "POL"))
                items = []
                for u in range(0, E1 * D1 // P, 4):
                    items.append(([(i * P, P, pin_n[:, u + i, :]) for i in range(4)], D, 4 * P,
                                  PIH[:, u * P:(u + 4) * P], PIL[:, u * P:(u + 4) * P]))
                    flat = lambda w: w[:, u:u + 4, :].rearrange("p u d -> p (u d)")
                    items.append(([(i * D, D, pout_n[:, (u + i) // 2, (u + i) % 2 * P:((u + i) % 2 + 1) * P]) for i in range(4)],
                                  P, 4 * D, flat(POH), flat(POL)))
                gates = Gates(st3)
                with ExitStack() as st:
                    turn_weights("k1", st, s_w1, 5, items)
                experts_phase("3", st3, E1, D1 // P, lambda u: [(PIH[:, u * P:(u + 1) * P], PIL[:, u * P:(u + 1) * P])],
                              lambda u: (POH[:, u, :], POL[:, u, :]), lambda u: P, 0, gates)

        if phases >= 4:
            with ExitStack() as st4:
                NQ = 3
                WQ = [sb(st4, n, [P, 4, P if n == "WQd" else P], bf16) for n in ("WQg", "WQu", "WQd")]
                ones = sb(st4, "ones4", [P, P])
                absum, mean = sb(st4, "absum", [P, NQ]), sb(st4, "meanw", [P, NQ])
                scale = sb(st4, "scalew", [P, NQ])
                wt, wi = sb(st4, "wt", [P, NQ, 4 * P]), sb(st4, "wi", [P, NQ, 4 * P], bf16)
                s_one, s_abs, s_sum, s_wi, s_wtb, s_wq, s_me = (
                    sem(st4, n) for n in ("s4_one", "s4_abs", "s4_sum", "s4_wi", "s4_wtb", "s4_wq", "s4_me0"))
                nat = [w[:, :, :].rearrange("p k i -> p (k i)") if n < 2 else w[:, :] for n, w in enumerate(q_n)]
                count = float(I1 * D)

                with nc.Block() as block:
                    @block.gpsimd
                    def _(pool):
                        pool.memset(ones[:, :], 1.0).then_inc(s_one, 1)

                    @block.tensor
                    def _(pe):
                        pe.wait_ge(s_one, 1)
                        pe.wait_ge(s_abs, NQ)
                        pe.matmul(bank[0][:, 0:NQ], ones[:, :], absum[:, :], start=True, stop=True).then_inc(s_sum, 1)
                        for n in range(NQ):
                            pe.wait_ge(s_wi, n + 1)
                            for k in range(4):
                                ins = pe.transpose(bank[1 + n][:, k * 64:(k + 1) * 64].bitcast(bf16),
                                                   wi[:, n, k * P:(k + 1) * P], identb[:, :])
                            ins.then_inc(s_wtb, 1)

                    @block.scalar
                    def _(act):
                        for n in range(NQ):
                            act.wait_ge(s_wtb, n + 1)
                            act.copy(WQ[n][:, :, :].rearrange("p k i -> p (k i)"),
                                     bank[1 + n][:, 0:256].bitcast(bf16)).then_inc(s_wq, 1)
                        act.wait_ge(s_wq, NQ)

                    @block.vector
                    def _(dve):
                        me = Self(dve, s_me)
                        dve.wait_ge(s_w1, 80)
                        for n in range(NQ):
                            dve.tensor_reduce(absum[:, n:n + 1], nat[n], AX.X, ALU.add,
                                              apply_absolute_value=True).then_inc(s_abs, 1)
                        dve.wait_ge(s_sum, 1)
                        me.done(dve.tensor_scalar(mean[:, :], bank[0][:, 0:NQ], 1.0 / count, 1e-5, ALU.mult, ALU.max))
                        me.wait()
                        me.done(dve.reciprocal(scale[:, :], mean[:, :]))
                        me.wait()
                        for n in range(NQ):
                            me.done(dve.tensor_scalar(wt[:, n, :], nat[n], scale[:, n:n + 1], ROUND, ALU.mult, ALU.add))
                        me.wait()
                        me.done(dve.tensor_scalar(wt[:, :, :], wt[:, :, :], -ROUND, 1.0, ALU.add, ALU.min))
                        me.wait()
                        for n in range(NQ):
                            dve.tensor_scalar(wi[:, n, :], wt[:, n, :], -1.0, None, ALU.max).then_inc(s_wi, 1)
                        me.done(dve.tensor_scalar(mean[:, :], mean[:, :], 1.0 / 127.0, None, ALU.mult))
                        me.wait()

                xn, stt = sb(st4, "xn4", [P, CT, D]), sb(st4, "stt4", [P, CT, 2])
                xr, xq = sb(st4, "xr4", [P, CT, D]), sb(st4, "xq4", [P, CT, D], bf16)
                xqT = sb(st4, "xqT", [D, CT, P], bf16)
                a1, r1, dg, du = (sb(st4, n, [P, CT]) for n in ("a1", "r1", "dg", "du"))
                sg, pr = sb(st4, "sg", [P, 2, I1]), sb(st4, "pr", [P, CT, I1])
                qr, qb = sb(st4, "qr", [P, CT, I1]), sb(st4, "qb", [P, CT, I1], bf16)
                qT = sb(st4, "qT", [P, CT, I1], bf16)
                a2, r2, dd = (sb(st4, n, [P, CT]) for n in ("a2", "r2", "dd"))
                dve_dev, act_dev = finish_deviation(st4, "4")
                G = Ring(bank[0:2], sem(st4, "gate_full"), sem(st4, "gate_free"))
                U = Ring(bank[2:4], sem(st4, "up_full"), sem(st4, "up_free"))
                T = Ring(bank[4:6], sem(st4, "turn_full"), sem(st4, "turn_free"))
                Y = Ring(bank[6:7], None, sem(st4, "y_free"))
                XT = Ring(bank[7:8], sem(st4, "xt_full"), sem(st4, "xt_free"))
                s_me, s_xq, s_dg, s_qr, s_qb, s_down, s_out = (
                    sem(st4, n) for n in ("s4_me", "s4_xq", "s4_dg", "s4_qr", "s4_qb", "s4_down", "s4_out"))

                def body4(c, ups, downs, more, do):
                    for stage, j in (("up", 0), ("up", 1), ("turn", 0), ("turn", 1), ("up", 2), ("down", 0), ("up", 3),
                                     ("turn", 2), ("down", 1), ("turn", 3), ("down", 2), ("down", 3)):
                        if stage == "up" and ups:
                            do(stage, j, c)
                        elif stage != "up" and downs:
                            do(stage, j, c - 1)
                    if more:
                        do("quant", 0, c + 1)
                    if downs:
                        do("add", 0, c - 1)
                    if more:
                        do("xT", 0, c + 1)
                    if ups:
                        do("requant", 0, c)

                def run4(eng, do, clear=lambda: None):
                    do("quant", 0, 0)
                    do("xT", 0, 0)
                    body4(0, True, False, True, do)
                    clear()
                    with eng.Fori(1, CHUNKS - 1) as c:
                        body4(c, True, True, True, do)
                        clear()
                    body4(CHUNKS - 1, True, True, False, do)
                    body4(CHUNKS, False, True, False, do)

                def positive(eng, sem_, value):
                    if not (isinstance(value, int) and value <= 0):
                        eng.wait_ge(sem_, value)

                with nc.Block() as block:
                    @block.sync
                    def _(sp):
                        def store(c):
                            Y.wait_read(sp, c)
                            sp.dma_start(out_t[:, bass.ds(c * CT, CT), :], X[:, bass.ds(c * CT, CT), :]).then_inc(s_out, 16)
                        store(0)
                        with sp.Fori(1, CHUNKS) as c:
                            store(c)
                        sp.wait_ge(s_out, 16 * CHUNKS)

                    @block.tensor
                    def _(pe):
                        def do(stage, j, c):
                            n = c * CT + j
                            if stage == "xT":
                                pe.wait_ge(s_xq, c + 1)
                                XT.wait_free(pe, c)
                                for q in range(CT):
                                    ins = pe.transpose(XT.bank(0)[:, q * 64:(q + 1) * 64].bitcast(bf16), xq[:, q, :], identb[:, :])
                                ins.then_inc(XT.full, 1)
                            elif stage == "up":
                                if j == 0:
                                    XT.wait_read(pe, c)
                                for R_, w in ((G, WQ[0]), (U, WQ[1])):
                                    R_.wait_free(pe, n)
                                    pe.matmul(R_.bank(j)[:, :], xqT[:, j, :], w[:, :, :].rearrange("p k i -> p (k i)"),
                                              start=True, stop=True).then_inc(R_.full, 1)
                            elif stage == "turn":
                                pe.wait_ge(s_qb, n + 1)
                                T.wait_free(pe, n)
                                for k in range(4):
                                    ins = pe.transpose(T.bank(j)[:, k * 64:(k + 1) * 64].bitcast(bf16),
                                                       qb[:, j, k * P:(k + 1) * P], identb[:, :])
                                ins.then_inc(T.full, 1)
                            elif stage == "down":
                                T.wait_read(pe, n)
                                if j == 0:
                                    Y.wait_free(pe, c)
                                for k in range(4):
                                    ins = pe.matmul(Y.bank(0)[:, j * D:(j + 1) * D], qT[:, j, k * P:(k + 1) * P], WQ[2][:, k, :],
                                                    start=(k == 0), stop=(k == 3))
                                ins.then_inc(s_down, 1)
                        run4(pe, do)

                    @block.scalar
                    def _(act):
                        act_dev(act)
                        act.sem_inc(G.free, 2)
                        act.sem_inc(T.free, 2)
                        act.sem_inc(XT.free, 1)

                        def do(stage, j, c):
                            n = c * CT + j
                            if stage == "xT":
                                positive(act, U.full, c * CT)
                                XT.wait_full(act, c)
                                act.copy(xqT[:, :, :].rearrange("p t d -> p (t d)"), XT.bank(0)[:, 0:256].bitcast(bf16)).then_inc(XT.free, 1)
                            elif stage == "up":
                                if j == 0:
                                    act.wait_ge(s_dg, c + 1)
                                U.wait_free(act, n)
                                G.wait_full(act, n)
                                act.activation(sg[:, j % 2, :], G.bank(j)[:, :], ACT.Silu, scale=dg[:, j:j + 1]).then_inc(G.free, 1)
                            elif stage == "turn":
                                act.wait_ge(s_qr, n + 1)
                                act.activation(qb[:, j, :], qr[:, j, :], ACT.Copy, bias=-ROUND).then_inc(s_qb, 1)
                            elif stage == "down":
                                act.wait_ge(s_down, n + 1)
                                T.wait_full(act, n)
                                act.copy(qT[:, j, :], T.bank(j)[:, 0:256].bitcast(bf16)).then_inc(T.free, 1)
                        run4(act, do)

                    @block.vector
                    def _(dve):
                        me = Self(dve, s_me)
                        dve.sem_inc(U.free, 2)
                        dve.sem_inc(Y.free, 1)
                        dve.sem_inc(s_down, CT)
                        dve_dev(dve, me)

                        def do(stage, j, c):
                            n = c * CT + j
                            if stage == "quant":
                                me.done(dve.tensor_copy(stt[:, :, :], MV[:, bass.ds(c * CT, CT), :]))
                                me.wait()
                                for q in range(CT):
                                    me.done(dve.tensor_scalar(xn[:, q, :], X[:, c * CT + q, :], stt[:, q, 0:1], stt[:, q, 1:2],
                                                              ALU.subtract, ALU.mult))
                                me.wait()
                                me.done(dve.tensor_reduce(a1[:, :], xn[:, :, :], AX.X, ALU.max, apply_absolute_value=True))
                                me.wait()
                                me.done(dve.tensor_scalar(a1[:, :], a1[:, :], 1e-5, None, ALU.max))
                                me.wait()
                                me.done(dve.reciprocal(r1[:, :], a1[:, :]))
                                dve.tensor_scalar(dg[:, :], a1[:, :], mean[:, 0:1], None, ALU.mult).then_inc(s_dg, 1)
                                me.done(dve.tensor_scalar(du[:, :], a1[:, :], mean[:, 1:2], None, ALU.mult))
                                me.wait()
                                me.done(dve.tensor_scalar(r1[:, :], r1[:, :], 127.0, None, ALU.mult))
                                me.wait()
                                for q in range(CT):
                                    me.done(dve.tensor_scalar(xr[:, q, :], xn[:, q, :], r1[:, q:q + 1], ROUND, ALU.mult, ALU.add))
                                me.wait()
                                positive(dve, XT.full, c)
                                dve.tensor_scalar(xq[:, :, :], xr[:, :, :], -ROUND, None, ALU.add).then_inc(s_xq, 1)
                            elif stage == "up":
                                G.wait_read(dve, n)
                                U.wait_full(dve, n)
                                positive(dve, s_qr, n - CT + 1)
                                dve.scalar_tensor_tensor(pr[:, j, :], U.bank(j)[:, :], du[:, j:j + 1], sg[:, j % 2, :],
                                                         ALU.mult, ALU.mult).then_inc(U.free, 1)
                            elif stage == "requant":
                                U.wait_read(dve, n + CT - 1)
                                me.done(dve.tensor_reduce(a2[:, :], pr[:, :, :], AX.X, ALU.max, apply_absolute_value=True))
                                me.wait()
                                me.done(dve.tensor_scalar(a2[:, :], a2[:, :], 1e-5, None, ALU.max))
                                me.wait()
                                me.done(dve.reciprocal(r2[:, :], a2[:, :]))
                                me.done(dve.tensor_scalar(dd[:, :], a2[:, :], mean[:, 2:3], None, ALU.mult))
                                me.wait()
                                me.done(dve.tensor_scalar(r2[:, :], r2[:, :], 127.0, None, ALU.mult))
                                me.wait()
                                positive(dve, s_qb, n)
                                for q in range(CT):
                                    dve.tensor_scalar(qr[:, q, :], pr[:, q, :], r2[:, q:q + 1], ROUND,
                                                      ALU.mult, ALU.add).then_inc(s_qr, 1)
                            elif stage == "add":
                                dve.wait_ge(s_down, n + 2 * CT)
                                for q in range(CT):
                                    ins = dve.scalar_tensor_tensor(X[:, n + q, :], Y.bank(0)[:, q * D:(q + 1) * D], dd[:, q:q + 1],
                                                                   X[:, n + q, :], ALU.mult, ALU.add)
                                ins.then_inc(Y.free, 1)
                        run4(dve, do, me.clear)
                        me.wait()

        if phases < 4:
            with ExitStack() as fin:
                s_out = sem(fin, "s_out")
                with nc.Block() as block:
                    @block.sync
                    def _(sp):
                        for q in range(4):
                            n = TILES // 4
                            sp.dma_start(out_t[:, q * n:(q + 1) * n, :], X[:, q * n:(q + 1) * n, :]).then_inc(s_out, 16)
                        sp.wait_ge(s_out, 64)



_INS = ["x", "ctx_512", "itok_BxS2xS_0_7", "L0_xattn_Wq", "L0_xattn_Wk", "L0_xattn_Wv", "L0_xattn_Wo", "L0_xattn_bo",
        "L0_ffn_Wg", "L0_ffn_routing_bias", "L0_ffn_W1", "L0_ffn_W2", "L0_ffn_W3", "L0_ffn_Ws1", "L0_ffn_Ws2",
        "L0_ffn_Ws3", "L1_xattn_proj_in", "L1_xattn_proj_out", "L1_ffn_w_gate", "L1_ffn_w_up", "L1_ffn_w_down"]


def kernel(**inputs):
    import numpy as np
    import concourse.bacc as bacc
    from concourse.bass_utils import run_bass_kernel_spmd

    nc = bacc.Bacc("TRN2", target_bir_lowering=False, num_devices=1)
    arrays, args = {}, []
    for name in _INS:
        a = np.ascontiguousarray(inputs[name])
        arrays[f"in_{name}"] = a
        args.append(nc.dram_tensor(f"in_{name}", a.shape, mybir.dt.from_np(a.dtype), kind="ExternalInput").ap())
    args.append(nc.dram_tensor("out_0", (B, S, D), fp32, kind="ExternalOutput").ap())
    kernel_program(nc, *args)
    return run_bass_kernel_spmd(nc, [arrays], core_ids=[0]).results[0]["out_0"]
```

```python
import concourse.bass as bass
from concourse import mybir
from contextlib import ExitStack

fp32 = mybir.dt.float32
f32r = mybir.dt.float32r
bf16 = mybir.dt.bfloat16
int32 = mybir.dt.int32
ALU = mybir.AluOpType
ACT = mybir.ActivationFunctionType
AX = mybir.AxisListType

B, S, D = 64, 64, 128
DC = 64
P = 128
TILES = B * S // P
CT = 4
CHUNKS = TILES // CT
CW = CT * P
BPT = P // S
HEADS, HD = 16, 64
HP = HEADS // 2
E0, H0 = 9, D * 2 * 4 // 3
ER = E0 - 1
TOPK = 4
MAIN = H0 // P
REST = H0 - MAIN * P
RU = -(-E0 * REST // P)
NU0 = E0 * MAIN + RU
REST_LAST = E0 * REST - (RU - 1) * P
REST_PIECES = [[(e, max(0, m * P - e * REST), min(REST, (m + 1) * P - e * REST) - max(0, m * P - e * REST),
                 max(0, e * REST - m * P)) for e in range(E0) if e * REST < (m + 1) * P and (e + 1) * REST > m * P]
               for m in range(RU)]
E1, D1 = 8, 256
I1 = 512
EPS = 1e-5
ROUND = 1.5 * 2.0 ** 23


class Self:

    def __init__(self, eng, sem):
        self.eng, self.sem, self.n = eng, sem, 0

    def done(self, ins):
        ins.then_inc(self.sem, 1)
        self.n += 1

    def wait(self):
        self.eng.wait_ge(self.sem, self.n)

    def clear(self):
        self.wait()
        self.eng.sem_clear(self.sem)
        self.n = 0


class Ring:

    def __init__(self, banks, full, free, mid=None):
        self.banks, self.full, self.free, self.mid = banks, full, free, mid

    def bank(self, k):
        return self.banks[k % len(self.banks)]

    def wait_free(self, eng, n):
        eng.wait_ge(self.free, n + 1)

    def wait_full(self, eng, n):
        eng.wait_ge(self.full, n + 1)

    def wait_mid(self, eng, n):
        eng.wait_ge(self.mid, n + 1)

    def wait_read(self, eng, n):
        eng.wait_ge(self.free, n + 1 + len(self.banks))


def raw(ap):
    return ap.bitcast(fp32)


def kernel_program(nc, x, ctx_in, itok, Wq, Wk, Wv, Wo, bo, Wg, rbias, W1, W2, W3, Ws1, Ws2, Ws3,
                   p_in, p_out, w_gate, w_up, w_down, out, phases=4):
    top = ExitStack()
    with top:
        def sb(stack, name, shape, dt=fp32):
            return stack.enter_context(nc.sbuf_tensor(name, shape, dt))

        def sem(stack, name):
            return stack.enter_context(nc.semaphore(name))

        X = sb(top, "X", [P, TILES, D])
        MV = sb(top, "MV", [P, TILES, 2])
        ident = sb(top, "ident", [P, P])
        identb = sb(top, "identb", [P, P], bf16)
        w1n, w2n = (sb(top, n, [P, NU0, D]) for n in ("w1n", "w2n"))
        w3n = sb(top, "w3n", [D, NU0 * P])
        wgn, rb_bc = sb(top, "wgn", [ER, D]), sb(top, "rb_bc", [P, ER])
        s_w0 = sem(top, "s_w0")
        W0_LOADS = 2 * (4 + sum(len(pieces) for pieces in REST_PIECES)) + 6
        bank = [top.enter_context(nc.psum_tensor(f"bank{i}", [P, 512], fp32)) for i in range(8)]
        x_t = x.rearrange("b s d -> (b s) d").rearrange("(t p) d -> p t d", p=P)
        out_t = out.rearrange("b s d -> (b s) d").rearrange("(t p) d -> p t d", p=P)


        def residual(dve, me, got, c):
            part = X[:, bass.ds(c * CT, CT), :]
            me.done(dve.tensor_tensor(part, got[:, :].rearrange("p (t d) -> p t d", t=CT), part, ALU.add))

        def statistics(dve, me, bs, ag, c, free=None):
            me.wait()
            for j in range(CT):
                ins = dve.bn_stats(bs[:, j, :], X[:, c * CT + j, :])
                if j == 0 and free is not None:
                    ins.then_inc(free, 1)
                else:
                    me.done(ins)
            me.wait()
            for j in range(CT):
                me.done(dve.bn_aggr(ag[:, j, :], bs[:, j, :]))
            me.wait()
            me.done(dve.tensor_copy(MV[:, bass.ds(c * CT, CT), :], ag[:, :, :]))

        def finish_deviation(stack, tag):
            dev = sb(stack, f"dev{tag}", [P, TILES])
            s_var, s_dev = sem(stack, f"s_var{tag}"), sem(stack, f"s_dev{tag}")

            def variance(dve):
                dve.tensor_scalar(dev[:, :], MV[:, :, 1], EPS, None, ALU.add).then_inc(s_var, 1)

            def on_vector(dve, me):
                dve.wait_ge(s_dev, 1)
                me.done(dve.reciprocal(MV[:, :, 1], dev[:, :]))
                me.wait()

            def on_scalar(act):
                act.wait_ge(s_var, 1)
                act.activation(dev[:, :], dev[:, :], ACT.Sqrt).then_inc(s_dev, 1)
            return variance, on_vector, on_scalar

        def normalise(dve, me, st, xn, c, signal):
            me.done(dve.tensor_copy(st[:, :, :], MV[:, bass.ds(c * CT, CT), :]))
            me.wait()
            for j in range(CT):
                ins = dve.tensor_scalar(xn[:, j, :], X[:, c * CT + j, :], st[:, j, 0:1], st[:, j, 1:2],
                                        ALU.subtract, ALU.mult)
            ins.then_inc(signal, 1)

        p1 = ExitStack()
        with p1:
            GH, GL = (sb(p1, n, [P, HP, P], f32r) for n in ("GH", "GL"))
            VH, VL = (sb(p1, n, [P, HP, P], f32r) for n in ("VH", "VL"))
            bo_bc = sb(p1, "bo_bc", [P, D])
            st_t = sb(p1, "st_t", [P, CT * BPT, P])
            st_v = sb(p1, "st_v", [P, CT, BPT, 2, DC + 1])
            sel = sb(p1, "sel", [2 * HEADS, HP, 2, S], bf16)
            bs, ag = sb(p1, "bs", [P, CT, 6]), sb(p1, "ag", [P, CT, 2])

            dve_var, dve_dev, act_dev = finish_deviation(p1, "1")

            p0 = ExitStack()
            with p0:
                wq = sb(p0, "wq", [P, HP, P])
                wk, wv = sb(p0, "wk", [DC, HP, P]), sb(p0, "wv", [DC, HP, P])
                wo = sb(p0, "wo", [P, HP, D])
                wqT = sb(p0, "wqT", [P, HP, P])
                wkT, wvT = sb(p0, "wkT", [P, HP, 2, DC]), sb(p0, "wvT", [P, HP, 2, DC])
                s_wq = sem(p0, "s0_wq")
                bs0 = sb(p0, "bs0", [P, TILES // 2, 6])
                s_x, s_w, s_ones = [sem(p0, "s0_x0"), sem(p0, "s0_x1")], sem(p0, "s0_w"), sem(p0, "s0_bo")
                s_const, s_tr, s_cp, s_cpa = (sem(p0, n) for n in ("s0_const", "s0_tr", "s0_cp", "s0_cpa"))
                s_mm, s_hi, s_lo, s_me, s_pool = (sem(p0, n) for n in ("s0_mm", "s0_hi", "s0_lo", "s0_me", "s0_pool"))
                wkT_bank, wvT_bank = (bank[i][:, :].rearrange("p (h c) -> p h c", h=HP) for i in (2, 3))
                with nc.Block() as block:
                    @block.sync
                    def _(sp):
                        sp.dma_start(wq[:, :, :], Wq.rearrange("i (h c) -> i h c", h=HP)).then_inc(s_wq, 16)
                        sp.dma_start(wk[:, :, :], Wk.rearrange("i (h c) -> i h c", h=HP)).then_inc(s_w, 16)
                        for q in range(4):
                            n = TILES // 4
                            sp.dma_start(X[:, q * n:(q + 1) * n, :], x_t[:, q * n:(q + 1) * n, :]).then_inc(s_x[q // 2], 16)

                    @block.scalar
                    def _(act):
                        act.dma_start(wv[:, :, :], Wv.rearrange("i (h c) -> i h c", h=HP)).then_inc(s_w, 16)
                        act.dma_start(wo[:, :, :], Wo.rearrange("(h p) n -> p h n", p=P)).then_inc(s_w, 16)
                        act.dma_start(bo_bc[:, :], bo.rearrange("(a n) -> a n", a=1).to_broadcast([P, D])).then_inc(s_ones, 16)
                        for k in range(2):
                            act.wait_ge(s_tr, k + 1)
                            act.activation(wqT[:, 4 * k:4 * k + 4, :].rearrange("p h c -> p (h c)"), bank[k][:, :],
                                           ACT.Copy, scale=float(HD) ** -0.5).then_inc(s_cpa, 1)
                        act.wait_ge(s_tr, 4)
                        act.wait_ge(s_const, 2)
                        act.copy(wvT[0:DC, :, 0, :], wvT_bank[0:DC]).then_inc(s_cpa, 1)
                        act.copy(wvT[DC:P, :, 1, :], wvT_bank[DC:P]).then_inc(s_cpa, 1)
                        for k in range(4):
                            act.wait_ge(s_mm, k + 1)
                            hi = (GH, VH)[k // 2]
                            act.copy(hi[:, 4 * (k % 2):4 * (k % 2) + 4, :].rearrange("p h c -> p (h c)"),
                                     bank[4 + k][:, :]).then_inc(s_hi, 1)
                        act_dev(act)
                        act.wait_ge(s_ones, 16)

                    @block.gpsimd
                    def _(pool):
                        me = Self(pool, s_pool)
                        me.done(pool.memset(ident[:, :], 0.0))
                        me.done(pool.memset(sel[:, :, :, :], 0.0))
                        me.wait()
                        me.done(pool.affine_select(out=ident[:, :], in_=ident[:, :], compare_op=ALU.not_equal, fill=1.0,
                                                   base=0, pattern=[[-1, P]], channel_multiplier=1))
                        me.wait()
                        pool.tensor_copy(identb[:, :], ident[:, :]).then_inc(s_const, 1)
                        pool.memset(wkT[:, :, :, :], 0.0)
                        pool.memset(wvT[:, :, :, :], 0.0).then_inc(s_const, 1)
                        for base in (0, -HEADS):
                            me.done(pool.affine_select(out=sel[:, :, :, :], in_=sel[:, :, :, :],
                                                       compare_op=ALU.not_equal, fill=1.0, base=base,
                                                       pattern=[[-2, HP], [-1, 2], [0, S]], channel_multiplier=1))
                            me.wait()
                        pool.memset(st_t[:, :, :], 0.0)
                        me.done(pool.memset(st_v[:, :, :, :, :], 0.0))
                        me.wait()
                        for par in range(2):
                            me.done(pool.memset(st_v[par * S:(par + 1) * S, :, :, par, DC:DC + 1], 1.0))
                        me.wait()

                    @block.tensor
                    def _(pe):
                        pe.wait_ge(s_const, 1)
                        pe.wait_ge(s_wq, 16)
                        for h in range(HP):
                            ins = pe.transpose(bank[h // 4][:, h % 4 * P:h % 4 * P + P], wq[:, h, :], ident[:, :])
                            if h % 4 == 3:
                                ins.then_inc(s_tr, 1)
                        pe.wait_ge(s_w, 48)
                        for w, b in ((wk, 2), (wv, 3)):
                            for h in range(HP):
                                ins = pe.transpose(bank[b][:, h * DC:(h + 1) * DC], w[:, h, :], ident[0:DC, 0:DC])
                            ins.then_inc(s_tr, 1)
                        pe.wait_ge(s_cpa, 2)
                        pe.wait_ge(s_cp, 2)
                        for h in range(HP):
                            ins = pe.matmul(bank[4 + h // 4][:, h % 4 * P:h % 4 * P + P], wqT[:, h, :],
                                            wkT[:, h, :, :].rearrange("p a c -> p (a c)"), start=True, stop=True)
                            if h % 4 == 3:
                                ins.then_inc(s_mm, 1)
                        pe.wait_ge(s_cpa, 4)
                        for h in range(HP):
                            ins = pe.matmul(bank[6 + h // 4][:, h % 4 * P:h % 4 * P + P],
                                            wvT[:, h, :, :].rearrange("p a c -> p (a c)"), wo[:, h, :],
                                            start=True, stop=True)
                            if h % 4 == 3:
                                ins.then_inc(s_mm, 1)

                    @block.vector
                    def _(dve):
                        me = Self(dve, s_me)

                        def statistics(half):
                            dve.wait_ge(s_x[half], 32)
                            for j in range(TILES // 2):
                                me.done(dve.bn_stats(bs0[:, j, :], X[:, half * (TILES // 2) + j, :]))
                            me.wait()
                            for j in range(TILES // 2):
                                me.done(dve.bn_aggr(MV[:, half * (TILES // 2) + j, :], bs0[:, j, :]))
                            me.wait()
                        dve.wait_ge(s_tr, 3)
                        dve.wait_ge(s_const, 2)
                        dve.tensor_copy(wkT[0:DC, :, 0, :], wkT_bank[0:DC]).then_inc(s_cp, 1)
                        dve.tensor_copy(wkT[DC:P, :, 1, :], wkT_bank[DC:P]).then_inc(s_cp, 1)
                        statistics(0)
                        statistics(1)
                        dve_var(dve)
                        for k in range(4):
                            dve.wait_ge(s_hi, k + 1)
                            hi, lo = ((GH, GL), (VH, VL))[k // 2]
                            part = slice(4 * (k % 2), 4 * (k % 2) + 4)
                            dve.tensor_tensor(lo[:, part, :].rearrange("p h c -> p (h c)"), bank[4 + k][:, :],
                                              raw(hi[:, part, :]).rearrange("p h c -> p (h c)"),
                                              ALU.subtract).then_inc(s_lo, 1)
                        dve_dev(dve, me)

            with ExitStack() as st1:
                XH, XL = (sb(st1, n, [P, CW], f32r) for n in ("XH", "XL"))
                QH, QL = (sb(st1, n, [P, HP, CW], f32r) for n in ("QH", "QL"))
                QB = sb(st1, "QB", [P, HP, CW], bf16)
                CH, CL = (sb(st1, n, [P, CT * BPT, P], f32r) for n in ("CH", "CL"))
                CB = sb(st1, "CB", [P, CT * BPT, P], bf16)
                PT = sb(st1, "PT", [P, HP, P])
                On = sb(st1, "On", [P, HEADS, HD])
                OH, OL = (sb(st1, n, [P, HP, CW], f32r) for n in ("OH", "OL"))
                xn, stt = sb(st1, "xn1", [P, CT, D]), sb(st1, "st1", [P, CT, 2])
                aT = sb(st1, "aT", [P, CW])
                one = sb(st1, "one", [P, 1, 1])
                nm = sb(st1, "nm", [P, HEADS])
                nmb = sb(st1, "nmb", [P, 2 * HEADS], bf16)
                mT = sb(st1, "mT", [2 * HEADS, P], bf16)
                rd = sb(st1, "rd", [P, HEADS])
                R = Ring(bank[0:2], sem(st1, "r_full"), sem(st1, "r_free"), sem(st1, "r_high"))
                A = Ring(bank[2:4], sem(st1, "scores_full"), sem(st1, "scores_free"))
                T = Ring(bank[4:6], sem(st1, "scoresT_full"), sem(st1, "scoresT_free"), sem(st1, "query_high"))
                O = Ring(bank[6:8], sem(st1, "o_full"), sem(st1, "o_free"))
                s_me, s_xn, s_nm = (sem(st1, n) for n in ("s1_me", "s1_xn", "s1_nm"))
                s_qb, s_cb, s_bo = (sem(st1, n) for n in ("s1_qb", "s1_cb", "s1_bo"))
                s_stt, s_one = sem(st1, "s1_st_t"), sem(st1, "s1_one")
                s_stv = [sem(st1, f"s1_st_v{j}") for j in range(CT)]
                R0, RN, AN, T0, TN, ON = 6, 14, 12, 6, 14, 14
                Q_ORDER = (1, 3, 0, 5, 2, 7, 4, 6)
                TQ, RQ = (1, 3, 5, 7, 4, 6), (0, 2)
                GRP = [(0, 3), (3, 6), (6, HP)]

                ctx_k = ctx_in.rearrange("b k s -> k b s")

                def pv_item(c, j):
                    return c * ON + 3 * j

                def chunk_order(c, first, more, do):
                    r, a, t, o = R0 + c * RN, c * AN, T0 + c * TN, c * ON
                    turned = (0, 2, 6, 12) if more else (0, 2, 4, 6)

                    def query(h):
                        if h in TQ:
                            do("query", h, t, 8 + TQ.index(h), c + 1, r + 5)
                        else:
                            do("query", h, r, 10 + RQ.index(h), c + 1, r + 5)
                    for j in range(CT):
                        if 0 < j < CT - 1:
                            do("max", j + 1, a, 3 * j + 3, c)
                        do("scoresT", j, t, 2 * j, c, r - 1)
                        if j:
                            do("turn", j - 1, r, turned[j - 1], c)
                        elif not first:
                            do("back", 0, o, -1, c - 1)
                        if j == CT - 1:
                            break
                        for g in range(3):
                            do("pv", j, o, 3 * j + g, c)
                            if j and g == 0:
                                do("turn low", j - 1, r, turned[j - 1], c)
                        if j == 0 and not first:
                            do("stats", 0, o, -1, c - 1)
                        if more and j == 1:
                            do("norm", 0, 0, 0, c + 1)
                        if more and j == 2:
                            do("normT", 0, r, 4, c + 1)
                        do("maxT", j + 1, a, 3 * j + 5, c)
                    for g, heads in enumerate(((1, 3), (0, 5), (2, 7, 4))):
                        do("pv", 3, o, 9 + g, c)
                        if g == 0:
                            do("turn low", 2, r, turned[2], c)
                        if more:
                            for h in heads:
                                query(h)
                            if g == 0:
                                do("ctxT", 0, r, 8, c + 1)
                    do("turn", 3, r, turned[3], c)
                    do("turn low", 3, r, turned[3], c)
                    if more:
                        query(6)
                    do("project", 0, o, 12, c, r + turned[3] + 1)
                    if more:
                        do("max", 0, a, 12, c + 1)
                    do("project", 1, o, 12, c, r + turned[3] + 1)
                    if more:
                        do("maxT", 0, a, 14, c + 1)
                    do("project", 2, o, 12, c)
                    if more:
                        do("max", 1, a, 15, c + 1)
                    else:
                        do("back", 0, o, 13, c)
                        do("stats", 0, o, 13, c)

                def start_order(do):
                    do("norm", 0, 0, 0, 0)
                    do("normT", 0, 0, 0, 0)
                    do("ctxT", 0, 0, 2, 0)
                    for h in Q_ORDER:
                        do("query", h, 0, TQ.index(h) if h in TQ else 4 + RQ.index(h), 0, 1)
                    do("max", 0, 0, 0, 0)
                    do("maxT", 0, 0, 2, 0)
                    do("max", 1, 0, 3, 0)

                def run(eng, do, clear=lambda: None):
                    start_order(do)
                    chunk_order(0, True, True, do)
                    clear()
                    with eng.Fori(1, CHUNKS - 1) as c:
                        chunk_order(c, False, True, do)
                        clear()
                    chunk_order(CHUNKS - 1, False, False, do)

                with nc.Block() as block:
                    @block.sync
                    def _(sp):
                        def load_t(c):
                            for par in range(2):
                                sp.dma_start(st_t[par * S:(par + 1) * S, :, par * DC:(par + 1) * DC],
                                             ctx_k[:, bass.ds(c * CT * BPT, CT * BPT), :]).then_inc(s_stt, 16)

                        def load_v(c, j):
                            for par in range(2):
                                sp.dma_start(st_v[par * S:(par + 1) * S, j, :, par, 0:DC],
                                             ctx_k[:, bass.ds((c * CT + j) * BPT, BPT), :]).then_inc(s_stv[j], 16)
                        load_t(0)
                        for j in range(CT):
                            load_v(0, j)
                        sp.wait_ge(R.full, 4)
                        load_t(1)
                        for to, shared, routed in ((w1n, Ws1, W1), (w2n, Ws2, W2)):
                            for k in range(MAIN):
                                h = slice(k * P, (k + 1) * P)
                                sp.dma_start(to[:, k, :], shared[h, :]).then_inc(s_w0, 16)
                                sp.dma_start(to[:, MAIN:E0 * MAIN, :].rearrange("p (e k) d -> p e k d", k=MAIN)[:, :, k, :],
                                             routed[:, h, :].rearrange("e h d -> h e d")).then_inc(s_w0, 16)
                            for m, pieces in enumerate(REST_PIECES):
                                for e, first, n, at in pieces:
                                    h = slice(MAIN * P + first, MAIN * P + first + n)
                                    sp.dma_start(to[at:at + n, E0 * MAIN + m, :],
                                                 routed[e - 1, h, :] if e else shared[h, :]).then_inc(s_w0, 16)
                        main, rest = slice(0, MAIN * P), slice(MAIN * P, H0)
                        r0 = E0 * MAIN * P
                        sp.dma_start(w3n[:, main], Ws3[:, main]).then_inc(s_w0, 16)
                        sp.dma_start(w3n[:, r0:r0 + REST], Ws3[:, rest]).then_inc(s_w0, 16)
                        sp.dma_start(w3n[:, MAIN * P:r0].rearrange("d (e h) -> d e h", e=ER),
                                     W3[:, :, main].rearrange("e d h -> d e h")).then_inc(s_w0, 16)
                        sp.dma_start(w3n[:, r0 + REST:r0 + E0 * REST].rearrange("d (e h) -> d e h", e=ER),
                                     W3[:, :, rest].rearrange("e d h -> d e h")).then_inc(s_w0, 16)
                        sp.dma_start(wgn[:, :], Wg).then_inc(s_w0, 16)
                        sp.dma_start(rb_bc[:, :], rbias.rearrange("(a e) -> a e", a=1).to_broadcast([P, ER])).then_inc(s_w0, 16)

                        def refill(c):
                            for j in range(CT):
                                sp.wait_ge(O.full, pv_item(c - 1, j) + 3)
                                load_v(c, j)
                        with sp.Fori(1, CHUNKS - 1) as c:
                            refill(c)
                            sp.wait_ge(R.full, R0 + (c - 1) * RN + 10)
                            load_t(c + 1)
                        refill(CHUNKS - 1)

                    @block.tensor
                    def _(pe):
                        def do(stage, j, base, k, c, needs=None):
                            n = base + k
                            if stage == "normT":
                                pe.wait_ge(s_xn, c + 1)
                                for i in range(2):
                                    R.wait_free(pe, n + i)
                                    for q in range(2):
                                        ins = pe.transpose(R.bank(k + i)[:, q * P:(q + 1) * P], xn[:, 2 * i + q, :], ident[:, :])
                                    ins.then_inc(R.full, 1)
                            elif stage == "ctxT":
                                pe.wait_ge(s_stt, 32 * (c + 1))
                                for i in range(2):
                                    R.wait_free(pe, n + i)
                                    for q in range(4):
                                        ins = pe.transpose(R.bank(k + i)[:, q * P:(q + 1) * P], st_t[:, 4 * i + q, :], ident[:, :])
                                    ins.then_inc(R.full, 1)
                            elif stage == "query":
                                if j == Q_ORDER[0]:
                                    R.wait_read(pe, needs)
                                K = T if j in TQ else R
                                K.wait_free(pe, n)
                                for i, (w, v) in enumerate(((GH, XH), (GL, XH), (GH, XL))):
                                    ins = pe.matmul(K.bank(k)[:, :], w[:, j, :], v[:, :], start=(i == 0), stop=(i == 2))
                                ins.then_inc(K.full, 1)
                            elif stage == "max":
                                if j == 0:
                                    pe.wait_ge(s_cb, c + 1)
                                for i in range(2):
                                    A.wait_free(pe, n + i)
                                    for h in range(4 * i, 4 * i + 4):
                                        if j == 0:
                                            pe.wait_ge(s_qb, HP * c + Q_ORDER.index(h) + 1)
                                        for b in range(BPT):
                                            ins = pe.matmul(A.bank(k + i)[b * S:(b + 1) * S, h % 4 * P:(h % 4 + 1) * P],
                                                            QB[:, h, j * P + b * S:j * P + (b + 1) * S],
                                                            CB[:, j * BPT + b, :], start=True, stop=True,
                                                            skip_group_check=True)
                                    ins.then_inc(A.full, 1)
                            elif stage == "maxT":
                                pe.wait_ge(s_nm, c * CT + j + 1)
                                A.wait_free(pe, n)
                                pe.transpose(A.bank(k)[0:2 * HEADS, 0:S].bitcast(bf16), nmb[:, :], identb[:, :]).then_inc(A.full, 1)
                            elif stage == "scoresT":
                                if j == 0:
                                    R.wait_read(pe, needs)
                                    T.wait_read(pe, base - 1)
                                for i in range(2):
                                    T.wait_free(pe, n + i)
                                    to = T.bank(k + i)[:, :].rearrange("p (h q) -> p h q", h=4)
                                    hs = slice(4 * i, 4 * i + 4)
                                    for b in range(BPT):
                                        q = slice(j * P + b * S, j * P + (b + 1) * S)
                                        for m, (w, v) in enumerate(((CH, QH), (CL, QH), (CH, QL))):
                                            pe.matmul(to[:, :, b * S:(b + 1) * S], w[:, j * BPT + b, :], v[:, hs, q],
                                                      start=(b == 0 and m == 0), stop=False, skip_group_check=True)
                                    if i == 0:
                                        A.wait_read(pe, c * AN + 3 * j + 2)
                                    for h in range(4):
                                        ins = pe.matmul(to[:, h, :], sel[:, 4 * i + h, :, :].rearrange("p a c -> p (a c)"),
                                                        mT[:, :], start=False, stop=(h == 3), skip_group_check=True)
                                    ins.then_inc(T.full, 1)
                            elif stage == "pv":
                                g = k - 3 * j
                                h0, h1 = GRP[g]
                                if g == 0:
                                    pe.wait_ge(s_stv[j], 32 * (c + 1))
                                T.wait_read(pe, T0 + c * TN + 2 * j + (h1 > 4))
                                O.wait_free(pe, n)
                                for h in range(h0, h1):
                                    for b in range(BPT):
                                        ins = pe.matmul(O.bank(k)[b * S:(b + 1) * S, (h - h0) * 130:(h - h0 + 1) * 130],
                                                        PT[:, h, b * S:(b + 1) * S],
                                                        st_v[:, j, b, :, :].rearrange("p a c -> p (a c)"),
                                                        start=True, stop=True, skip_group_check=True)
                                ins.then_inc(O.full, 1)
                            elif stage == "turn":
                                O.wait_read(pe, pv_item(c, j) + 2)
                                for i in range(2):
                                    R.wait_free(pe, n + i)
                                    for q in range(4):
                                        h = 4 * i + q
                                        ins = pe.transpose(R.bank(k + i)[:, q * P:(q + 1) * P],
                                                           On[:, 2 * h:2 * h + 2, :].rearrange("p a c -> p (a c)"), ident[:, :])
                                    ins.then_inc(R.full, 1)
                            elif stage == "project":
                                if j == 0:
                                    R.wait_read(pe, needs - 1)
                                    O.wait_free(pe, n)
                                steps = [(w, v, h) for h in range(HP) for w, v in ((VH, OH), (VH, OL), (VL, OH))]
                                for i, (w, v, h) in list(enumerate(steps))[(0, 12, 20)[j]:(12, 20, 24)[j]]:
                                    if i == 12:
                                        R.wait_read(pe, needs)
                                    ins = pe.matmul(O.bank(k)[:, :], w[:, h, :], v[:, h, :],
                                                    start=(i == 0), stop=(i == len(steps) - 1))
                                if j == 2:
                                    ins.then_inc(O.full, 1)
                            elif stage == "back":
                                O.wait_read(pe, n - 1)
                                O.wait_free(pe, n)
                                for q in range(CT):
                                    ins = pe.transpose(O.bank(k)[:, q * P:(q + 1) * P], aT[:, q * P:(q + 1) * P], ident[:, :])
                                ins.then_inc(O.full, 1)
                        run(pe, do)

                    @block.scalar
                    def _(act):
                        act.sem_inc(T.free, 2)

                        def high(to, k, n, width=512, heads=1):
                            R.wait_full(act, n)
                            got = R.bank(k)[:, 0:width]
                            if heads > 1:
                                got = got.rearrange("p (h q) -> p h q", h=heads)
                            act.copy(to, got).then_inc(R.mid, 1)

                        def do(stage, j, base, k, c, needs=None):
                            n = base + k
                            if stage == "normT":
                                for i in range(2):
                                    high(XH[:, i * 2 * P:(i + 1) * 2 * P], k + i, n + i, 2 * P)
                            elif stage == "ctxT":
                                for i in range(2):
                                    high(CH[:, 4 * i:4 * i + 4, :].rearrange("p h c -> p (h c)"), k + i, n + i)
                            elif stage == "query":
                                K = T if j in TQ else R
                                K.wait_full(act, n)
                                act.copy(QH[:, j, :], K.bank(k)[:, :]).then_inc(K.mid, 1)
                            elif stage == "maxT":
                                A.wait_full(act, n)
                                act.copy(mT[:, :], A.bank(k)[0:2 * HEADS, 0:S].bitcast(bf16)).then_inc(A.free, 1)
                            elif stage == "project" and j == 2:
                                O.wait_full(act, n)
                                act.copy(aT[:, :], O.bank(k)[:, :]).then_inc(O.free, 1)
                            elif stage == "turn":
                                for i in range(2):
                                    high(OH[:, 4 * i:4 * i + 4, j * P:(j + 1) * P], k + i, n + i, heads=4)
                            elif stage == "scoresT":
                                for i in range(2):
                                    T.wait_full(act, n + i)
                                    act.activation(PT[:, 4 * i:4 * i + 4, :].rearrange("p h c -> p (h c)"),
                                                   T.bank(k + i)[:, :], ACT.Exp).then_inc(T.free, 1)
                        run(act, do)

                    @block.gpsimd
                    def _(pool):
                        pool.memset(one[:, :, :], 1.0).then_inc(s_one, 1)
                        pool.wait_ge(s_one, 1)

                        def do(stage, j, base, k, c, needs=None):
                            n = base + k
                            if stage == "norm":
                                pool.wait_ge(s_xn, c + 1)
                                for q in range(CT):
                                    ins = pool.tensor_tensor(X[:, c * CT + q, :], X[:, c * CT + q, :], bo_bc[:, :], ALU.add)
                                ins.then_inc(s_bo, 1)
                            elif stage == "ctxT":
                                R.wait_mid(pool, n + 1)
                                pool.tensor_tensor(CB[:, :, :], raw(CH[:, :, :]), one[:, :, :].to_broadcast([P, CT * BPT, P]), ALU.mult).then_inc(s_cb, 1)
                            elif stage == "query":
                                if j in TQ:
                                    pool.wait_ge(T.mid, len(TQ) * c + TQ.index(j) + 1)
                                else:
                                    R.wait_mid(pool, n)
                                pool.tensor_tensor(QB[:, j, :], raw(QH[:, j, :]), one[:, 0, :].to_broadcast([P, CW]), ALU.mult).then_inc(s_qb, 1)
                        run(pool, do)

                    @block.vector
                    def _(dve):
                        me = Self(dve, s_me)
                        dve.sem_inc(R.free, 2)
                        dve.sem_inc(A.free, 2)
                        dve.sem_inc(O.free, 2)

                        def low(hi, lo, k, n, width=512, heads=1):
                            R.wait_mid(dve, n)
                            got = R.bank(k)[:, 0:width]
                            if heads > 1:
                                got = got.rearrange("p (h q) -> p h q", h=heads)
                            dve.tensor_tensor(lo, got, raw(hi), ALU.subtract).then_inc(R.free, 1)

                        def do(stage, j, base, k, c, needs=None):
                            n = base + k
                            if stage == "norm":
                                normalise(dve, me, stt, xn, c, s_xn)
                            elif stage == "normT":
                                for i in range(2):
                                    part = slice(i * 2 * P, (i + 1) * 2 * P)
                                    low(XH[:, part], XL[:, part], k + i, n + i, 2 * P)
                            elif stage == "ctxT":
                                for i in range(2):
                                    low(CH[:, 4 * i:4 * i + 4, :].rearrange("p h c -> p (h c)"),
                                        CL[:, 4 * i:4 * i + 4, :].rearrange("p h c -> p (h c)"), k + i, n + i)
                            elif stage in ("turn", "turn low"):
                                for i in (int(stage == "turn low"),):
                                    hs, q = slice(4 * i, 4 * i + 4), slice(j * P, (j + 1) * P)
                                    low(OH[:, hs, q], OL[:, hs, q], k + i, n + i, heads=4)
                            elif stage == "query":
                                if j in TQ:
                                    dve.wait_ge(T.mid, len(TQ) * c + TQ.index(j) + 1)
                                    dve.tensor_tensor(QL[:, j, :], T.bank(k)[:, :], raw(QH[:, j, :]), ALU.subtract).then_inc(T.free, 1)
                                else:
                                    low(QH[:, j, :], QL[:, j, :], k, n)
                            elif stage == "max":
                                if not (isinstance(n, int) and n == 0):
                                    A.wait_read(dve, n - 1)
                                for i in range(2):
                                    A.wait_full(dve, n + i)
                                    dve.tensor_reduce(nm[:, 8 * i:8 * i + 8], A.bank(k + i)[:, :].rearrange("p (h s) -> p h s", s=S),
                                                      AX.X, ALU.max, negate=True).then_inc(A.free, 1)
                                A.wait_read(dve, n + 1)
                                me.done(dve.tensor_copy(nmb[:, 0:HEADS], nm[:, :]))
                                me.wait()
                                dve.tensor_tensor(nmb[:, HEADS:2 * HEADS], nm[:, :], nmb[:, 0:HEADS], ALU.subtract).then_inc(s_nm, 1)
                            elif stage == "pv":
                                h0, h1 = GRP[k - 3 * j]
                                O.wait_full(dve, n)
                                w = 2 * (h1 - h0)
                                got = O.bank(k)[:, 0:w * 65].rearrange("p (h c) -> p h c", c=65)
                                me.done(dve.reciprocal(rd[:, 2 * h0:2 * h1], got[:, :, 64]))
                                me.wait()
                                dve.tensor_tensor(On[:, 2 * h0:2 * h1, :], got[:, :, 0:HD],
                                                  rd[:, 2 * h0:2 * h1].rearrange("p (h a) -> p h a", a=1).to_broadcast([P, w, HD]),
                                                  ALU.mult).then_inc(O.free, 1)
                            elif stage == "back":
                                O.wait_full(dve, n)
                                dve.wait_ge(s_bo, c + 1)
                                residual(dve, me, O.bank(k), c)
                                me.wait()
                                dve.sem_inc(O.free, 1)
                            elif stage == "stats":
                                statistics(dve, me, bs, ag, c)
                        run(dve, do, me.clear)
                        me.wait()

        def turn_weights(name, st, s_in, loads, items, dev, gates, load, ternary=None):
            dve_var, dve_dev, act_dev = dev
            gates.temporaries(st)
            s_me = sem(st, name + "_me")
            K = Ring(bank[0:6], sem(st, name + "_full"), sem(st, name + "_free"), sem(st, name + "_high"))
            with nc.Block() as block:
                @block.sync
                def _(sp):
                    load(sp)
                    sp.wait_ge(s_in, 16 * loads)

                @block.tensor
                def _(pe):
                    pe.wait_ge(s_in, 16 * loads)
                    for n, (parts, rows, cols, hi, lo) in enumerate(items):
                        if ternary and n == 4:
                            ternary.sums(pe)
                        K.wait_free(pe, n)
                        for col, m, src in parts:
                            ins = pe.transpose(K.bank(n)[0:rows, col:col + m], src, ident[0:m, 0:m])
                        ins.then_inc(K.full, 1)
                    if ternary:
                        ternary.turn(pe)

                @block.scalar
                def _(act):
                    act_dev(act)
                    for n, (parts, rows, cols, hi, lo) in enumerate(items):
                        K.wait_full(act, n)
                        act.copy(hi, K.bank(n)[0:rows, 0:cols]).then_inc(K.mid, 1)
                    if ternary:
                        ternary.on_scalar(act)

                @block.vector
                def _(dve):
                    dve.sem_inc(K.free, len(K.banks))
                    dve_var(dve)
                    if ternary:
                        ternary.on_vector(dve)
                    dve_dev(dve, Self(dve, s_me))
                    for n, (parts, rows, cols, hi, lo) in enumerate(items):
                        K.wait_mid(dve, n)
                        dve.tensor_tensor(lo, K.bank(n)[0:rows, 0:cols], raw(hi), ALU.subtract).then_inc(K.free, 1)
                        if ternary and n == len(items) - 4:
                            ternary.clip(dve)
                    gates.constants_on_vector(dve)

                @block.gpsimd
                def _(pool):
                    gates.constants_on_gpsimd(pool)
                    if ternary:
                        ternary.on_gpsimd(pool)

        HALF = 64

        def experts_phase(tag, st, NU, up, down, rows, weighted, gates):
            glu = len(up(0)) == 2
            NS = max(w for w in weighted if w is not None) + 1
            NG = sum(w is not None for w in weighted)
            user = [[u for u in range(NU) if weighted[u] == s] for s in range(NS)]
            HD = 3 if glu else 4
            LAG, TURN = (3, 1) if glu else (4, 1)
            AHEAD = 4
            NORM, NORMT = (6, 9) if glu else (10, 13)
            assert NU % HD == 0 and NU % 4 == 0 and NS % 2 == 0 and CHUNKS % 2 == 0
            XH, XL = ([sb(st, f"{n}{tag}{q}", [P, CW], f32r) for q in range(2)] for n in ("XH", "XL"))
            xn, stt = sb(st, "xn" + tag, [P, CT, D]), sb(st, "stt" + tag, [P, CT, 2])
            bs, ag = sb(st, "bs" + tag, [P, CT, 6]), sb(st, "ag" + tag, [P, CT, 2])
            act1 = sb(st, "act1" + tag, [P, 2, CW]) if glu else None
            hid = sb(st, "hid" + tag, [P, HD, CW])
            HH, HL = (sb(st, n + tag, [P, HD, CW], f32r) for n in ("HH", "HL"))
            WB = sb(st, "WB" + tag, [P, 2, CW])
            acc = sb(st, "acc" + tag, [P, CW])
            U1 = Ring(bank[0:2] if glu else bank[0:4], sem(st, "u1_full" + tag), sem(st, "u1_free" + tag))
            U2 = Ring(bank[2:4], sem(st, "u2_full" + tag), sem(st, "u2_free" + tag))
            EO = Ring(bank[4:6], None, sem(st, "eo_free" + tag))
            R = Ring(bank[6:7], sem(st, "r_full" + tag), sem(st, "r_free" + tag), sem(st, "r_high" + tag))
            WBK = Ring(bank[7:8], sem(st, "wb_full" + tag), sem(st, "wb_free" + tag))
            s_me, s_xn, s_gated, s_hi, s_lo, s_down = (
                sem(st, n + tag) for n in ("me", "x_normal", "hidden_weighted", "h_high", "h_low", "down_done"))
            RI = gates.items

            def r_item(c, i):
                return RI * c + RI - 2 + i

            def x_item(c):
                return 0 if isinstance(c, int) and c == 0 else r_item(c - 1, 1)

            def wait_count(eng, sem_, value):
                if not (isinstance(value, int) and value <= 0):
                    eng.wait_ge(sem_, value)

            def gated(c, u):
                return c * NG + sum(w is not None for w in weighted[:u + 1])

            def order(c, q, first, last, do):
                def past(stage, u):
                    if u >= 0:
                        do(stage, u, c, q)
                    elif not first:
                        do(stage, NU + u, c - 1, 1 - q)

                for v in range(NU):
                    do("up", v, c, q)
                    if v == 1 and first:
                        for stage, item in gates.late:
                            do(stage, item, 0, 0)
                        if user[0][0] == 0:
                            do("spread", 0, 0, 0)
                    for s in range(NS):
                        if gates.masks and user[s][0] - AHEAD == v:
                            do("mask", s, c, q)
                        if gates.masks and user[s][0] - AHEAD == v - NU and not last:
                            do("mask", s, c + 1, 1 - q)
                        if user[s][0] - 1 == v:
                            do("spread", s, c, q)
                        if user[s][0] - 1 == v - NU and not last:
                            do("spread", s, c + 1, 1 - q)
                    past("hidden", v - TURN)
                    past("down", v - LAG)
                    if v == LAG and not first:
                        do("collect", 0, c - 1, 1 - q)
                    if v == LAG + 2 and not first:
                        do("back", r_item(c, 0), c - 1, 1 - q)
                    if v == LAG + 4 and not first:
                        do("stats", r_item(c, 0), c - 1, 1 - q)
                    if not last:
                        if v == NORM:
                            do("norm", 0, c + 1, 1 - q)
                        if v == NORMT:
                            do("normT", r_item(c, 1), c + 1, 1 - q)
                        for stage, step, i in gates.stages:
                            if v == step:
                                do(stage, r_item(c, i), c + 1, 1 - q)

            def run(eng, do, clear=lambda: None):
                do("norm", 0, 0, 0)
                do("normT", 0, 0, 0)
                for stage, item in gates.first:
                    do(stage, item, 0, 0)
                for s in range(NS):
                    if gates.masks and user[s][0] < AHEAD:
                        do("mask", s, 0, 0)
                order(0, 0, True, False, do)
                clear()
                with eng.Fori(0, CHUNKS // 2 - 1) as i:
                    order(i * 2 + 1, 1, False, False, do)
                    order(i * 2 + 2, 0, False, False, do)
                    clear()
                order(CHUNKS - 1, 1, False, True, do)
                for v in range(LAG):
                    if NU - TURN + v < NU:
                        do("hidden", NU - TURN + v, CHUNKS - 1, 1)
                    do("down", NU - LAG + v, CHUNKS - 1, 1)
                do("collect", 0, CHUNKS - 1, 1)
                do("back", r_item(CHUNKS - 1, 1), CHUNKS - 1, 1)
                do("stats", r_item(CHUNKS - 1, 1), CHUNKS - 1, 1)

            with nc.Block() as block:
                @block.tensor
                def _(pe):
                    def do(stage, v, c, q):
                        n = c * NU + v
                        if stage == "up":
                            if v == 0:
                                R.wait_read(pe, x_item(c))
                            for i, (hi, lo) in enumerate(up(v)):
                                U = (U1, U2)[i]
                                U.wait_free(pe, n)
                                for m, (w, x_) in enumerate(((hi, XH), (lo, XH), (hi, XL))):
                                    ins = pe.matmul(U.bank(v)[0:rows(v), :], w, x_[q][:, :], start=(m == 0), stop=(m == 2))
                                ins.then_inc(U.full, 1)
                        elif stage == "down":
                            pe.wait_ge(s_lo, n + 1)
                            if v == 0:
                                EO.wait_free(pe, c)
                            hi, lo = down(v)
                            for m, (w, h) in enumerate(((hi, HH), (lo, HH), (hi, HL))):
                                ins = pe.matmul(EO.bank(q)[:, :], w, h[0:rows(v), v % HD, :],
                                                start=(v == 0 and m == 0), stop=(v == NU - 1 and m == 2))
                            ins.then_inc(s_down, 1)
                        elif stage == "spread":
                            gates.ready(pe, R, v, c)
                            WBK.wait_free(pe, c * NS + v)
                            w, x_ = gates.product(v)
                            pe.matmul(WBK.bank(0)[:, :], w, x_, start=True, stop=True).then_inc(WBK.full, 1)
                        elif stage == "back":
                            EO.wait_read(pe, c)
                            R.wait_free(pe, v)
                            for j in range(CT):
                                ins = pe.transpose(R.bank(0)[:, j * P:(j + 1) * P], acc[:, j * P:(j + 1) * P], ident[:, :])
                            ins.then_inc(R.full, 1)
                        elif stage == "normT":
                            pe.wait_ge(s_xn, c + 1)
                            R.wait_free(pe, v)
                            for j in range(CT):
                                ins = pe.transpose(R.bank(0)[:, j * P:(j + 1) * P], xn[:, j, :], ident[:, :])
                            ins.then_inc(R.full, 1)
                        elif stage != "stats":
                            gates.on_tensor(pe, stage, R, v, c, XH[q], XL[q])
                    run(pe, do)

                @block.scalar
                def _(act):
                    if glu:
                        act.sem_inc(U1.free, 2)
                    act.sem_inc(WBK.free, 1)
                    act.sem_inc(EO.free, 2)

                    def do(stage, v, c, q):
                        n = c * NU + v
                        if stage == "up":
                            m = rows(v)
                            if glu:
                                U2.wait_free(act, n)
                                U1.wait_full(act, n)
                                act.activation(act1[0:m, v % 2, :], U1.bank(v)[0:m, :], ACT.Silu).then_inc(U1.free, 1)
                            else:
                                wait_count(act, s_lo, n + 1 - HD)
                                U1.wait_full(act, n)
                                act.activation(hid[0:m, v % HD, :], U1.bank(v)[0:m, :], ACT.Relu).then_inc(U1.free, 1)
                        elif stage == "hidden":
                            m = rows(v)
                            wait_count(act, s_down, n + 1 - HD)
                            if weighted[v] is None:
                                U2.wait_read(act, n)
                            else:
                                act.wait_ge(s_gated, gated(c, v))
                            act.copy(HH[0:m, v % HD, :], hid[0:m, v % HD, :]).then_inc(s_hi, 1)
                        elif stage == "spread":
                            if v >= 2:
                                act.wait_ge(s_gated, gated(c, user[v - 2][-1]))
                            elif not (isinstance(c, int) and c == 0):
                                act.wait_ge(s_gated, gated(c - 1, user[NS + v - 2][-1]))
                            WBK.wait_full(act, c * NS + v)
                            act.copy(WB[:, v % 2, :], WBK.bank(0)[:, :]).then_inc(WBK.free, 1)
                        elif stage == "collect":
                            if not (isinstance(c, int) and c == 0):
                                R.wait_full(act, r_item(c, 0))
                            act.wait_ge(s_down, (c + 1) * NU)
                            act.copy(acc[:, :], EO.bank(q)[:, :]).then_inc(EO.free, 1)
                        elif stage == "normT":
                            R.wait_full(act, v)
                            act.copy(XH[q][:, :], R.bank(0)[:, :]).then_inc(R.mid, 1)
                        elif stage != "stats":
                            gates.on_scalar(act, stage, c)
                    run(act, do)

                @block.gpsimd
                def _(pool):
                    def do(stage, v, c, q):
                        if stage == "up" and weighted[v] is not None:
                            m, s = rows(v), weighted[v]
                            (U2 if glu else U1).wait_read(pool, c * NU + v)
                            WBK.wait_read(pool, c * NS + s)
                            pool.tensor_tensor(hid[0:m, v % HD, :], hid[0:m, v % HD, :], WB[0:m, s % 2, :],
                                               ALU.mult).then_inc(s_gated, 1)
                    run(pool, do)

                @block.vector
                def _(dve):
                    me = Self(dve, s_me)
                    dve.sem_inc(R.free, 1)
                    dve.sem_inc(U2.free if glu else U1.free, 2 if glu else 4)

                    def do(stage, v, c, q):
                        n = c * NU + v
                        if stage == "up" and glu:
                            m = rows(v)
                            wait_count(dve, s_lo, n + 1 - HD)
                            U1.wait_read(dve, n)
                            U2.wait_full(dve, n)
                            dve.tensor_tensor(hid[0:m, v % HD, :], U2.bank(v)[0:m, :], act1[0:m, v % 2, :],
                                              ALU.mult).then_inc(U2.free, 1)
                        elif stage == "hidden":
                            m = rows(v)
                            wait_count(dve, s_down, n + 1 - HD)
                            dve.wait_ge(s_hi, n + 1)
                            dve.tensor_tensor(HL[0:m, v % HD, :], hid[0:m, v % HD, :], raw(HH[0:m, v % HD, :]),
                                              ALU.subtract).then_inc(s_lo, 1)
                        elif stage == "norm":
                            normalise(dve, me, stt, xn, c, s_xn)
                        elif stage == "normT":
                            R.wait_mid(dve, c)
                            dve.tensor_tensor(XL[q][:, :], R.bank(0)[:, :], raw(XH[q][:, :]), ALU.subtract).then_inc(R.free, 1)
                        elif stage == "back":
                            R.wait_full(dve, v)
                            residual(dve, me, R.bank(0), c)
                        elif stage == "stats":
                            statistics(dve, me, bs, ag, c, R.free)
                        elif stage == "mask":
                            gates.mask(dve, v, c, WBK)
                        elif stage in ("up", "spread", "down", "collect"):
                            pass
                        else:
                            gates.on_vector(dve, me, stage, R, v, c)
                    run(dve, do, me.clear)
                    me.wait()

        class Router:
            items, masks, first, late = 4, False, (("weights", 1), ("exp", 0)), (("weightsT", 2),)
            stages = (("weights", 11, 2), ("exp", 12, 0), ("weightsT", NU0 - 1, 3))

            def __init__(self, st, wgT):
                self.wgT = wgT
                self.wtok = sb(st, "wtok", [P, CT, 2, HALF])
                self.WT = sb(st, "WT", [2 * HALF, CW], f32r)
                self.sel = sb(st, "sel_e", [2 * HALF, ER + RU, P], f32r)
                self.s_wtok = sem(st, "w_ready")
                self.lg, self.ex, self.w0 = (sb(st, n, [P, CT, ER]) for n in ("logits", "exps", "w_raw"))
                self.mx, self.total = sb(st, "mx", [P, CT]), sb(st, "w_total", [P, CT])
                self.gt, self.eq = (sb(st, n, [P, CT, ER, ER]) for n in ("gt", "eq"))
                self.lower = sb(st, "lower", [P, ER, ER])
                self.s_sub, self.s_exp, self.s_tri = (sem(st, n) for n in ("s_sub", "s_exp", "s_tri"))
                self.s_p, self.s_f = sem(st, "sel_pool"), sem(st, "sel_made")

            def temporaries(self, st):
                self.f, self.g = sb(st, "sel_f", [2 * HALF, ER + RU, P]), sb(st, "sel_g", [2 * HALF, RU, P])

            def constants_on_gpsimd(self, pool):
                f, g = self.f, self.g
                me = Self(pool, self.s_p)
                pool.memset(self.lower[:, :, :], 1.0).then_inc(self.s_tri, 1)
                pool.wait_ge(self.s_tri, 1)
                pool.affine_select(out=self.lower[:, :, :], in_=self.lower[:, :, :], compare_op=ALU.is_gt,
                                   fill=0.0, base=0, pattern=[[1, ER], [-1, ER]],
                                   channel_multiplier=0).then_inc(self.s_tri, 1)
                me.done(pool.memset(self.wtok[:, :, :, :], 0.0))
                me.wait()
                me.done(pool.memset(self.wtok[:, :, :, 0:1], 1.0))
                me.done(pool.memset(f[:, 0:ER, :], 0.0))
                me.done(pool.memset(f[:, ER:ER + RU, :], 1.0))
                me.done(pool.memset(g[:, :, :], 1.0))
                me.wait()
                for base in (0, HALF):
                    me.done(pool.affine_select(out=f[:, 0:ER, :], in_=f[:, 0:ER, :], compare_op=ALU.not_equal,
                                               fill=1.0, base=-1 - base, pattern=[[-1, ER], [0, P]],
                                               channel_multiplier=1))
                    me.wait()
                for to, base in ((f[:, ER:ER + RU, :], 0), (g[:, :, :], HALF * REST)):
                    me.done(pool.affine_select(out=to, in_=to, compare_op=ALU.is_ge, fill=0.0, base=base,
                                               pattern=[[P, RU], [1, P]], channel_multiplier=-REST))
                    me.wait()
                    me.done(pool.affine_select(out=to, in_=to, compare_op=ALU.is_ge, fill=0.0, base=REST - 1 - base,
                                               pattern=[[-P, RU], [-1, P]], channel_multiplier=REST))
                    me.wait()
                pool.tensor_tensor(f[:, ER:ER + RU, :], f[:, ER:ER + RU, :], g[:, :, :], ALU.add).then_inc(self.s_f, 1)

            def constants_on_vector(self, dve):
                dve.wait_ge(self.s_f, 1)
                dve.tensor_copy(self.sel[:, :, :], self.f[:, :, :]).then_inc(self.s_f, 1)
                dve.wait_ge(self.s_f, 2)

            def ready(self, pe, R, s, c):
                if s == 0:
                    R.wait_read(pe, 2 if isinstance(c, int) and c == 0 else 4 * c + 1)

            def product(self, s):
                return self.sel[:, s, :], self.WT[:, :]

            def on_tensor(self, pe, stage, R, n, c, XH, XL):
                if stage == "weights":
                    R.wait_read(pe, n - 1)
                    R.wait_free(pe, n)
                    for j in range(CT):
                        for m, x_ in enumerate((XH, XL)):
                            ins = pe.matmul(R.bank(0)[:, j * 2 * ER:(j + 1) * 2 * ER], x_[:, j * P:(j + 1) * P], self.wgT[:, :],
                                            start=(m == 0), stop=(m == 1))
                    ins.then_inc(R.full, 1)
                elif stage == "weightsT":
                    pe.wait_ge(self.s_wtok, c + 1)
                    R.wait_free(pe, n)
                    for j in range(CT):
                        ins = pe.transpose(R.bank(0)[0:2 * HALF, j * P:(j + 1) * P],
                                           self.wtok[:, j, :, :].rearrange("p a e -> p (a e)"), ident[:, :])
                    ins.then_inc(R.full, 1)

            def on_scalar(self, act, stage, c):
                if stage == "exp":
                    act.wait_ge(self.s_sub, c + 1)
                    act.activation(self.ex[:, :, :], self.ex[:, :, :], ACT.Exp).then_inc(self.s_exp, 1)

            def on_vector(self, dve, me, stage, R, n, c):
                if stage == "weights":
                    self.rank(dve, me, R, n)
                elif stage == "exp":
                    self.weigh(dve, me, c)
                elif stage == "weightsT":
                    R.wait_full(dve, n)
                    me.done(dve.tensor_copy(self.WT[:, :], R.bank(0)[0:2 * HALF, :]))
                    me.wait()
                    lower = self.WT[HALF:2 * HALF, :]
                    dve.tensor_tensor(lower, R.bank(0)[HALF:2 * HALF, :], raw(lower), ALU.subtract).then_inc(R.free, 1)

            def rank(self, dve, me, R, n):
                lg, ex = self.lg, self.ex
                wide = [P, CT, ER, ER]
                got = R.bank(0)[:, 0:CT * 2 * ER].rearrange("p (t h e) -> p t h e", t=CT, h=2)
                R.wait_full(dve, n)
                me.done(dve.tensor_tensor(lg[:, :, :], got[:, :, 1, :],
                                          rb_bc[:, :].rearrange("p (a e) -> p a e", a=1).to_broadcast([P, CT, ER]), ALU.add))
                me.wait()
                ins = dve.tensor_tensor(lg[:, :, :], got[:, :, 0, :], lg[:, :, :], ALU.add)
                ins.then_inc(R.free, 1)
                R.wait_read(dve, n)
                me.done(dve.tensor_reduce(self.mx[:, :], lg[:, :, :], AX.X, ALU.max))
                me.wait()
                dve.tensor_tensor(ex[:, :, :], lg[:, :, :], self.mx[:, :].rearrange("p (t a) -> p t a", a=1).to_broadcast([P, CT, ER]),
                                  ALU.subtract).then_inc(self.s_sub, 1)
                other = lg[:, :, :].rearrange("p t (a f) -> p t a f", a=1).to_broadcast(wide)
                mine = lg[:, :, :].rearrange("p t (e a) -> p t e a", a=1).to_broadcast(wide)
                me.done(dve.tensor_tensor(self.gt[:, :, :, :], other, mine, ALU.is_gt))
                me.done(dve.tensor_tensor(self.eq[:, :, :, :], other, mine, ALU.is_equal))
                me.wait()
                me.done(dve.tensor_tensor(self.eq[:, :, :, :], self.eq[:, :, :, :],
                                          self.lower[:, :, :].rearrange("p (a e) f -> p a e f", a=1).to_broadcast(wide), ALU.mult))
                me.wait()
                me.done(dve.tensor_tensor(self.gt[:, :, :, :], self.gt[:, :, :, :], self.eq[:, :, :, :], ALU.add))
                me.wait()
                me.done(dve.tensor_reduce(self.w0[:, :, :], self.gt[:, :, :, :], AX.X, ALU.add))
                me.wait()

            def weigh(self, dve, me, c):
                ex = self.ex
                dve.wait_ge(self.s_exp, c + 1)
                me.done(dve.scalar_tensor_tensor(self.w0[:, :, :], self.w0[:, :, :], float(TOPK), ex[:, :, :], ALU.is_lt, ALU.mult))
                me.wait()
                me.done(dve.tensor_reduce(self.total[:, :], self.w0[:, :, :], AX.X, ALU.add))
                me.wait()
                me.done(dve.reciprocal(self.total[:, :], self.total[:, :]))
                me.wait()
                for a in range(2):
                    ins = dve.tensor_tensor(self.wtok[:, :, a, 1:1 + ER], self.w0[:, :, :],
                                            self.total[:, :].rearrange("p (t a) -> p t a", a=1).to_broadcast([P, CT, ER]),
                                            ALU.mult)
                    if a:
                        ins.then_inc(self.s_wtok, 1)

        class Gates:
            items, masks, first, late = 2, True, (("names", 0),), ()
            stages = (("names", 9, 0),)

            def __init__(self, st):
                self.names = sb(st, "names", [P, TILES * BPT, S], int32)
                self.cn = sb(st, "cn", [P, TILES * BPT, S])
                self.chl = sb(st, "chl", [P, CHUNKS, CW], f32r)
                self.masked = sb(st, "masked", [P, 4, CW], f32r)
                self.ones = sb(st, "ones3", [P, P], f32r)
                self.s_first, self.s_rest, self.s_one, self.s_copied, self.s_split, self.s_mask = (
                    sem(st, n) for n in ("first_context", "rest_context", "ones3_made", "context_high", "context_split", "masked_ready"))

            def load(self, sp):
                ck, ik = ctx_in.rearrange("b k s -> k b s"), itok.rearrange("b k s -> k b s")
                nb = CT * BPT
                for part, done in ((slice(0, nb), self.s_first), (slice(nb, TILES * BPT), self.s_rest)):
                    for h in (0, S):
                        sp.dma_start(self.cn[h:h + S, part, :], ck[:, part, :]).then_inc(done, 16)
                        sp.dma_start(self.names[h:h + S, part, :], ik[:, part, :]).then_inc(done, 16)

            def temporaries(self, st):
                self.ones_f = sb(st, "ones3f", [P, P])

            def constants_on_gpsimd(self, pool):
                pool.memset(self.ones_f[:, :], 1.0).then_inc(self.s_one, 1)

            def constants_on_vector(self, dve):
                dve.wait_ge(self.s_one, 1)
                dve.tensor_copy(self.ones[:, :], self.ones_f[:, :]).then_inc(self.s_one, 1)
                dve.wait_ge(self.s_one, 2)

            def of(self, c, h=0):
                nb = CT * BPT
                return self.cn[h:P, bass.ds(c * nb, nb), :].rearrange("k b s -> k (b s)")

            def here(self, eng, c):
                eng.wait_ge(*((self.s_first, 64) if isinstance(c, int) and c == 0 else (self.s_rest, 64)))

            def ready(self, pe, R, s, c):
                pe.wait_ge(self.s_mask, c * E1 + s + 1)

            def product(self, s):
                return self.ones[:, :], self.masked[:, s % 4, :]

            def on_tensor(self, pe, stage, R, n, c, XH, XL):
                pass

            def on_scalar(self, act, stage, c):
                if stage == "names":
                    self.here(act, c)
                    act.copy(self.chl[:, c, :], self.of(c)).then_inc(self.s_copied, 1)

            def on_vector(self, dve, me, stage, R, n, c):
                if stage == "names":
                    self.here(dve, c)
                    dve.wait_ge(self.s_copied, c + 1)
                    dve.tensor_tensor(self.chl[S:P, c, :], self.of(c, S), raw(self.chl[S:P, c, :]),
                                      ALU.subtract).then_inc(self.s_split, 1)

            def mask(self, dve, e, c, WBK):
                n = c * E1 + e
                if e == 0:
                    dve.wait_ge(self.s_split, c + 1)
                if not (isinstance(n, int) and n < 4):
                    WBK.wait_full(dve, n - 4)
                nb = CT * BPT
                names = self.names[:, bass.ds(c * nb, nb), :].rearrange("k b s -> k (b s)")
                dve.scalar_tensor_tensor(self.masked[:, e % 4, :], names, float(e), raw(self.chl[:, c, :]),
                                         ALU.is_equal, ALU.mult).then_inc(self.s_mask, 1)

        pin_n = sb(top, "pin_n", [P, E1 * D1 // P, D])
        pout_n = sb(top, "pout_n", [D, E1, D1])
        q_n = [sb(top, "wgate_n", [P, I1 // P, D]), sb(top, "wup_n", [P, I1 // P, D]), sb(top, "wdown_n", [D, I1])]
        s_w1 = sem(top, "s_w1")

        if phases >= 2:
            with ExitStack() as st2:
                W1H, W1L, W2H, W2L = (sb(st2, n, [D, NU0, P], f32r) for n in ("W1H", "W1L", "W2H", "W2L"))
                W3H, W3L = (sb(st2, n, [P, NU0, D], f32r) for n in ("W3H", "W3L"))
                wgT = sb(st2, "wgT", [D, 2 * ER], f32r)
                rows = lambda u: REST_LAST if u == NU0 - 1 else P
                items = [([(0, ER, wgn[:, :])], P, ER, wgT[:, 0:ER], wgT[:, ER:2 * ER])]
                for u0 in range(0, NU0, 4):
                    for src, hi, lo in ((w1n, W1H, W1L), (w2n, W2H, W2L)):
                        flat = lambda w: w[:, u0:u0 + 4, :].rearrange("d u h -> d (u h)")[:, 0:3 * P + rows(u0 + 3)]
                        items.append(([(i * P, rows(u0 + i), src[0:rows(u0 + i), u0 + i, :]) for i in range(4)],
                                      D, 3 * P + rows(u0 + 3), flat(hi), flat(lo)))
                    n = rows(u0 + 3)
                    part = lambda w, m, r: w[0:r, u0:u0 + m, :].rearrange("p u d -> p (u d)")
                    if n == P:
                        items.append(([(i * D, D, w3n[:, (u0 + i) * P:(u0 + i + 1) * P]) for i in range(4)],
                                      P, 4 * D, part(W3H, 4, P), part(W3L, 4, P)))
                    else:
                        items.append(([(i * D, D, w3n[:, (u0 + i) * P:(u0 + i + 1) * P]) for i in range(3)],
                                      P, 3 * D, part(W3H, 3, P), part(W3L, 3, P)))
                        u = NU0 - 1
                        items.append(([(0, D, w3n[:, u * P:u * P + n])], n, D, W3H[0:n, u, :], W3L[0:n, u, :]))
                def load_later(sp):
                    sp.dma_start(pin_n[:, :, :], p_in.rearrange("e (h p) i -> p (e h) i", p=P)).then_inc(s_w1, 16)
                    sp.dma_start(pout_n[:, :, :], p_out.rearrange("e i d -> i e d")).then_inc(s_w1, 16)
                    sp.dma_start(q_n[0][:, :, :], w_gate.rearrange("(k p) i -> p k i", p=P)).then_inc(s_w1, 16)
                    sp.dma_start(q_n[1][:, :, :], w_up.rearrange("(k p) i -> p k i", p=P)).then_inc(s_w1, 16)
                    sp.dma_start(q_n[2][:, :], w_down).then_inc(s_w1, 16)
                gates, dev = Router(st2, wgT), finish_deviation(st2, "2")
                with ExitStack() as st:
                    turn_weights("k0", st, s_w0, W0_LOADS, items, dev, gates, load_later)

                up2 = lambda u: [(W1H[:, u, 0:rows(u)], W1L[:, u, 0:rows(u)]), (W2H[:, u, 0:rows(u)], W2L[:, u, 0:rows(u)])]
                down2 = lambda u: (W3H[0:rows(u), u, :], W3L[0:rows(u), u, :])
                weighted = [None] * MAIN + [e for e in range(ER) for _ in range(MAIN)] + [ER + m for m in range(RU)]
                experts_phase("2", st2, NU0, up2, down2, rows, weighted, gates)

        NQ = 3

        class Ternary:

            def __init__(self, st):
                self.ones = sb(st, "ones4", [P, P])
                self.absum, self.mean, self.scale = (sb(st, n, [P, NQ]) for n in ("absum", "meanw", "scalew"))
                self.wt, self.wi = sb(st, "wt", [P, NQ, 4 * P]), sb(st, "wi", [P, NQ, 4 * P], bf16)
                self.s_one, self.s_abs, self.s_sum, self.s_scale, self.s_wi, self.s_turned, self.s_wq, self.s_me, self.s_round, self.s_clip = (
                    sem(st, n) for n in ("s4_one", "s4_abs", "s4_sum", "s4_scale", "s4_wi", "s4_turned", "s4_wq", "s4_me0", "s4_round", "s4_clip"))
                self.nat = [w[:, :, :].rearrange("p k i -> p (k i)") if n < 2 else w[:, :] for n, w in enumerate(q_n)]

            def on_gpsimd(self, pool):
                pool.memset(self.ones[:, :], 1.0).then_inc(self.s_one, 1)
                pool.wait_ge(s_w1, 80)
                pool.wait_ge(self.s_scale, 1)
                for n in range(NQ):
                    pool.tensor_scalar(self.wt[:, n, :], self.nat[n], self.scale[:, n:n + 1], ROUND,
                                       ALU.mult, ALU.add).then_inc(self.s_round, 1)

            def sums(self, pe):
                pe.wait_ge(self.s_one, 1)
                pe.wait_ge(self.s_abs, NQ)
                pe.matmul(bank[6][:, 0:NQ], self.ones[:, :], self.absum[:, :], start=True, stop=True).then_inc(self.s_sum, 1)

            def turn(self, pe):
                for n in range(NQ):
                    pe.wait_ge(self.s_wi, n + 1)
                    if n == 2:
                        pe.wait_ge(self.s_scale, 1)
                    for k in range(4):
                        at = (n % 2 * 4 + k) * 64
                        ins = pe.transpose(bank[7 - n // 2][:, at:at + 64].bitcast(bf16),
                                           self.wi[:, n, k * P:(k + 1) * P], identb[:, :])
                    if n:
                        ins.then_inc(self.s_turned, 1)

            def on_scalar(self, act):
                for n in range(NQ):
                    act.wait_ge(self.s_turned, 1 + n // 2)
                    act.copy(WQ[n][:, :, :].rearrange("p k i -> p (k i)"),
                             bank[7 - n // 2][:, n % 2 * 256:n % 2 * 256 + 256].bitcast(bf16)).then_inc(self.s_wq, 1)
                act.wait_ge(self.s_wq, NQ)

            def on_vector(self, dve):
                me = Self(dve, self.s_me)
                dve.wait_ge(s_w1, 80)
                for n in range(NQ):
                    dve.tensor_reduce(self.absum[:, n:n + 1], self.nat[n], AX.X, ALU.add,
                                      apply_absolute_value=True).then_inc(self.s_abs, 1)
                dve.wait_ge(self.s_sum, 1)
                me.done(dve.tensor_scalar(self.mean[:, :], bank[6][:, 0:NQ], 1.0 / (I1 * D), 1e-5, ALU.mult, ALU.max))
                me.wait()
                dve.reciprocal(self.scale[:, :], self.mean[:, :]).then_inc(self.s_scale, 1)
                me.done(dve.tensor_scalar(mean127[:, :], self.mean[:, :], 1.0 / 127.0, None, ALU.mult))
                me.wait()

            def clip(self, dve):
                for n in range(NQ):
                    dve.wait_ge(self.s_round, n + 1)
                    dve.tensor_scalar(self.wt[:, n, :], self.wt[:, n, :], -ROUND, 1.0, ALU.add, ALU.min).then_inc(self.s_clip, 1)
                    dve.wait_ge(self.s_clip, n + 1)
                    dve.tensor_scalar(self.wi[:, n, :], self.wt[:, n, :], -1.0, None, ALU.max).then_inc(self.s_wi, 1)

        WQ, mean127 = [sb(top, n, [P, 4, P], bf16) for n in ("WQg", "WQu", "WQd")], sb(top, "mean127", [P, NQ])
        if phases >= 3:
            with ExitStack() as st3:
                PIH, PIL = (sb(st3, n, [D, E1 * D1], f32r) for n in ("PIH", "PIL"))
                POH, POL = (sb(st3, n, [P, E1 * D1 // P, D], f32r) for n in ("POH", "POL"))
                items = []
                for u in range(0, E1 * D1 // P, 4):
                    items.append(([(i * P, P, pin_n[:, u + i, :]) for i in range(4)], D, 4 * P,
                                  PIH[:, u * P:(u + 4) * P], PIL[:, u * P:(u + 4) * P]))
                    flat = lambda w: w[:, u:u + 4, :].rearrange("p u d -> p (u d)")
                    items.append(([(i * D, D, pout_n[:, (u + i) // 2, (u + i) % 2 * P:((u + i) % 2 + 1) * P]) for i in range(4)],
                                  P, 4 * D, flat(POH), flat(POL)))
                gates, dev = Gates(st3), finish_deviation(st3, "3")
                with ExitStack() as st:
                    turn_weights("k1", st, s_w1, 5, items, dev, gates, gates.load, Ternary(st))
                experts_phase("3", st3, E1 * D1 // P, lambda u: [(PIH[:, u * P:(u + 1) * P], PIL[:, u * P:(u + 1) * P])],
                              lambda u: (POH[:, u, :], POL[:, u, :]), lambda u: P, [u * P // D1 for u in range(E1 * D1 // P)], gates)

        if phases >= 4:
            with ExitStack() as st4:
                xn, stt = sb(st4, "xn4", [P, CT, D]), sb(st4, "stt4", [P, CT, 2])
                shift = sb(st4, "shift", [P, 1, 1])
                xr, xq = sb(st4, "xr4", [P, CT, D]), sb(st4, "xq4", [P, CT, D], bf16)
                xqT = sb(st4, "xqT", [D, CT, P], bf16)
                a1, r1, dg, du = (sb(st4, n, [P, CT]) for n in ("a1", "r1", "dg", "du"))
                sg, pr = sb(st4, "sg", [P, 2, I1]), sb(st4, "pr", [P, CT, I1])
                qr, qb = sb(st4, "qr", [P, CT, I1]), sb(st4, "qb", [P, CT, I1], bf16)
                qT = sb(st4, "qT", [P, CT, I1], bf16)
                a2, r2, dd = (sb(st4, n, [P, CT]) for n in ("a2", "r2", "dd"))
                dve_var, dve_dev, act_dev = finish_deviation(st4, "4")
                G = Ring(bank[0:2], sem(st4, "gate_full"), sem(st4, "gate_free"))
                U = Ring(bank[2:4], sem(st4, "up_full"), sem(st4, "up_free"))
                T = Ring(bank[4:6], sem(st4, "turn_full"), sem(st4, "turn_free"))
                Y = Ring(bank[6:7], None, sem(st4, "y_free"))
                XT = Ring(bank[7:8], sem(st4, "xt_full"), sem(st4, "xt_free"))
                s_xn, s_r1, s_mv, s_pool = (sem(st4, n) for n in ("s4_xn", "s4_r1", "s4_mv", "s4_pool"))
                s_me, s_xq, s_dg, s_qr, s_qb, s_down, s_out = (
                    sem(st4, n) for n in ("s4_me", "s4_xq", "s4_dg", "s4_qr", "s4_qb", "s4_down", "s4_out"))

                def body4(c, ups, downs, more, do):
                    for stage, j in (("up", 0), ("up", 1), ("up", 2), ("up", 3), ("turn", 0), ("turn", 1), ("down", 0), ("turn", 2), ("down", 1), ("turn", 3), ("down", 2), ("down", 3)):
                        if stage == "up" and ups:
                            do(stage, j, c)
                        elif stage != "up" and downs:
                            do(stage, j, c - 1)
                        if (stage, j) == ("up", 1) and more:
                            do("quant", 0, c + 1)
                    if more:
                        do("scales", 0, c + 1)
                    if ups:
                        do("largest", 0, c)
                    if downs:
                        do("add", 0, c - 1)
                    if more:
                        do("xT", 0, c + 1)
                    if ups:
                        do("requant", 0, c)

                def run4(eng, do, clear=lambda: None):
                    do("quant", 0, 0)
                    do("scales", 0, 0)
                    do("xT", 0, 0)
                    body4(0, True, False, True, do)
                    clear()
                    with eng.Fori(1, CHUNKS - 1) as c:
                        body4(c, True, True, True, do)
                        clear()
                    body4(CHUNKS - 1, True, True, False, do)
                    body4(CHUNKS, False, True, False, do)

                def positive(eng, sem_, value):
                    if not (isinstance(value, int) and value <= 0):
                        eng.wait_ge(sem_, value)

                with nc.Block() as block:
                    @block.sync
                    def _(sp):
                        def store(c):
                            Y.wait_read(sp, c)
                            sp.dma_start(out_t[:, bass.ds(c * CT, CT), :], X[:, bass.ds(c * CT, CT), :]).then_inc(s_out, 16)
                        store(0)
                        with sp.Fori(1, CHUNKS) as c:
                            store(c)
                        sp.wait_ge(s_out, 16 * CHUNKS)

                    @block.tensor
                    def _(pe):
                        def do(stage, j, c):
                            n = c * CT + j
                            if stage == "xT":
                                pe.wait_ge(s_xq, c + 1)
                                XT.wait_free(pe, c)
                                for q in range(CT):
                                    ins = pe.transpose(XT.bank(0)[:, q * 64:(q + 1) * 64].bitcast(bf16), xq[:, q, :], identb[:, :])
                                ins.then_inc(XT.full, 1)
                            elif stage == "up":
                                if j == 0:
                                    XT.wait_read(pe, c)
                                for R_, w in ((G, WQ[0]), (U, WQ[1])):
                                    R_.wait_free(pe, n)
                                    pe.matmul(R_.bank(j)[:, :], xqT[:, j, :], w[:, :, :].rearrange("p k i -> p (k i)"),
                                              start=True, stop=True).then_inc(R_.full, 1)
                            elif stage == "turn":
                                pe.wait_ge(s_qb, n + 1)
                                T.wait_free(pe, n)
                                for k in range(4):
                                    ins = pe.transpose(T.bank(j)[:, k * 64:(k + 1) * 64].bitcast(bf16),
                                                       qb[:, j, k * P:(k + 1) * P], identb[:, :])
                                ins.then_inc(T.full, 1)
                            elif stage == "down":
                                T.wait_read(pe, n)
                                if j == 0:
                                    Y.wait_free(pe, c)
                                for k in range(4):
                                    ins = pe.matmul(Y.bank(0)[:, j * D:(j + 1) * D], qT[:, j, k * P:(k + 1) * P], WQ[2][:, k, :],
                                                    start=(k == 0), stop=(k == 3))
                                ins.then_inc(s_down, 1)
                        run4(pe, do)

                    @block.scalar
                    def _(act):
                        act_dev(act)
                        act.sem_inc(G.free, 2)
                        act.sem_inc(T.free, 2)
                        act.sem_inc(XT.free, 1)

                        def do(stage, j, c):
                            n = c * CT + j
                            if stage == "xT":
                                positive(act, U.full, c * CT)
                                XT.wait_full(act, c)
                                act.copy(xqT[:, :, :].rearrange("p t d -> p (t d)"), XT.bank(0)[:, 0:256].bitcast(bf16)).then_inc(XT.free, 1)
                            elif stage == "up":
                                if j == 0:
                                    act.wait_ge(s_dg, c + 1)
                                U.wait_free(act, n)
                                G.wait_full(act, n)
                                act.activation(sg[:, j % 2, :], G.bank(j)[:, :], ACT.Silu, scale=dg[:, j:j + 1]).then_inc(G.free, 1)
                            elif stage == "turn":
                                act.wait_ge(s_qr, n + 1)
                                act.activation(qb[:, j, :], qr[:, j, :], ACT.Copy, bias=-ROUND).then_inc(s_qb, 1)
                            elif stage == "down":
                                act.wait_ge(s_down, n + 1)
                                T.wait_full(act, n)
                                act.copy(qT[:, j, :], T.bank(j)[:, 0:256].bitcast(bf16)).then_inc(T.free, 1)
                        run4(act, do)

                    @block.gpsimd
                    def _(pool):
                        me = Self(pool, s_pool)
                        wide = lambda ap: ap.to_broadcast([P, CT, D])
                        me.done(pool.memset(shift[:, :, :], ROUND))
                        me.wait()

                        def do(stage, j, c):
                            if stage != "quant":
                                return
                            if isinstance(c, int) and c == 0:
                                pool.wait_ge(s_mv, 1)
                            positive(pool, s_r1, c)
                            part = bass.ds(c * CT, CT)
                            me.done(pool.tensor_tensor(xn[:, :, :], X[:, part, :], wide(MV[:, part, 0:1]), ALU.subtract))
                            me.wait()
                            pool.tensor_tensor(xn[:, :, :], xn[:, :, :], wide(MV[:, part, 1:2]), ALU.mult).then_inc(s_xn, 1)
                            pool.wait_ge(s_r1, c + 1)
                            me.done(pool.tensor_tensor(xr[:, :, :], xn[:, :, :],
                                                       wide(r1[:, :].rearrange("p (t a) -> p t a", a=1)), ALU.mult))
                            me.wait()
                            me.done(pool.tensor_tensor(xr[:, :, :], xr[:, :, :], wide(shift[:, 0:1, :]), ALU.add))
                            positive(pool, XT.full, c)
                            me.wait()
                            pool.tensor_tensor(xq[:, :, :], xr[:, :, :], wide(shift[:, 0:1, :]), ALU.subtract).then_inc(s_xq, 1)
                        run4(pool, do, me.clear)
                        me.wait()

                    @block.vector
                    def _(dve):
                        me = Self(dve, s_me)
                        dve.sem_inc(U.free, 2)
                        dve.sem_inc(Y.free, 1)
                        dve_var(dve)
                        dve.sem_inc(s_down, CT)
                        dve_dev(dve, me)
                        dve.sem_inc(s_mv, 1)

                        def do(stage, j, c):
                            n = c * CT + j
                            if stage == "quant":
                                dve.wait_ge(s_xn, c + 1)
                                me.done(dve.tensor_reduce(a1[:, :], xn[:, :, :], AX.X, ALU.max, apply_absolute_value=True))
                                me.wait()
                                me.done(dve.tensor_scalar(a1[:, :], a1[:, :], 1e-5, None, ALU.max))
                                me.wait()
                                me.done(dve.reciprocal(r1[:, :], a1[:, :]))
                                me.wait()
                                dve.tensor_scalar(r1[:, :], r1[:, :], 127.0, None, ALU.mult).then_inc(s_r1, 1)
                            elif stage == "scales":
                                positive(dve, U.free, c * CT + (0 if isinstance(c, int) and c == 0 else 2))
                                dve.tensor_scalar(dg[:, :], a1[:, :], mean127[:, 0:1], None, ALU.mult).then_inc(s_dg, 1)
                                me.done(dve.tensor_scalar(du[:, :], a1[:, :], mean127[:, 1:2], None, ALU.mult))
                                me.wait()
                            elif stage == "up":
                                G.wait_read(dve, n)
                                U.wait_full(dve, n)
                                positive(dve, s_qr, n - CT + 1)
                                dve.scalar_tensor_tensor(pr[:, j, :], U.bank(j)[:, :], du[:, j:j + 1], sg[:, j % 2, :],
                                                         ALU.mult, ALU.mult).then_inc(U.free, 1)
                            elif stage == "largest":
                                U.wait_read(dve, n + CT - 1)
                                me.done(dve.tensor_reduce(a2[:, :], pr[:, :, :], AX.X, ALU.max, apply_absolute_value=True))
                                me.wait()
                                me.done(dve.tensor_scalar(a2[:, :], a2[:, :], 1e-5, None, ALU.max))
                                me.wait()
                                me.done(dve.reciprocal(r2[:, :], a2[:, :]))
                                me.wait()
                                me.done(dve.tensor_scalar(r2[:, :], r2[:, :], 127.0, None, ALU.mult))
                            elif stage == "requant":
                                if not (isinstance(c, int) and c == 0):
                                    dve.wait_ge(Y.free, c + 1)
                                me.wait()
                                me.done(dve.tensor_scalar(dd[:, :], a2[:, :], mean127[:, 2:3], None, ALU.mult))
                                positive(dve, s_qb, n)
                                for q in range(CT):
                                    dve.tensor_scalar(qr[:, q, :], pr[:, q, :], r2[:, q:q + 1], ROUND,
                                                      ALU.mult, ALU.add).then_inc(s_qr, 1)
                            elif stage == "add":
                                dve.wait_ge(s_down, n + 2 * CT)
                                for q in range(CT):
                                    ins = dve.scalar_tensor_tensor(X[:, n + q, :], Y.bank(0)[:, q * D:(q + 1) * D], dd[:, q:q + 1],
                                                                   X[:, n + q, :], ALU.mult, ALU.add)
                                ins.then_inc(Y.free, 1)
                        run4(dve, do, me.clear)
                        me.wait()

        if phases < 4:
            with ExitStack() as fin:
                s_out = sem(fin, "s_out")
                with nc.Block() as block:
                    @block.sync
                    def _(sp):
                        for q in range(4):
                            n = TILES // 4
                            sp.dma_start(out_t[:, q * n:(q + 1) * n, :], X[:, q * n:(q + 1) * n, :]).then_inc(s_out, 16)
                        sp.wait_ge(s_out, 64)



_INS = ["x", "ctx_512", "itok_BxS2xS_0_7", "L0_xattn_Wq", "L0_xattn_Wk", "L0_xattn_Wv", "L0_xattn_Wo", "L0_xattn_bo",
        "L0_ffn_Wg", "L0_ffn_routing_bias", "L0_ffn_W1", "L0_ffn_W2", "L0_ffn_W3", "L0_ffn_Ws1", "L0_ffn_Ws2",
        "L0_ffn_Ws3", "L1_xattn_proj_in", "L1_xattn_proj_out", "L1_ffn_w_gate", "L1_ffn_w_up", "L1_ffn_w_down"]


def kernel(**inputs):
    import numpy as np
    import concourse.bacc as bacc
    from concourse.bass_utils import run_bass_kernel_spmd

    nc = bacc.Bacc("TRN2", target_bir_lowering=False, num_devices=1)
    arrays, args = {}, []
    for name in _INS:
        a = np.ascontiguousarray(inputs[name])
        arrays[f"in_{name}"] = a
        args.append(nc.dram_tensor(f"in_{name}", a.shape, mybir.dt.from_np(a.dtype), kind="ExternalInput").ap())
    args.append(nc.dram_tensor("out_0", (B, S, D), fp32, kind="ExternalOutput").ap())
    kernel_program(nc, *args)
    return run_bass_kernel_spmd(nc, [arrays], core_ids=[0]).results[0]["out_0"]
```
